# Optimizing a Trainium2 kernel written in Bass

```python
import numpy as np
import jax
import jax.numpy as jnp

def _softmax(x, axis=-1):
    return jax.nn.softmax(x, axis=axis)

def _gelu(x):
    return jax.nn.gelu(x, approximate=True)

def _silu(x):
    return jax.nn.silu(x)

def _sigmoid(x):
    return jax.nn.sigmoid(x)

def _layernorm(x, axis=-1, eps=1e-05):
    m = jnp.mean(x, axis=axis, keepdims=True)
    v = jnp.var(x, axis=axis, keepdims=True)
    return (x - m) / jnp.sqrt(v + eps)

def _scatter_add(tgt, idx, src, axis=0):
    return tgt.at[idx].add(src)

def _segment_sum(src, seg, n):
    return jax.ops.segment_sum(src, seg, n)
kernel_name = 'mk_gnn_resnorm_d2_gnn_r8_d54c33'

def setup_inputs(seed: int=0):
    np.random.seed(seed)
    _w = jnp.asarray

    def _rec_inputs():
        import jax
        import jax.numpy as jnp
        _gk = jax.random.key(seed)
        x = -0.0005121 + 1.001 * jax.random.normal(jax.random.fold_in(_gk, 1), (12500, 160), jnp.float32)
        _s = jax.random.randint(jax.random.fold_in(_gk, 2), (100000,), 0, 12500, jnp.int32)
        _d = jax.random.randint(jax.random.fold_in(_gk, 3), (100000,), 0, 12500, jnp.int32)
        _loop = jnp.arange(12500, dtype=jnp.int32)
        src = jnp.concatenate([_s, _d, _loop])
        dst = jnp.concatenate([_d, _s, _loop])
        _o = jnp.argsort(dst, stable=True)
        src = src[_o]
        dst = dst[_o]
        edge_attr_16 = jax.random.uniform(jax.random.fold_in(_gk, 12), (212500, 16), jnp.float32, 0.0, 1)
        edge_attr_4 = 0.000898722 + 1.00012 * jax.random.normal(jax.random.fold_in(_gk, 13), (212500, 4), jnp.float32)
        node_vec1 = jax.random.uniform(jax.random.fold_in(_gk, 15), (12500, 1), jnp.float32, 0.0, 1)
        return (x, src, dst, edge_attr_16, edge_attr_4, node_vec1)
    x, src, dst, edge_attr_16, edge_attr_4, node_vec1 = _rec_inputs()

    def _L0_gnn_setup():
        import jax, jax.numpy as jnp
        import numpy as np
        N, E = (2500, 40000)
        CS, CV = (64, 32)
        AS_, AV, H = (16, 8, 4)
        NB = 16
        SQRT3 = 1.7320508075688772
        SQRT2 = 1.4142135623730951
        EPS = 1e-05

        def _cg_tp(s, v, y0, y1, w_ss, w_sv, w_vs, w_vv0, w_vv1):
            out_s = jnp.concatenate([w_ss * s * y0[:, None], w_vv0 * (jnp.einsum('eci,ei->ec', v, y1) / SQRT3)], axis=-1)
            out_v = jnp.concatenate([(w_sv * s)[:, :, None] * y1[:, None, :], (w_vs * jnp.ones_like(v[..., 0]))[..., None] * v * y0[:, None, None], (w_vv1 * jnp.ones_like(v[..., 0]))[..., None] * (jnp.cross(v, y1[:, None, :]) / SQRT2)], axis=1)
            return (out_s, out_v)

        def _equiv_layernorm(s, v, gamma_s, beta_s, gamma_v):
            mu = jnp.mean(s, axis=-1, keepdims=True)
            var = jnp.var(s, axis=-1, keepdims=True)
            s_n = (s - mu) * jax.lax.rsqrt(var + EPS) * gamma_s + beta_s
            rms = jnp.sqrt(jnp.mean(jnp.sum(v * v, axis=-1), axis=-1, keepdims=True) + EPS)
            v_n = v / rms[..., None] * gamma_v[None, :, None]
            return (s_n, v_n)
        key = jax.random.key(seed)
        ks = jax.random.split(key, 26)

        def rn(k, shape, fan):
            return jax.random.normal(k, shape, jnp.float32) / np.sqrt(fan)
        D1S, D1V = (CS + CV, CS + 2 * CV)
        WN = 2 * CS + 3 * CV
        inp = {'node': jax.random.normal(ks[0], (N, CS + 3 * CV), jnp.float32), 'edge_index': jax.random.randint(ks[1], (2, E), 0, N, jnp.int64 if jax.config.jax_enable_x64 else jnp.int32), 'rbf': jax.random.uniform(ks[2], (E, NB), jnp.float32), 'rsh': jax.random.normal(ks[3], (E, 4), jnp.float32), 'gamma_s': jnp.ones((CS,), jnp.float32), 'beta_s': jnp.zeros((CS,), jnp.float32), 'gamma_v': jnp.ones((CV,), jnp.float32), 'Ws_src': rn(ks[4], (CS, CS), CS), 'Wv_src': rn(ks[5], (CV, CV), CV), 'Ws_dst': rn(ks[6], (CS, CS), CS), 'Wv_dst': rn(ks[7], (CV, CV), CV), 'W_rbf': rn(ks[8], (NB, WN), NB), 'W_alpha': rn(ks[9], (D1S, H * AS_), D1S), 'alpha_dot': rn(ks[10], (1, H, AS_), AS_), 'Ws_val': rn(ks[11], (D1S, CS), D1S), 'Wv_val': rn(ks[12], (D1V, CV), D1V), 'Wg': rn(ks[13], (CS, CV), CS), 'w2_ss': rn(ks[14], (CS,), 1), 'w2_sv': rn(ks[15], (CS,), 1), 'w2_vs': rn(ks[16], (CV,), 1), 'w2_vv0': rn(ks[17], (CV,), 1), 'w2_vv1': rn(ks[18], (CV,), 1), 'Ws_vlin': rn(ks[19], (D1S, H * AS_), D1S), 'Wv_vlin': rn(ks[20], (D1V, H * AV), D1V), 'Wps': rn(ks[21], (H * AS_, CS), H * AS_), 'Wpv': rn(ks[22], (H * AV, CV), H * AV)}
        return inp
    _L0_gnn_all = _L0_gnn_setup()
    _L0_gnn_in = {k: v for k, v in _L0_gnn_all.items() if k in ('gamma_s', 'beta_s', 'gamma_v', 'Ws_src', 'Wv_src', 'Ws_dst', 'Wv_dst', 'W_rbf', 'W_alpha', 'alpha_dot', 'Ws_val', 'Wv_val', 'Wg', 'w2_ss', 'w2_sv', 'w2_vs', 'w2_vv0', 'w2_vv1', 'Ws_vlin', 'Wv_vlin', 'Wps', 'Wpv')}
    del _L0_gnn_all

    def _L1_gnn_setup():
        import jax, jax.numpy as jnp
        import numpy as np
        N = 2500
        E = 40000
        MUL0 = 64
        MUL1 = 32
        FC_IN = 16
        FC_H = 64
        WNUM = 192
        key = jax.random.key(seed)
        ks = jax.random.split(key, 16)
        return {'x': jax.random.normal(ks[0], (N, MUL0 + 3 * MUL1), jnp.float32), 'node_attr': jnp.ones((N, 1), jnp.float32), 'edge_scalars': jax.random.normal(ks[1], (E, FC_IN), jnp.float32), 'edge_attr_sh': jax.random.normal(ks[2], (E, 4), jnp.float32), 'edge_src': jax.random.randint(ks[3], (E,), 0, N), 'edge_dst': jax.random.randint(ks[4], (E,), 0, N), 'Wfc1': jax.random.normal(ks[5], (FC_IN, FC_H), jnp.float32), 'Wfc2': jax.random.normal(ks[6], (FC_H, WNUM), jnp.float32), 'Wsc0': jax.random.normal(ks[7], (MUL0, MUL0), jnp.float32), 'Wsc1': jax.random.normal(ks[8], (MUL1, MUL1), jnp.float32), 'Wl1_0': jax.random.normal(ks[9], (MUL0, MUL0), jnp.float32), 'Wl1_1': jax.random.normal(ks[10], (MUL1, MUL1), jnp.float32), 'Wl2_s': jax.random.normal(ks[11], (MUL0 + MUL1, MUL0), jnp.float32), 'Wl2_v': jax.random.normal(ks[12], (MUL0 + MUL1, MUL1), jnp.float32), 'Wa': 0.1 * jax.random.normal(ks[13], (MUL0 + MUL1, 1), jnp.float32)}
    _L1_gnn_all = _L1_gnn_setup()
    _L1_gnn_in = {k: v for k, v in _L1_gnn_all.items() if k in ('Wfc1', 'Wfc2', 'Wsc0', 'Wsc1', 'Wl1_0', 'Wl1_1', 'Wl2_s', 'Wl2_v', 'Wa')}
    del _L1_gnn_all
    return {'x': x, 'src': src, 'dst': dst, 'edge_attr_16': edge_attr_16, 'edge_attr_4': edge_attr_4, 'node_vec1': node_vec1, 'L0_gnn_gamma_s': _L0_gnn_in['gamma_s'], 'L0_gnn_beta_s': _L0_gnn_in['beta_s'], 'L0_gnn_gamma_v': _L0_gnn_in['gamma_v'], 'L0_gnn_Ws_src': _L0_gnn_in['Ws_src'], 'L0_gnn_Wv_src': _L0_gnn_in['Wv_src'], 'L0_gnn_Ws_dst': _L0_gnn_in['Ws_dst'], 'L0_gnn_Wv_dst': _L0_gnn_in['Wv_dst'], 'L0_gnn_W_rbf': _L0_gnn_in['W_rbf'], 'L0_gnn_W_alpha': _L0_gnn_in['W_alpha'], 'L0_gnn_alpha_dot': _L0_gnn_in['alpha_dot'], 'L0_gnn_Ws_val': _L0_gnn_in['Ws_val'], 'L0_gnn_Wv_val': _L0_gnn_in['Wv_val'], 'L0_gnn_Wg': _L0_gnn_in['Wg'], 'L0_gnn_w2_ss': _L0_gnn_in['w2_ss'], 'L0_gnn_w2_sv': _L0_gnn_in['w2_sv'], 'L0_gnn_w2_vs': _L0_gnn_in['w2_vs'], 'L0_gnn_w2_vv0': _L0_gnn_in['w2_vv0'], 'L0_gnn_w2_vv1': _L0_gnn_in['w2_vv1'], 'L0_gnn_Ws_vlin': _L0_gnn_in['Ws_vlin'], 'L0_gnn_Wv_vlin': _L0_gnn_in['Wv_vlin'], 'L0_gnn_Wps': _L0_gnn_in['Wps'], 'L0_gnn_Wpv': _L0_gnn_in['Wpv'], 'L1_gnn_Wfc1': _L1_gnn_in['Wfc1'], 'L1_gnn_Wfc2': _L1_gnn_in['Wfc2'], 'L1_gnn_Wsc0': _L1_gnn_in['Wsc0'], 'L1_gnn_Wsc1': _L1_gnn_in['Wsc1'], 'L1_gnn_Wl1_0': _L1_gnn_in['Wl1_0'], 'L1_gnn_Wl1_1': _L1_gnn_in['Wl1_1'], 'L1_gnn_Wl2_s': _L1_gnn_in['Wl2_s'], 'L1_gnn_Wl2_v': _L1_gnn_in['Wl2_v'], 'L1_gnn_Wa': _L1_gnn_in['Wa']}

def reference(x, src, dst, edge_attr_16, edge_attr_4, node_vec1, L0_gnn_gamma_s, L0_gnn_beta_s, L0_gnn_gamma_v, L0_gnn_Ws_src, L0_gnn_Wv_src, L0_gnn_Ws_dst, L0_gnn_Wv_dst, L0_gnn_W_rbf, L0_gnn_W_alpha, L0_gnn_alpha_dot, L0_gnn_Ws_val, L0_gnn_Wv_val, L0_gnn_Wg, L0_gnn_w2_ss, L0_gnn_w2_sv, L0_gnn_w2_vs, L0_gnn_w2_vv0, L0_gnn_w2_vv1, L0_gnn_Ws_vlin, L0_gnn_Wv_vlin, L0_gnn_Wps, L0_gnn_Wpv, L1_gnn_Wfc1, L1_gnn_Wfc2, L1_gnn_Wsc0, L1_gnn_Wsc1, L1_gnn_Wl1_0, L1_gnn_Wl1_1, L1_gnn_Wl2_s, L1_gnn_Wl2_v, L1_gnn_Wa):
    import jax
    import jax.numpy as jnp

    def _L0_gnn_ref(node, rbf, rsh, gamma_s, beta_s, gamma_v, Ws_src, Wv_src, Ws_dst, Wv_dst, W_rbf, W_alpha, alpha_dot, Ws_val, Wv_val, Wg, w2_ss, w2_sv, w2_vs, w2_vv0, w2_vv1, Ws_vlin, Wv_vlin, Wps, Wpv, edge_index):
        import jax, jax.numpy as jnp
        import numpy as np
        N, E = (2500, 40000)
        CS, CV = (64, 32)
        AS_, AV, H = (16, 8, 4)
        NB = 16
        SQRT3 = 1.7320508075688772
        SQRT2 = 1.4142135623730951
        EPS = 1e-05

        def _cg_tp(s, v, y0, y1, w_ss, w_sv, w_vs, w_vv0, w_vv1):
            out_s = jnp.concatenate([w_ss * s * y0[:, None], w_vv0 * (jnp.einsum('eci,ei->ec', v, y1) / SQRT3)], axis=-1)
            out_v = jnp.concatenate([(w_sv * s)[:, :, None] * y1[:, None, :], (w_vs * jnp.ones_like(v[..., 0]))[..., None] * v * y0[:, None, None], (w_vv1 * jnp.ones_like(v[..., 0]))[..., None] * (jnp.cross(v, y1[:, None, :]) / SQRT2)], axis=1)
            return (out_s, out_v)

        def _equiv_layernorm(s, v, gamma_s, beta_s, gamma_v):
            mu = jnp.mean(s, axis=-1, keepdims=True)
            var = jnp.var(s, axis=-1, keepdims=True)
            s_n = (s - mu) * jax.lax.rsqrt(var + EPS) * gamma_s + beta_s
            rms = jnp.sqrt(jnp.mean(jnp.sum(v * v, axis=-1), axis=-1, keepdims=True) + EPS)
            v_n = v / rms[..., None] * gamma_v[None, :, None]
            return (s_n, v_n)
        n = node.shape[0]
        e = rsh.shape[0]
        s = node[:, :CS]
        v = node[:, CS:].reshape(n, CV, 3)
        s_n, v_n = _equiv_layernorm(s, v, gamma_s, beta_s, gamma_v)
        src, dst = (edge_index[0], edge_index[1])
        msg_s = (s_n @ Ws_src)[src] + (s_n @ Ws_dst)[dst]
        msg_v = jnp.einsum('ncx,cd->ndx', v_n, Wv_src)[src] + jnp.einsum('ncx,cd->ndx', v_n, Wv_dst)[dst]
        y0, y1 = (rsh[:, 0], rsh[:, 1:4])
        w1 = rbf @ W_rbf
        m1_s, m1_v = _cg_tp(msg_s, msg_v, y0, y1, w1[:, :CS], w1[:, CS:2 * CS], w1[:, 2 * CS:2 * CS + CV], w1[:, 2 * CS + CV:2 * CS + 2 * CV], w1[:, 2 * CS + 2 * CV:])
        a = (m1_s @ W_alpha).reshape(e, H, AS_)
        a = jnp.where(a > 0, a, 0.2 * a)
        a = jnp.sum(a * alpha_dot, axis=-1, keepdims=True)
        amax = jax.ops.segment_max(a, dst, num_segments=n)
        amax = jnp.where(jnp.isfinite(amax), amax, 0.0)
        ex = jnp.exp(a - amax[dst])
        den = jax.ops.segment_sum(ex, dst, num_segments=n)
        alpha = ex / (den[dst] + 1e-16)
        val_s = m1_s @ Ws_val
        val_v = jnp.einsum('ecx,cd->edx', m1_v, Wv_val)
        val_v = val_v * jax.nn.sigmoid(val_s @ Wg)[..., None]
        val_s = jax.nn.sigmoid(val_s)
        m2_s, m2_v = _cg_tp(val_s, val_v, y0, y1, w2_ss, w2_sv, w2_vs, w2_vv0, w2_vv1)
        hs = (m2_s @ Ws_vlin).reshape(e, H, AS_)
        hv = jnp.einsum('ecx,cd->edx', m2_v, Wv_vlin).reshape(e, H, AV, 3)
        h = jnp.concatenate([hs, hv.reshape(e, H, AV * 3)], axis=-1)
        agg = jax.ops.segment_sum(alpha * h, dst, num_segments=n)
        agg_s = agg[:, :, :AS_].reshape(n, H * AS_)
        agg_v = agg[:, :, AS_:].reshape(n, H * AV, 3)
        out = node + jnp.concatenate([agg_s @ Wps, jnp.einsum('ncx,cd->ndx', agg_v, Wpv).reshape(n, CV * 3)], axis=-1)
        return out

    def _L1_gnn_ref(x, node_attr, edge_scalars, edge_attr_sh, edge_src, edge_dst, Wfc1, Wfc2, Wsc0, Wsc1, Wl1_0, Wl1_1, Wl2_s, Wl2_v, Wa):
        import jax, jax.numpy as jnp
        import numpy as np
        N = 2500
        E = 40000
        MUL0 = 64
        MUL1 = 32
        FC_IN = 16
        FC_H = 64
        WNUM = 192
        n = x.shape[0]
        x0 = x[:, :MUL0]
        x1 = x[:, MUL0:].reshape(n, MUL1, 3)
        a = node_attr
        h = jax.nn.silu(edge_scalars @ (Wfc1 / jnp.sqrt(jnp.float32(FC_IN))))
        w = h @ (Wfc2 / jnp.sqrt(jnp.float32(FC_H)))
        w0 = w[:, :64]
        w1 = w[:, 64:128]
        w2 = w[:, 128:160]
        w3 = w[:, 160:192]
        inv8 = 1.0 / jnp.sqrt(jnp.float32(MUL0))
        inv32 = 1.0 / jnp.sqrt(jnp.float32(MUL1))
        sc = jnp.concatenate([x0 @ Wsc0 * a * inv8, (jnp.einsum('num,uv->nvm', x1, Wsc1) * a[..., None] * inv32).reshape(n, 3 * MUL1)], axis=1)
        f0 = x0 @ Wl1_0 * a * inv8
        f1 = jnp.einsum('num,uv->nvm', x1, Wl1_1) * a[..., None] * inv32
        e0 = f0[edge_src]
        e1 = f1[edge_src]
        sh0 = edge_attr_sh[:, :1]
        sh1 = edge_attr_sh[:, 1:4]
        mid0 = w0 * e0 * sh0
        mid1 = w3 * jnp.einsum('eum,em->eu', e1, sh1) / jnp.sqrt(3.0)
        mid2 = w1[:, :, None] * e0[:, :, None] * sh1[:, None, :]
        mid3 = w2[:, :, None] * e1 * sh0[:, :, None]
        cnt = jnp.clip(jax.ops.segment_sum(jnp.ones(edge_dst.shape, x.dtype), edge_dst, num_segments=n), 1.0)

        def smean(v):
            s = jax.ops.segment_sum(v, edge_dst, num_segments=n)
            return s / cnt.reshape((n,) + (1,) * (v.ndim - 1))
        n0, n1 = (smean(mid0), smean(mid1))
        n2, n3 = (smean(mid2), smean(mid3))
        scal = jnp.concatenate([n0, n1], axis=1)
        vec = jnp.concatenate([n2, n3], axis=1)
        inv96 = 1.0 / jnp.sqrt(jnp.float32(MUL0 + MUL1))
        alpha = scal @ Wa * a * inv96
        out_s = scal @ Wl2_s * a * inv96
        out_v = jnp.einsum('num,uv->nvm', vec, Wl2_v) * a[..., None] * inv96
        conv = jnp.concatenate([out_s, out_v.reshape(n, 3 * MUL1)], axis=1)
        return sc + alpha * conv
    edge_index = jnp.stack([src, dst])
    x = _layernorm(x + _L0_gnn_ref(x, edge_attr_16, edge_attr_4, L0_gnn_gamma_s, L0_gnn_beta_s, L0_gnn_gamma_v, L0_gnn_Ws_src, L0_gnn_Wv_src, L0_gnn_Ws_dst, L0_gnn_Wv_dst, L0_gnn_W_rbf, L0_gnn_W_alpha, L0_gnn_alpha_dot, L0_gnn_Ws_val, L0_gnn_Wv_val, L0_gnn_Wg, L0_gnn_w2_ss, L0_gnn_w2_sv, L0_gnn_w2_vs, L0_gnn_w2_vv0, L0_gnn_w2_vv1, L0_gnn_Ws_vlin, L0_gnn_Wv_vlin, L0_gnn_Wps, L0_gnn_Wpv, edge_index), axis=-1)
    x = _layernorm(x + _L1_gnn_ref(x, node_vec1, edge_attr_16, edge_attr_4, src, dst, L1_gnn_Wfc1, L1_gnn_Wfc2, L1_gnn_Wsc0, L1_gnn_Wsc1, L1_gnn_Wl1_0, L1_gnn_Wl1_1, L1_gnn_Wl2_s, L1_gnn_Wl2_v, L1_gnn_Wa), axis=-1)
    return x

_drawn_inputs = setup_inputs


def setup_inputs(seed=0):
    import zlib

    import numpy as np

    out = dict(_drawn_inputs(seed))
    spreads = {'L0_gnn_gamma_s': (1.0, 0.6), 'L0_gnn_beta_s': (0.0, 0.8), 'L0_gnn_gamma_v': (1.0, 0.6)}
    factors = {'L0_gnn_w2_vv1': 2.918,
     'L1_gnn_Wfc1': 8.0,
     'L1_gnn_Wfc2': 8.0,
     'L1_gnn_Wl1_0': 8.0,
     'L1_gnn_Wl1_1': 8.0,
     'L1_gnn_Wl2_s': 8.0,
     'L1_gnn_Wl2_v': 8.0,
     'L1_gnn_Wa': 8.0,
     'L1_gnn_Wsc0': 4.772,
     'L1_gnn_Wsc1': 4.137}
    for name, (base, spread) in spreads.items():
        noise = np.random.default_rng([zlib.crc32(name.encode()), seed]).standard_normal(out[name].shape)
        drawn = base * np.exp(spread * noise) if base else spread * noise
        out[name] = jnp.asarray(drawn.astype(out[name].dtype))
    for name, factor in factors.items():
        out[name] = (out[name] * factor).astype(out[name].dtype)
    return out
```

```python
import concourse.bass as bass
from concourse import mybir
from contextlib import ExitStack

P = 128
TG = 4
S, V, C = 64, 96, 32
D = S + V
H = 4
AGG0 = D + 2 * H
AGG1 = D + 2
OFF = 3.0e38
NODE_BATCH = 7
F32, BF16, I32 = mybir.dt.float32, mybir.dt.bfloat16, mybir.dt.int32
ALU, ACT, AX = mybir.AluOpType, mybir.ActivationFunctionType, mybir.AxisListType.X


def rep(ap, axis, n):
    ap = ap.unsqueeze(axis)
    shape = list(ap.shape)
    shape[axis] = n
    return ap.broadcast_to(shape)


def need(eng, sem, value):
    if isinstance(value, int) and value <= 0:
        return
    eng.wait_ge(sem, value)


def settle(eng):
    eng.nop(nofuse=True)


def hold(sp, sem, value):
    need(sp, sem, value)
    if not isinstance(value, int):
        settle(sp)


class Chain:

    def __init__(self, eng, sem):
        self.eng, self.sem, self.count = eng, sem, 0

    def link(self, ins):
        ins.then_inc(self.sem, 1)
        self.count = self.count + 1
        return self.count

    def wait(self, mark=None):
        self.eng.wait_ge(self.sem, self.count if mark is None else mark)


class Group:

    def __init__(self, base, slot):
        self.base, self.slot, self.n = base, slot, base + slot

    def back(self, k):
        if self.slot >= k:
            return Group(self.base, self.slot - k)
        return Group(self.base - 4, self.slot - k + 4)

    def loads(self, unit):
        return self.base * (unit // 4) + unit


def steps(eng_or_nc, groups, step):
    for n in range(4):
        step(Group(0, n), True, n >= 1, n >= 2)
    with eng_or_nc.Fori(1, groups // 4, 1) as i:
        for u in range(4):
            step(Group(i * 4, u), True, True, True)
    step(Group(groups, 0), False, True, True)
    step(Group(groups, 1), False, False, True)


def build(nc, ins, out, weights_at, NT, NK):
    NG = NT // TG
    SB = NT // P
    EP = NT * P
    NB = NK // NODE_BATCH
    ctx = ExitStack()
    with ctx:
        def dram(name, shape, dt=F32):
            return nc.dram_tensor(name, shape, dt, kind="Internal").ap()

        def sem(name):
            return ctx.enter_context(nc.semaphore(name))

        def sb(name, shape, dt=F32, where=ctx):
            return where.enter_context(nc.sbuf_tensor(name, shape, dt))

        rbf_parts = dram("rbf_parts", (3, 16, EP), BF16)
        edge_cut = dram("edge_cut", (NG, TG * H, P + 1))
        src_table = dram("src_table", (NK * P, D))
        dst_table = dram("dst_table", (NK * P, D))
        conv_table = dram("conv_table", (NK * P, D))
        agg0 = dram("agg0", (EP, AGG0))
        agg1 = dram("agg1", (EP, AGG1))
        carry0 = dram("carry0", (NT + 1, AGG0))
        carry1 = dram("carry1", (NT + 1, AGG1))

        banks = [ctx.enter_context(nc.psum_tensor(f"bank{i}", [P, 512], F32)) for i in range(8)]
        W = sb("W", [P, weights_at["_width"]])

        def wt(name, rows=None, c0=0, c1=None):
            at, r, c = weights_at[name]
            return W[0:r, at + c0:at + (c if c1 is None else c1)]

        ident = sb("ident", [P, P])
        rbf_w = sb("rbf_w", [P, 416], BF16)
        row_idx = sb("row_idx", [P, NK], I32)
        carry_idx = sb("carry_idx", [P, NK], I32)
        has_row = sb("has_row", [P, NK])
        has_carry = sb("has_carry", [P, NK])
        node_a = sb("node_a", [P, NK])
        stat = sb("stat", [P, NK])
        stat2 = sb("stat2", [P, NK])

        with ExitStack() as ph:
            wload, split_load, cut_load = sem("wload"), sem("split_load"), sem("cut_load")
            stored, eye, prod, made, dma_w = (sem("prep_stored"), sem("eye"), sem("gate_product"),
                                              sem("prep_vector"), sem("prep_moved"))
            hi_done, mid_done, rest_done, low_done = (sem("split_hi"), sem("split_mid"), sem("split_rest"),
                                                      sem("split_low"))
            wr = sb("wr", [P, 416], F32, ph)
            wparts = [sb(f"wpart{i}", [P, 416], BF16, ph) for i in range(3)]
            xin = sb("xin", [P, 2048], F32, ph)
            xrest = sb("xrest", [P, 2048], F32, ph)
            xp = [sb(f"xp{i}", [P, 2048], BF16, ph) for i in range(3)]
            dsts = sb("dsts", [P, SB, P + 1], I32, ph)
            cut = sb("cut", [P, SB, P + 1], F32, ph)
            zrow = sb("zrow", [P, AGG0], F32, ph)
            rbf_v = ins["rbf_t"].rearrange("c (h n) -> (c h) n", h=8)
            parts_v = [rbf_parts[i].rearrange("c (h n) -> (c h) n", h=8) for i in range(3)]

            with nc.Block() as block:
                @block.sync
                def _(sp):
                    sp.dma_start(W[:, :], ins["weights"]).then_inc(wload, 16)
                    for c in range(8):
                        sp.dma_start(wr[16 * c:16 * c + 16, :], ins["rbf_w"]).then_inc(wload, 16)
                    sp.dma_start(dsts[:, :, :], ins["dst_rows"].rearrange("(b t) e -> t b e", t=P))\
                        .then_inc(cut_load, 16)
                    sp.dma_start(node_a[:, :], ins["node_a"]).then_inc(wload, 16)
                    hold(sp, made, 3)
                    for c, wp in enumerate((0, 1, 2, 0, 1, 2, 0, 1)):
                        sp.dma_start(rbf_w[16 * c:16 * c + 16, :], wparts[wp][16 * c:16 * c + 16, :])\
                            .then_inc(dma_w, 16)
                    hold(sp, dma_w, 128)
                    for b in range(SB):
                        if b >= 1:
                            hold(sp, stored, 48 * b)
                        sp.dma_start(xin[:, :], rbf_v[:, 2048 * b:2048 * b + 2048]).then_inc(split_load, 16)
                        hold(sp, hi_done, b + 1)
                        sp.dma_start(parts_v[0][:, 2048 * b:2048 * b + 2048], xp[0][:, :]).then_inc(stored, 16)
                        hold(sp, mid_done, b + 1)
                        sp.dma_start(parts_v[1][:, 2048 * b:2048 * b + 2048], xp[1][:, :]).then_inc(stored, 16)
                        hold(sp, low_done, b + 1)
                        sp.dma_start(parts_v[2][:, 2048 * b:2048 * b + 2048], xp[2][:, :]).then_inc(stored, 16)
                    hold(sp, stored, 48 * SB)
                    hold(sp, made, 6)
                    for h in range(H):
                        sp.dma_start(edge_cut.rearrange("g (j h) e -> h (g j) e", h=H)[h]
                                     .rearrange("(b t) e -> t b e", t=P), cut[:, :, :]).then_inc(dma_w, 16)
                    sp.dma_start(carry0[0:1, :], zrow[0:1, :]).then_inc(dma_w, 16)
                    sp.dma_start(carry1[0:1, :], zrow[0:1, 0:AGG1]).then_inc(dma_w, 16)
                    hold(sp, dma_w, 128 + 16 * (H + 2))

                @block.gpsimd
                def _(pool):
                    pool.memset(ident[:, :], 0.0).then_inc(eye, 1)
                    pool.wait_ge(eye, 1)
                    pool.affine_select(out=ident[:, :], in_=ident[:, :], compare_op=ALU.not_equal, fill=1.0,
                                       base=0, pattern=[[-1, P]], channel_multiplier=1).then_inc(eye, 1)

                @block.scalar
                def _(act):
                    for b in range(SB):
                        act.wait_ge(split_load, 16 * b + 16)
                        act.activation(xp[0][:, :], xin[:, :], ACT.Copy).then_inc(hi_done, 1)
                        act.wait_ge(rest_done, b + 1)
                        act.activation(xp[1][:, :], xrest[:, :], ACT.Copy).then_inc(mid_done, 1)

                @block.vector
                def _(dve):
                    ch = Chain(dve, sem("prep_chain"))
                    dve.wait_ge(wload, 160)
                    dve.tensor_copy(wparts[0][:, :], wr[:, :]).then_inc(made, 1)
                    dve.wait_ge(made, 1)
                    ch.link(dve.tensor_tensor(wr[:, :], wr[:, :], wparts[0][:, :], ALU.subtract))
                    ch.wait()
                    dve.tensor_copy(wparts[1][:, :], wr[:, :]).then_inc(made, 1)
                    dve.wait_ge(made, 2)
                    dve.tensor_tensor(wparts[2][:, :], wr[:, :], wparts[1][:, :], ALU.subtract).then_inc(made, 1)
                    dve.wait_ge(cut_load, 16)
                    ch.link(dve.tensor_tensor(cut[:, :, 1:P], dsts[:, :, 2:P + 1], dsts[:, :, 1:P], ALU.not_equal))
                    ch.wait()
                    dve.tensor_scalar(cut[:, :, 1:P], cut[:, :, 1:P], -OFF, None, ALU.mult).then_inc(made, 1)
                    dve.memset(cut[:, :, 0:P + 1:P], -OFF).then_inc(made, 1)
                    dve.memset(zrow[:, :], 0.0).then_inc(made, 1)
                    r3, r2 = 3.0 ** -0.5, 2.0 ** -0.5
                    dve.wait_ge(prod, 1)
                    ch.link(dve.tensor_copy(wt("W1a", c0=64, c1=96)[64:128], banks[0][64:128, 0:C]))
                    ch.link(dve.tensor_copy(wt("W1b", c0=64, c1=96)[96:128], banks[1][96:128, 0:C]))
                    ch.wait()
                    ch.link(dve.tensor_scalar(wt("W1b")[96:128], wt("W1b")[96:128], r3, None, ALU.mult))
                    ch.link(dve.tensor_scalar(wt("W1c"), wt("W1c"), r2, None, ALU.mult))
                    for k, (n, f) in enumerate((("W2a", 0.5), ("W2b", 0.5), ("W2c", 0.5 * r2))):
                        r = weights_at[n][1]
                        ch.link(dve.tensor_scalar(wt(n), wt(n), wt("r2")[0:r, k:k + 1], f, ALU.mult, ALU.mult))
                    ch.wait()
                    ch.link(dve.tensor_scalar(wt("W2b")[96:128], wt("W2b")[96:128], r3, None, ALU.mult))
                    ch.link(dve.tensor_scalar(wt("W3a")[0:64], wt("W3a")[0:64], 0.125, None, ALU.mult))
                    ch.link(dve.tensor_scalar(wt("W3a")[64:128], wt("W3a")[64:128], 32.0 ** -0.5, None, ALU.mult))
                    ch.link(dve.tensor_scalar(wt("W3b"), wt("W3b"), 32.0 ** -0.5, None, ALU.mult))
                    ch.link(dve.tensor_scalar(wt("Wfc2"), wt("Wfc2"), 0.125 * 0.125, None, ALU.mult))
                    for n in ("W4a", "W4b", "W4c"):
                        ch.link(dve.tensor_scalar(wt(n), wt(n), 96.0 ** -0.5, None, ALU.mult))
                    ch.wait()
                    ch.link(dve.tensor_scalar(wt("W4a")[64:96], wt("W4a")[64:96], r3, None, ALU.mult))
                    ch.wait()
                    for b in range(SB):
                        dve.wait_ge(hi_done, b + 1)
                        dve.tensor_tensor(xrest[:, :], xin[:, :], xp[0][:, :], ALU.subtract).then_inc(rest_done, 1)
                        dve.wait_ge(mid_done, b + 1)
                        dve.tensor_tensor(xp[2][:, :], xrest[:, :], xp[1][:, :], ALU.subtract).then_inc(low_done, 1)

                @block.tensor
                def _(pe):
                    pe.wait_ge(wload, 160)
                    pe.matmul(banks[0][:, 0:C], wt("WvT1"), wt("Wg"), start=True, stop=True)
                    pe.matmul(banks[1][:, 0:C], wt("WvT2"), wt("Wg"), start=True, stop=True).then_inc(prod, 1)

        with ExitStack() as ph:
            X = sb("X", [P, NK, D], F32, ph)
            scr = sb("scr", [P, NK, V], F32, ph)
            nf = sb("nf", [P, NK], F32, ph)
            n_int = sb("n_int", [P, NK], I32, ph)
            level = sb("level", [P, NK], F32, ph)
            found = sb("found", [P, NK], F32, ph)
            level_i = sb("level_i", [P, NK], I32, ph)
            idx_s = sb("idx_s", [P, NODE_BATCH], I32, ph)
            sup = sb("sup", [P, SB], I32, ph)
            rows = sb("rows", [P, NODE_BATCH, P + 1], I32, ph)
            cmp = sb("cmp", [P, NODE_BATCH, P], F32, ph)
            xk = [sb(f"xk{i}", [P, D], F32, ph) for i in range(2)]
            xts = [sb(f"xts{i}", [S, P], F32, ph) for i in range(2)]
            xtv = [sb(f"xtv{i}", [V, P], F32, ph) for i in range(2)]
            tab = [sb(f"ntab{i}", [P, 2 * D], F32, ph) for i in range(2)]
            xload, normed, copied, xT, evacT, projd, tabbed, rooted, varred = (
                sem("xload"), sem("node_normed"), sem("node_copied"), sem("node_T"), sem("node_T_out"),
                sem("node_projected"), sem("node_tab"), sem("node_rooted"), sem("node_var"))
            tab_out = [sem(f"node_tab_stored{i}") for i in range(2)]
            iota_done, lvl_idx, idx_copied, batch_done = (sem("iota"), sem("level_index"), sem("index_copied"),
                                                          sem("batch_compared"))
            rows_in = [sem(f"rows_in{i}") for i in range(2)]
            src_v = src_table.rearrange("(p k) d -> p k d", k=NK)
            dst_v = dst_table.rearrange("(p k) d -> p k d", k=NK)
            last_rows = ins["last"].rearrange("(b t) -> b t", t=P)

            def node_loop(eng, body):
                for k in range(2):
                    body(k, k)
                with eng.Fori(1, NK // 2, 1) as i:
                    for u in range(2):
                        body(i * 2 + u, u)

            def batch_loop(eng, body):
                body(0)
                if NB > 1:
                    with eng.Fori(1, NB, 1) as b:
                        body(b)

            with nc.Block() as block:
                @block.sync
                def _(sp):
                    sp.dma_start(X[:, :, :], ins["x"].rearrange("(p k) d -> p k d", k=NK)).then_inc(xload, 16)
                    sp.dma_start(sup[:, :], ins["sup"].partition_broadcast(P)).then_inc(xload, 16)

                    def store(k, q):
                        hold(sp, tabbed, k + 1)
                        sp.dma_start(src_v[:, bass.ds(k, 1), :].squeeze(1), tab[q][:, 0:D]).then_inc(tab_out[q], 16)
                        sp.dma_start(dst_v[:, bass.ds(k, 1), :].squeeze(1), tab[q][:, D:2 * D])\
                            .then_inc(tab_out[q], 16)
                    node_loop(sp, store)
                    for q in range(2):
                        hold(sp, tab_out[q], 32 * (NK // 2))

                @block.gpsimd
                def _(pool):
                    pool.iota(n_int[:, :], pattern=[[1, NK]], base=0, channel_multiplier=NK).then_inc(iota_done, 1)
                    for lvl in range(2):
                        table = last_rows if lvl == 0 else ins["dst_rows"]
                        width = P if lvl == 0 else P + 1

                        def batch(b):
                            if isinstance(b, int) and b == 0:
                                pool.wait_ge(lvl_idx, lvl + 1)
                                need(pool, batch_done, lvl * NB)
                            else:
                                pool.wait_ge(batch_done, b + lvl * NB)
                            pool.tensor_copy(idx_s[:, :], level_i[:, bass.ds(b * NODE_BATCH, NODE_BATCH)])\
                                .then_inc(idx_copied, 1)
                            pool.wait_ge(idx_copied, b + (lvl * NB + 1))
                            settle(pool)
                            for j in range(NODE_BATCH):
                                pool.indirect_dma_start(
                                    out=rows[:, j, 0:width], out_offset=None, in_=table,
                                    in_offset=bass.IndirectOffsetOnAxis(ap=idx_s[:, j:j + 1], axis=0)
                                ).then_inc(rows_in[lvl], 16)
                        batch_loop(pool, batch)

                @block.scalar
                def _(act):
                    act.wait_ge(varred, 2)
                    act.activation(stat[:, :], stat[:, :], ACT.Sqrt).then_inc(rooted, 1)
                    act.activation(stat2[:, :], stat2[:, :], ACT.Sqrt).then_inc(rooted, 1)
                    act.wait_ge(normed, 2)

                    def body(k, q):
                        need(act, xT, k - 1)
                        act.activation(xk[q][:, :], X[:, bass.ds(k, 1), :].squeeze(1), ACT.Copy).then_inc(copied, 1)
                        act.wait_ge(xT, k + 1)
                        need(act, projd, k - 1)
                        act.activation(xts[q][:, :], banks[2 * q][0:S, 0:P], ACT.Identity,
                                       scale=wt("gs"), bias=wt("bs"))
                        act.activation(xtv[q][:, :], banks[2 * q][0:V, P:2 * P], ACT.Copy,
                                       scale=wt("gv")).then_inc(evacT, 1)
                        act.wait_ge(projd, k + 1)
                        if not (isinstance(k, int) and k < 2):
                            act.wait_ge(tab_out[q], k * 16 - 16 * q)
                        act.activation(tab[q][:, :], banks[2 * q + 1][:, 0:2 * D], ACT.Copy).then_inc(tabbed, 1)
                    node_loop(act, body)

                @block.tensor
                def _(pe):
                    def body(k, q):
                        pe.wait_ge(copied, k + 1)
                        need(pe, evacT, k - 1)
                        settle(pe)
                        pe.transpose(banks[2 * q][0:S, 0:P], xk[q][:, 0:S], ident[:, :])
                        pe.transpose(banks[2 * q][0:V, P:2 * P], xk[q][:, S:D], ident[:, :]).then_inc(xT, 1)
                        pe.wait_ge(evacT, k + 1)
                        need(pe, tabbed, k - 1)
                        o = banks[2 * q + 1]
                        for t in range(2):
                            pe.matmul(o[:, D * t:D * t + S], xts[q][:, :], wt("WsSD", c0=S * t, c1=S * t + S),
                                      start=True, stop=True)
                            mm = pe.matmul(o[:, D * t + S:D * t + D], xtv[q][:, :],
                                           wt("WvSD", c0=V * t, c1=V * t + V), start=True, stop=True)
                        mm.then_inc(projd, 1)
                    node_loop(pe, body)

                @block.vector
                def _(dve):
                    ch = Chain(dve, sem("node_chain"))
                    dve.wait_ge(xload, 32)
                    Xs, Xv = X[:, :, 0:S], X[:, :, S:D]
                    ch.link(dve.tensor_reduce(stat[:, :], Xs, AX, ALU.add)); ch.wait()
                    ch.link(dve.tensor_scalar(stat[:, :], stat[:, :], 1.0 / S, None, ALU.mult)); ch.wait()
                    ch.link(dve.tensor_tensor(Xs, Xs, rep(stat[:, :], 2, S), ALU.subtract)); ch.wait()
                    ch.link(dve.tensor_tensor(scr[:, :, 0:S], Xs, Xs, ALU.mult)); ch.wait()
                    ch.link(dve.tensor_reduce(stat[:, :], scr[:, :, 0:S], AX, ALU.add)); ch.wait()
                    dve.tensor_scalar(stat[:, :], stat[:, :], 1.0 / S, 1e-5, ALU.mult, ALU.add).then_inc(varred, 1)
                    ch.link(dve.tensor_tensor(scr[:, :, :], Xv, Xv, ALU.mult)); ch.wait()
                    ch.link(dve.tensor_reduce(stat2[:, :], scr[:, :, :], AX, ALU.add)); ch.wait()
                    dve.tensor_scalar(stat2[:, :], stat2[:, :], 1.0 / C, 1e-5, ALU.mult, ALU.add).then_inc(varred, 1)
                    dve.wait_ge(rooted, 2)
                    ch.link(dve.reciprocal(stat[:, :], stat[:, :]))
                    ch.link(dve.reciprocal(stat2[:, :], stat2[:, :])); ch.wait()
                    dve.tensor_tensor(Xs, Xs, rep(stat[:, :], 2, S), ALU.mult).then_inc(normed, 1)
                    dve.tensor_tensor(Xv, Xv, rep(stat2[:, :], 2, V), ALU.mult).then_inc(normed, 1)
                    dve.wait_ge(iota_done, 1)
                    ch.link(dve.tensor_copy(nf[:, :], n_int[:, :])); ch.wait()
                    ch.link(dve.tensor_tensor(scr[:, :, 0:SB], rep(sup[:, :], 1, NK), rep(nf[:, :], 2, SB),
                                              ALU.is_le)); ch.wait()
                    ch.link(dve.tensor_reduce(level[:, :], scr[:, :, 0:SB], AX, ALU.add)); ch.wait()
                    ch.link(dve.tensor_scalar(level[:, :], level[:, :], float(SB - 1), None, ALU.min)); ch.wait()
                    dve.tensor_copy(level_i[:, :], level[:, :]).then_inc(lvl_idx, 1)

                    def count(lvl, first):
                        def batch(b):
                            dve.wait_ge(rows_in[lvl], b * (16 * NODE_BATCH) + 16 * NODE_BATCH)
                            cols = bass.ds(b * NODE_BATCH, NODE_BATCH)
                            e0 = 0 if lvl == 0 else 1
                            dve.tensor_tensor(cmp[:, :, :], rows[:, :, e0:e0 + P], rep(nf[:, cols], 2, P), ALU.is_le)\
                                .then_inc(cmp_step, 1)
                            s = 1 if lvl == 0 else 4
                            dve.wait_ge(cmp_step, b * s + (first + 1))
                            if lvl == 0:
                                dve.tensor_reduce(found[:, cols], cmp[:, :, :], AX, ALU.add).then_inc(batch_done, 1)
                                return
                            dve.tensor_reduce(found[:, cols], cmp[:, :, :], AX, ALU.add).then_inc(cmp_step, 1)
                            dve.wait_ge(cmp_step, b * 4 + (first + 2))
                            dve.tensor_tensor(cmp[:, :, :], rows[:, :, 1:P + 1], rep(nf[:, cols], 2, P),
                                              ALU.is_equal).then_inc(cmp_step, 1)
                            dve.wait_ge(cmp_step, b * 4 + (first + 3))
                            dve.tensor_reduce(has_row[:, cols], cmp[:, :, :], AX, ALU.max).then_inc(cmp_step, 1)
                            dve.tensor_tensor(has_carry[:, cols], rows[:, :, 0], nf[:, cols], ALU.is_equal)\
                                .then_inc(batch_done, 1)
                        return batch
                    cmp_step = sem("compare_step")
                    batch_loop(dve, count(0, 0))
                    dve.wait_ge(batch_done, NB)
                    ch.link(dve.scalar_tensor_tensor(out=level[:, :], in0=level[:, :], scalar=float(P),
                                                     in1=found[:, :], op0=ALU.mult, op1=ALU.add)); ch.wait()
                    ch.link(dve.tensor_scalar(level[:, :], level[:, :], float(NT - 1), None, ALU.min)); ch.wait()
                    dve.tensor_copy(level_i[:, :], level[:, :]).then_inc(lvl_idx, 1)
                    dve.wait_ge(lvl_idx, 2)
                    ch.link(dve.tensor_copy(carry_idx[:, :], level_i[:, :]))
                    batch_loop(dve, count(1, NB))
                    dve.wait_ge(batch_done, 2 * NB)
                    ch.link(dve.tensor_scalar(found[:, :], found[:, :], -1.0, 0.0, ALU.add, ALU.max)); ch.wait()
                    ch.link(dve.scalar_tensor_tensor(out=level[:, :], in0=level[:, :], scalar=float(P),
                                                     in1=found[:, :], op0=ALU.mult, op1=ALU.add)); ch.wait()
                    ch.link(dve.tensor_copy(row_idx[:, :], level[:, :])); ch.wait()

        edge_loop_0(nc, ctx, sem, banks, W, wt, ident, rbf_w, ins, rbf_parts, edge_cut, src_table, dst_table,
                    agg0, NG)
        carry_scan(nc, ctx, sem, banks, ident, ins, agg0, carry0, NT, AGG0, True)

        X1 = sb("X1", [P, NK, D])
        node_step_0(nc, ctx, sem, banks, wt, ident, ins, agg0, carry0, conv_table, X1, row_idx, carry_idx,
                    has_row, has_carry, node_a, stat, stat2, NK)
        edge_loop_1(nc, ctx, sem, banks, wt, rbf_w, ins, rbf_parts, conv_table, agg1, NG)
        carry_scan(nc, ctx, sem, banks, ident, ins, agg1, carry1, NT, AGG1, False)
        node_step_1(nc, ctx, sem, banks, agg1, carry1, out, X1, row_idx, carry_idx, has_row, has_carry,
                    node_a, stat, NK)


def edge_loop_0(nc, ctx, sem, banks, W, wt, ident, rbf_w, ins, rbf_parts, edge_cut, src_table, dst_table,
                agg0, NG):
    with ExitStack() as ph:
        def sb(name, shape, dt=F32):
            return ph.enter_context(nc.sbuf_tensor(name, shape, dt))
        pack = [sb(f"e_pack{i}", [P, 32], I32) for i in range(4)]
        idx = [p[:, 0:8] for p in pack]
        Y = [p[:, 8:32].bitcast(F32).rearrange("p (t c) -> p t c", t=TG) for p in pack]
        xs = [sb(f"e_xs{i}", [P, 512], BF16) for i in range(4)]
        drow = [sb(f"e_drow{i}", [P, 512], I32) for i in range(4)]
        cut = [sb(f"e_cut{i}", [16, P + 1]) for i in range(4)]
        feat = [sb(f"feat{i}", [P, TG, D + 64]) for i in range(4)]
        stg = [sb(f"stg{i}", [P, TG, 352]) for i in range(2)]
        feat2 = sb("mid_feat", [P, TG, D + 64])
        tmp = [sb(f"tmp{i}", [P, TG, V]) for i in range(6)]
        vlin = sb("vlin", [P, TG, V])
        tabs = [sb(f"tabs{k}", [P, 512]) for k in range(3)]
        prods = [sb(f"prods{k}", [P, 512]) for k in range(3)]
        st2 = [sb(f"st2_{k}", [P, 512]) for k in range(3)]
        lg = sb("lg", [P, TG, S])
        th = [sb(f"th{i}", [P, TG, V]) for i in range(2)]
        av = [sb(f"av{i}", [P, TG, 192]) for i in range(2)]
        gate = sb("gate", [P, TG, C])
        a_e = sb("a_e", [P, 16])
        one = sb("one", [P, 1])
        run_max = sb("run_max", [16, P])
        seg_max = sb("seg_max", [16, P])
        diff = sb("diff", [P, 16])
        ex8 = sb("ex8", [P, TG, C])
        ha = [sb(f"ha{i}", [P, TG, D + H]) for i in range(2)]
        hv = sb("hv", [P, TG, V])
        eq = [sb(f"eq{i}", [P, TG, P]) for i in range(4)]
        orow = [sb(f"orow{i}", [P, TG, AGG0]) for i in range(2)]

        small_in = [sem(f"l0_small_in{i}") for i in range(4)]
        big_in = [sem(f"l0_big_in{i}") for i in range(4)]
        gathered = [sem(f"l0_gathered{i}") for i in range(4)]
        out_done = [sem(f"l0_out_done{i}") for i in range(2)]
        (table_mm, table_out, v_dup, scaled1, v2_done, v2_dup, scaled2, gated, staged1, staged1_T, product,
         stage1, stage1_out, logit, logit_T, logit_read, maxed, max_T, diffed, exped, max_out, staged2,
         staged2_T, st2_out, stage2, eq_made, ha_made, agg, agg_out) = (sem("l0_" + n) for n in (
             "table_mm", "table_out", "v_dup", "scaled1", "v2_done", "v2_dup", "scaled2", "gated", "staged1",
             "staged1_T", "product", "stage1", "stage1_out", "logit", "logit_T", "logit_read", "maxed", "max_T",
             "diffed", "exped", "max_out", "staged2", "staged2_T", "st2_out", "stage2", "eq_made", "ha_made",
             "agg", "agg_out"))
        own, one_made = sem("l0_vector_chain"), sem("l0_one_made")
        agg_v = agg0.rearrange("(g j p) c -> g p j c", j=TG, p=P)
        xs_v = rbf_parts.rearrange("s c (g n) -> s g c n", n=512)
        drow_v = ins["dst_flat"].rearrange("(g n) -> g n", n=512)
        PARTS = ((0, 3), (1, 3), (2, 2))

        with nc.Block() as block:
            @block.sync
            def _(sp):
                def step(g, front, mid, tail):
                    if front:
                        s, n = g.slot, g.n
                        hold(sp, table_mm, 3 * (n - 3))
                        hold(sp, eq_made, n - 3)
                        hold(sp, maxed, n - 3)
                        hold(sp, ha_made, n - 3)
                        if not (isinstance(g.base, int) and g.base == 0):
                            hold(sp, gathered[s], g.base * 32)
                        at = bass.ds(n, 1)
                        sp.dma_start(pack[s][:, :], ins["edge_pack"][at].squeeze(0)).then_inc(small_in[s], 16)
                        sp.dma_start(cut[s][:, :], edge_cut[at].squeeze(0)).then_inc(small_in[s], 16)
                        c0 = 0
                        for part, copies in PARTS:
                            sp.dma_start(xs[s][c0:c0 + 16 * copies, :], rep(xs_v[part, at], 0, copies).squeeze(1))\
                                .then_inc(big_in[s], 16)
                            c0 += 16 * copies
                        sp.dma_start(drow[s][:, :], drow_v[at].broadcast_to([P, 512])).then_inc(big_in[s], 16)
                steps(sp, NG, step)

            @block.gpsimd
            def _(pool):
                def gather(table, s, col, j, op):
                    pool.indirect_dma_start(
                        out=feat[s][:, j, 0:D], out_offset=None, in_=table,
                        in_offset=bass.IndirectOffsetOnAxis(ap=idx[s][:, col + j:col + j + 1], axis=0),
                        compute_op=op).then_inc(gathered[s], 16)

                def step(g, front, mid, tail):
                    if front:
                        s = g.slot
                        need(pool, staged1, g.n - 3)
                        need(pool, scaled1, g.n - 3)
                        pool.wait_ge(small_in[s], g.loads(32))
                        settle(pool)
                        for j in range(TG):
                            gather(src_table, s, 0, j, ALU.bypass)
                    if mid:
                        m = g.back(1)
                        s = m.slot
                        pool.wait_ge(gathered[s], m.base * 32 + 64)
                        settle(pool)
                        for j in range(TG):
                            gather(dst_table, s, 4, j, ALU.add)
                steps(pool, NG, step)

            @block.vector
            def _(dve):
                ch = Chain(dve, own)

                def comp(ap, c0, n=3, w=C):
                    return ap[:, :, c0:c0 + n * w].rearrange("p t (x c) -> p t x c", c=w)

                def yx(y, c0, w=C):
                    return rep(y[:, :, c0:c0 + 3], 3, w)

                def products_with_y(st, f, tmp, y, dup_sem, dup_at, last_sem):
                    a = ch.link(dve.tensor_tensor(comp(tmp[0], 0), comp(f, S), yx(y, 1), ALU.mult))
                    dve.wait_ge(dup_sem, dup_at)
                    b = ch.link(dve.tensor_tensor(comp(tmp[1], 0), comp(f, S + C), yx(y, 3), ALU.mult))
                    ch.wait(a)
                    a = ch.link(dve.tensor_tensor(st[:, :, 224:256], tmp[0][:, :, 0:C], tmp[0][:, :, C:2 * C],
                                                  ALU.add))
                    c = ch.link(dve.tensor_tensor(comp(tmp[2], 0), comp(f, S + 2 * C), yx(y, 2), ALU.mult))
                    ch.wait(a)
                    ch.link(dve.tensor_tensor(st[:, :, 224:256], st[:, :, 224:256], tmp[0][:, :, 2 * C:V],
                                              ALU.add))
                    ch.wait(c)
                    dve.tensor_tensor(st[:, :, 256:352], tmp[1][:, :, :], tmp[2][:, :, :], ALU.subtract)\
                        .then_inc(last_sem, 1)

                def step(g, front, mid, tail):
                    n = g.n
                    if tail:
                        t = g.back(2)
                        y, q = Y[t.slot], t.slot % 2
                        dve.wait_ge(max_T, t.n + 1)
                        need(dve, exped, t.n)
                        dve.tensor_tensor(diff[:, :], a_e[:, :], banks[7][:, 328:344], ALU.subtract)\
                            .then_inc(diffed, 1)
                    if front:
                        s = g.slot
                        dve.wait_ge(gathered[s], g.loads(128))
                        need(dve, staged1_T, 3 * n)
                        need(dve, staged1, n)
                        products_with_y(stg[0], feat[s], tmp[0:3], Y[s], v_dup, n + 1, staged1)
                    if tail:
                        dve.wait_ge(exped, t.n + 1)
                        need(dve, ha_made, t.n)
                        marks = []
                        for b in range(2):
                            dve.wait_ge(stage2, 2 * t.n + (b + 1))
                            o = banks[5 + b][:, 0:384].rearrange("p (t c) -> p t c", t=2)
                            ts2 = slice(2 * b, 2 * b + 2)
                            marks.append(ch.link(dve.tensor_tensor(
                                hv[:, ts2, :].rearrange("p t (x c) -> p t x c", c=C), rep(o[:, :, 64:96], 2, 3),
                                rep(y[:, ts2, 1:4], 3, C), ALU.mult)))
                            ch.link(dve.tensor_tensor(
                                ha[q][:, ts2, 0:S].rearrange("p t (h c) -> p t h c", h=H),
                                o[:, :, 0:64].rearrange("p t (h c) -> p t h c", h=H),
                                rep(ha[q][:, ts2, D:D + H], 3, 16), ALU.mult))
                        for b in range(2):
                            ts2 = slice(2 * b, 2 * b + 2)
                            o = banks[5 + b][:, 0:384].rearrange("p (t c) -> p t c", t=2)
                            ch.wait(marks[b])
                            ch.link(dve.tensor_tensor(hv[:, ts2, :], hv[:, ts2, :], o[:, :, 96:192], ALU.add))
                    if mid:
                        m = g.back(1)
                        q, y = m.slot % 2, Y[m.slot]
                        dve.wait_ge(stage1_out, 4 * (m.n + 1))
                        need(dve, diffed, m.n)
                        need(dve, staged2, m.n)
                        b = ch.link(dve.tensor_tensor(comp(vlin, 0), rep(av[q][:, :, S:V], 2, 3), yx(y, 1), ALU.mult))
                    if tail:
                        ch.wait(b - 1 if mid else None)
                        dve.tensor_tensor(comp(ha[t.slot % 2], S), comp(hv, 0), rep(ex8[:, :, :], 2, 3), ALU.mult)\
                            .then_inc(ha_made, 1)
                    if mid:
                        a = ch.link(dve.scalar_tensor_tensor(out=lg[:, :, :], in0=av[q][:, :, 0:S], scalar=0.2,
                                                             in1=av[q][:, :, 0:S], op0=ALU.mult, op1=ALU.max))
                        ch.wait(b)
                        b = ch.link(dve.tensor_tensor(vlin[:, :, :], vlin[:, :, :], av[q][:, :, V:192], ALU.add))
                        ch.wait(a)
                        a = ch.link(dve.tensor_tensor(lg[:, :, :], lg[:, :, :], rep(wt("adot"), 1, TG), ALU.mult))
                        dve.wait_ge(gated, m.n + 1)
                        ch.wait(b)
                        dve.tensor_tensor(comp(feat2, S), comp(vlin, 0), rep(gate[:, :, :], 2, 3), ALU.mult)\
                            .then_inc(v2_done, 1)
                        ch.wait(a)
                        need(dve, logit_T, m.n)
                        dve.tensor_reduce(a_e[:, :], lg[:, :, :].rearrange("p t (h c) -> p (t h) c", h=H), AX,
                                          ALU.add).then_inc(logit, 1)
                    if front:
                        dve.wait_ge(big_in[s], g.loads(64))
                        need(dve, agg, 2 * (n - 3))
                        dve.tensor_tensor(eq[s][:, :, :], drow[s][:, :].rearrange("p (t e) -> p t e", t=TG),
                                          rep(idx[s][:, 4:8], 2, P), ALU.is_equal).then_inc(eq_made, 1)
                        for k, r in enumerate((P, P, V)):
                            dve.wait_ge(staged1_T, 3 * n + (k + 1))
                            dve.wait_ge(table_out, 3 * n + (k + 1))
                            if k == 0:
                                need(dve, stage1, 4 * n)
                            dve.tensor_tensor(prods[k][0:r, :], tabs[k][0:r, :], banks[k][0:r, :], ALU.mult)\
                                .then_inc(product, 1)
                    if mid:
                        dve.wait_ge(logit_T, m.n + 1)
                        dve.wait_ge(small_in[m.slot], m.loads(32))
                        dve.tensor_tensor_scan(run_max[:, :], cut[m.slot][:, 0:P], banks[5][0:16, 384:512], -OFF,
                                               ALU.add, ALU.max).then_inc(logit_read, 1)
                        need(dve, staged2_T, 3 * m.n)
                        dve.wait_ge(v2_done, m.n + 1)
                        products_with_y(stg[1], feat2, tmp[3:6], y, v2_dup, m.n + 1, staged2)
                        dve.wait_ge(logit_read, m.n + 1)
                        need(dve, max_T, m.n)
                        dve.tensor_tensor_scan(seg_max[:, ::-1], cut[m.slot][:, P:0:-1], run_max[:, ::-1], -OFF,
                                               ALU.add, ALU.max).then_inc(maxed, 1)
                dve.memset(one[:, :], 1.0).then_inc(one_made, 1)
                chain_steps(dve, NG, step, ch)

            @block.scalar
            def _(act):
                def scaled_by_y0(st, f, y, done):
                    for j in range(TG):
                        last = act.activation(st[:, j, S:S + D], f[:, j, 0:D], ACT.Copy, scale=y[:, j, 0:1])
                    last.then_inc(done, 1)

                def step(g, front, mid, tail):
                    n = g.n
                    if tail:
                        t = g.back(2)
                        q = t.slot % 2
                        if not (isinstance(t.base, int) and t.base == 0 and t.slot < 2):
                            act.wait_ge(out_done[q], t.base * 8 + 16 * (t.slot // 2))
                        act.wait_ge(diffed, t.n + 1)
                        need(act, ha_made, t.n)
                        act.activation(ha[q][:, :, D:D + H], diff[:, :].rearrange("p (t h) -> p t h", t=TG), ACT.Exp)
                        act.activation(ex8[:, :, :].rearrange("p t (h c) -> p (t h) c", h=H), rep(diff[:, :], 2, 8),
                                       ACT.Exp).then_inc(exped, 1)
                        act.activation(orow[q][:, :, D + H:AGG0],
                                       banks[7][:, 328:344].rearrange("p (t h) -> p t h", t=TG), ACT.Copy)\
                            .then_inc(max_out, 1)
                    if front:
                        f = feat[g.slot]
                        act.wait_ge(gathered[g.slot], g.loads(128))
                        act.activation(f[:, :, D:D + 64], f[:, :, S:S + 64], ACT.Copy).then_inc(v_dup, 1)
                        need(act, staged1_T, 3 * n)
                        act.activation(stg[0][:, :, 0:S], f[:, :, 0:S], ACT.Copy)
                        scaled_by_y0(stg[0], f, Y[g.slot], scaled1)
                        for k, r in enumerate((P, P, V)):
                            act.wait_ge(table_mm, 3 * n + (k + 1))
                            need(act, product, 3 * n - 2 + k)
                            act.activation(tabs[k][0:r, :], banks[k][0:r, :], ACT.Copy).then_inc(table_out, 1)
                    if tail:
                        agg_evac(t, 0)
                    if mid:
                        m = g.back(1)
                        act.wait_ge(v2_done, m.n + 1)
                        act.activation(feat2[:, :, D:D + 64], feat2[:, :, S:S + 64], ACT.Copy).then_inc(v2_dup, 1)
                        scaled_by_y0(stg[1], feat2, Y[m.slot], scaled2)
                    if front:
                        q = g.slot % 2
                        need(act, v2_done, n - 1)
                        need(act, logit, n - 1)
                        for j in range(TG):
                            act.wait_ge(stage1, 4 * n + (j + 1))
                            o = banks[3 + j % 2]
                            act.activation(th[q][:, j, :], o[:, 0:V], ACT.Tanh, scale=0.5)
                            act.activation(av[q][:, j, :], o[:, V:288], ACT.Copy).then_inc(stage1_out, 1)
                    if mid:
                        for k, r in enumerate((P, P, V)):
                            act.wait_ge(staged2_T, 3 * m.n + (k + 1))
                            need(act, stage2, 2 * m.n)
                            act.activation(st2[k][0:r, :], banks[k][0:r, :], ACT.Copy).then_inc(st2_out, 1)
                    if tail:
                        agg_evac(t, 1)
                        act.wait_ge(agg_out, 2 * (t.n + 1))
                        act.dma_start(agg_v[bass.ds(t.n, 1)].squeeze(0), orow[t.slot % 2][:, :, :])\
                            .then_inc(out_done[t.slot % 2], 16)
                    if front:
                        act.wait_ge(stage1_out, 4 * (n + 1))
                        need(act, v2_done, n)
                        need(act, staged2, n)
                        need(act, scaled2, n)
                        q = g.slot % 2
                        act.activation(stg[1][:, :, 0:S], th[q][:, :, 0:S], ACT.Identity, bias=one[:, 0:1])
                        act.activation(feat2[:, :, 0:S], th[q][:, :, 0:S], ACT.Identity, bias=one[:, 0:1])
                        act.activation(gate[:, :, :], th[q][:, :, S:V], ACT.Identity, bias=one[:, 0:1])\
                            .then_inc(gated, 1)

                def agg_evac(t, b):
                    q = t.slot % 2
                    act.wait_ge(agg, 2 * t.n + (b + 1))
                    act.activation(orow[q][:, 2 * b:2 * b + 2, 0:D + H],
                                   banks[7][:, 0:2 * (D + H)].rearrange("p (t c) -> p t c", t=2), ACT.Copy)\
                        .then_inc(agg_out, 1)
                act.wait_ge(one_made, 1)
                steps(act, NG, step)
                for i in range(2):
                    act.wait_ge(out_done[i], 16 * (NG // 2))

            @block.tensor
            def _(pe):
                def sums(t, b):
                    q, e = t.slot % 2, t.slot
                    need(pe, agg_out, 2 * t.n + b)
                    for j in (2 * b, 2 * b + 1):
                        mm = pe.matmul(banks[7][:, (j % 2) * (D + H):(j % 2 + 1) * (D + H)], eq[e][:, j, :],
                                       ha[q][:, j, :], start=True, stop=True)
                    mm.then_inc(agg, 1)

                def step(g, front, mid, tail):
                    n = g.n
                    if front:
                        s = g.slot
                        pe.wait_ge(big_in[s], g.loads(64))
                        for k, r in enumerate((P, P, V)):
                            need(pe, st2_out, 3 * (n - 1) + k - 2)
                            pe.matmul(banks[k][0:r, :], rbf_w[:, P * k:P * k + r], xs[s][:, :],
                                      start=True, stop=True).then_inc(table_mm, 1)
                        pe.wait_ge(staged1, n + 1)
                        pe.wait_ge(scaled1, n + 1)
                        for k, r in enumerate((P, P, V)):
                            pe.wait_ge(table_out, 3 * n + (k + 1))
                            for j in range(TG):
                                mm = pe.transpose(banks[k][0:r, P * j:P * j + P], stg[0][:, j, P * k:P * k + r],
                                                  ident[:, :])
                            mm.then_inc(staged1_T, 1)
                    if tail:
                        t = g.back(2)
                        pe.wait_ge(eq_made, t.n + 1)
                        pe.wait_ge(ha_made, t.n + 1)
                        pe.wait_ge(max_out, t.n + 1)
                        sums(t, 0)
                    if mid:
                        m = g.back(1)
                        pe.wait_ge(logit, m.n + 1)
                        need(pe, logit_read, m.n)
                        need(pe, ha_made, m.n)
                        pe.transpose(banks[5][0:16, 384:512], a_e[:, :], ident[:, :]).then_inc(logit_T, 1)
                    if front:
                        pe.wait_ge(product, 3 * n + 3)
                        for j in range(TG):
                            need(pe, stage1_out, 4 * n + j - 1)
                            o = banks[3 + j % 2]
                            e = slice(P * j, P * j + P)
                            pe.matmul(o[:, 0:288], prods[1][:, e], wt("W1b"), start=True, stop=False)
                            pe.matmul(o[:, 0:192], prods[0][:, e], wt("W1a"), start=False, stop=False)
                            pe.matmul(o[:, 192:288], prods[2][0:V, e], wt("W1c"), start=False, stop=True)\
                                .then_inc(stage1, 1)
                    if mid:
                        pe.wait_ge(staged2, m.n + 1)
                        pe.wait_ge(scaled2, m.n + 1)
                        for k, r in enumerate((P, P, V)):
                            if front:
                                pe.wait_ge(product, 3 * n + (k + 1))
                            for j in range(TG):
                                mm = pe.transpose(banks[k][0:r, P * j:P * j + P], stg[1][:, j, P * k:P * k + r],
                                                  ident[:, :])
                            mm.then_inc(staged2_T, 1)
                    if tail:
                        sums(t, 1)
                    if mid:
                        pe.wait_ge(maxed, m.n + 1)
                        need(pe, agg_out, 2 * (m.n - 1) + 2)
                        need(pe, diffed, m.n)
                        need(pe, max_out, m.n)
                        settle(pe)
                        pe.transpose(banks[7][:, 328:344], seg_max[:, :], ident[0:16, 0:16]).then_inc(max_T, 1)
                        pe.wait_ge(st2_out, 3 * m.n + 3)
                        need(pe, ha_made, m.n)
                        for j in range(TG):
                            o = banks[5 + j // 2]
                            c = 192 * (j % 2)
                            e = slice(P * j, P * j + P)
                            pe.matmul(o[:, c:c + 192], st2[1][:, e], wt("W2b"), start=True, stop=False)
                            pe.matmul(o[:, c:c + 96], st2[0][:, e], wt("W2a"), start=False, stop=False)
                            mm = pe.matmul(o[:, c + 96:c + 192], st2[2][0:V, e], wt("W2c"), start=False, stop=True)
                            if j % 2:
                                mm.then_inc(stage2, 1)
                steps(pe, NG, step)


def chain_steps(eng, groups, step, ch):
    for n in range(4):
        before = ch.count
        step(Group(0, n), True, n >= 1, n >= 2)
    full, entry = ch.count - before, ch.count
    with eng.Fori(1, groups // 4, 1) as i:
        ch.count = i * (4 * full) + (entry - 4 * full)
        for u in range(4):
            step(Group(i * 4, u), True, True, True)
    ch.count = entry + (groups - 4) * full
    step(Group(groups, 0), False, True, True)
    step(Group(groups, 1), False, False, True)


def carry_scan(nc, ctx, sem, banks, ident, ins, agg, carry, NT, width, softmax):
    SB = NT // P
    tag = "c0_" if softmax else "c1_"
    R = D + H if softmax else width
    parts = ((0, P), (P, R - P))
    with ExitStack() as ph:
        def sb(name, shape, dt=F32):
            return ph.enter_context(nc.sbuf_tensor(tag + name, shape, dt))
        last = sb("last", [P, SB, width])
        mrep = sb("mrep", [P, SB, R]) if softmax else None
        edges = [sb(f"edge{i}", [P, NT], I32) for i in range(3)]
        go_on = sb("go_on", [P, NT])
        cut = sb("cut", [P, NT])
        val = [sb(f"val{i}", [P, NT]) for i in range(2)]
        mx = [sb(f"mx{i}", [P, NT]) for i in range(2)] if softmax else None
        mtop = [sb(f"mtop{i}", [P, NT]) for i in range(2)] if softmax else None
        keep = sb("keep", [P, NT])
        gain = sb("gain", [P, NT])
        back = sb("back", [P, SB, width])
        loaded, rep_done, turned, turned_out, scanned, back_T, back_out, stored, arg_done, exp_done = (
            sem(tag + n) for n in ("loaded", "rep_done", "turned", "turned_out", "scanned", "back_T", "back_out",
                                   "stored", "arg_done", "exp_done"))
        with nc.Block() as block:
            @block.sync
            def _(sp):
                sp.dma_start(last[:, :, :], agg.rearrange("(b t e) c -> e t b c", t=P, e=P)[P - 1])\
                    .then_inc(loaded, 16)
                for i, n in enumerate(("first", "last", "before")):
                    sp.dma_start(edges[i][:, :], ins[n].partition_broadcast(P)).then_inc(loaded, 16)
                hold(sp, back_out, SB)
                sp.dma_start(carry[1:NT + 1].rearrange("(b t) c -> t b c", t=P), back[:, :, :]).then_inc(stored, 16)
                hold(sp, stored, 16)

            @block.tensor
            def _(pe):
                pe.wait_ge(loaded, 64)
                if softmax:
                    pe.wait_ge(rep_done, 3)
                k = 0
                for b in range(SB):
                    for i, (c, r) in enumerate(parts):
                        for src in ((last, mrep) if softmax else (last,)):
                            if k >= 4:
                                pe.wait_ge(turned_out, k - 3)
                            pe.transpose(banks[k % 4][0:r, 0:P], src[:, b, c:c + r], ident[:, :]).then_inc(turned, 1)
                            k += 1
                pe.wait_ge(scanned, 2)
                k = 0
                for b in range(SB):
                    if k >= 4:
                        pe.wait_ge(back_out, b - 3)
                    o = banks[4 + b % 4]
                    e = slice(b * P, b * P + P)
                    for i, (c, r) in enumerate(parts):
                        mm = pe.transpose(o[:, c:c + r], val[i][0:r, e], ident[0:r, 0:r])
                    if softmax:
                        mm = pe.transpose(o[:, 256:256 + R - P], mtop[1][0:R - P, e], ident[0:R - P, 0:R - P])
                    mm.then_inc(back_T, 1)
                    k += 1

            @block.scalar
            def _(act):
                k = 0
                for b in range(SB):
                    for i, (c, r) in enumerate(parts):
                        for dst in ((val, mx) if softmax else (val,)):
                            act.wait_ge(turned, k + 1)
                            act.activation(dst[i][0:r, b * P:b * P + P], banks[k % 4][0:r, 0:P], ACT.Copy)\
                                .then_inc(turned_out, 1)
                            k += 1
                if softmax:
                    for i, (c, r) in enumerate(parts):
                        act.wait_ge(arg_done, 2 * i + 2)
                        act.activation(keep[0:r, :], keep[0:r, :], ACT.Exp)
                        act.activation(gain[0:r, :], gain[0:r, :], ACT.Exp).then_inc(exp_done, 1)
                for b in range(SB):
                    act.wait_ge(back_T, b + 1)
                    o = banks[4 + b % 4]
                    if softmax:
                        act.activation(back[:, b, D + H:], o[:, 256 + R - P - H:256 + R - P], ACT.Copy)
                    act.activation(back[:, b, 0:R], o[:, 0:R], ACT.Copy).then_inc(back_out, 1)

            @block.vector
            def _(dve):
                ch = Chain(dve, sem(tag + "chain"))
                dve.wait_ge(loaded, 64)
                if softmax:
                    m = last[:, :, D + H:]
                    dve.tensor_copy(mrep[:, :, 0:S].rearrange("p b (h c) -> p b h c", h=H), rep(m, 3, 16))\
                        .then_inc(rep_done, 1)
                    for x in range(3):
                        ins_ = dve.tensor_copy(
                            mrep[:, :, S + C * x:S + C * x + C].rearrange("p b (h c) -> p b h c", h=H), rep(m, 3, 8))
                    ins_.then_inc(rep_done, 1)
                    dve.tensor_copy(mrep[:, :, D:R], m).then_inc(rep_done, 1)
                ch.link(dve.tensor_tensor(go_on[:, :], edges[0][:, :], edges[1][:, :], ALU.is_equal))
                ch.link(dve.tensor_tensor(cut[:, :], edges[0][:, :], edges[2][:, :], ALU.is_equal))
                ch.wait()
                ch.link(dve.tensor_tensor(go_on[:, :], go_on[:, :], cut[:, :], ALU.mult))
                ch.wait()
                dve.wait_ge(turned_out, SB * len(parts) * (2 if softmax else 1))
                if not softmax:
                    for i, (c, r) in enumerate(parts):
                        dve.tensor_tensor_scan(val[i][0:r, :], go_on[0:r, :], val[i][0:r, :], 0.0, ALU.mult, ALU.add)\
                            .then_inc(scanned, 1)
                    return
                ch.link(dve.tensor_scalar(cut[:, :], go_on[:, :], -1.0, OFF, ALU.add, ALU.mult))
                ch.wait()
                for i, (c, r) in enumerate(parts):
                    if i >= 1:
                        dve.wait_ge(scanned, i)
                    top = mtop[i]
                    ch.link(dve.tensor_tensor_scan(top[0:r, :], cut[0:r, :], mx[i][0:r, :], -OFF, ALU.add, ALU.max))
                    ch.wait()
                    ch.link(dve.memset(keep[0:r, 0:1], 0.0))
                    ch.link(dve.tensor_tensor(keep[0:r, 1:NT], top[0:r, 0:NT - 1], top[0:r, 1:NT], ALU.subtract))
                    ch.wait()
                    dve.tensor_scalar(keep[0:r, :], keep[0:r, :], 0.0, None, ALU.min).then_inc(arg_done, 1)
                    dve.tensor_tensor(gain[0:r, :], mx[i][0:r, :], top[0:r, :], ALU.subtract).then_inc(arg_done, 1)
                    dve.wait_ge(exp_done, i + 1)
                    ch.link(dve.tensor_tensor(keep[0:r, :], keep[0:r, :], go_on[0:r, :], ALU.mult))
                    ch.link(dve.tensor_tensor(gain[0:r, :], gain[0:r, :], val[i][0:r, :], ALU.mult))
                    ch.wait()
                    dve.tensor_tensor_scan(val[i][0:r, :], keep[0:r, :], gain[0:r, :], 0.0, ALU.mult, ALU.add)\
                        .then_inc(scanned, 1)


def layer_norm(dve, ch, X, scr, stat, varred, rooted):
    ch.link(dve.tensor_reduce(stat[:, :], X[:, :, :], AX, ALU.add)); ch.wait()
    ch.link(dve.tensor_scalar(stat[:, :], stat[:, :], 1.0 / D, None, ALU.mult)); ch.wait()
    ch.link(dve.tensor_tensor(X[:, :, :], X[:, :, :], rep(stat[:, :], 2, D), ALU.subtract)); ch.wait()
    ch.link(dve.tensor_tensor(scr[:, :, :], X[:, :, :], X[:, :, :], ALU.mult)); ch.wait()
    ch.link(dve.tensor_reduce(stat[:, :], scr[:, :, :], AX, ALU.add)); ch.wait()
    dve.tensor_scalar(stat[:, :], stat[:, :], 1.0 / D, 1e-5, ALU.mult, ALU.add).then_inc(varred, 1)
    dve.wait_ge(rooted, 1)
    ch.link(dve.reciprocal(stat[:, :], stat[:, :])); ch.wait()


def gather_batches(pool, NB, row_idx, carry_idx, idx_s, agg, carry, ga, gc, copied, used, gathered):
    def batch(b):
        if not (isinstance(b, int) and b == 0):
            pool.wait_ge(gathered, b * (32 * NODE_BATCH))
            pool.wait_ge(used, b)
        cols = bass.ds(b * NODE_BATCH, NODE_BATCH)
        pool.tensor_copy(idx_s[0][:, :], row_idx[:, cols]).then_inc(copied, 1)
        pool.tensor_copy(idx_s[1][:, :], carry_idx[:, cols]).then_inc(copied, 1)
        pool.wait_ge(copied, b * 2 + 2)
        settle(pool)
        for j in range(NODE_BATCH):
            for i, (table, dst) in enumerate(((agg, ga), (carry, gc))):
                pool.indirect_dma_start(out=dst[:, j, :], out_offset=None, in_=table,
                                        in_offset=bass.IndirectOffsetOnAxis(ap=idx_s[i][:, j:j + 1], axis=0))\
                    .then_inc(gathered, 16)
    run_batches(pool, NB, batch)


def run_batches(eng, NB, batch):
    batch(0)
    if NB > 1:
        with eng.Fori(1, NB, 1) as b:
            batch(b)


def node_step_0(nc, ctx, sem, banks, wt, ident, ins, agg0, carry0, conv_table, X1, row_idx, carry_idx,
                has_row, has_carry, node_a, stat, stat2, NK):
    NB = NK // NODE_BATCH
    U = NODE_BATCH
    R = D + H
    with ExitStack() as ph:
        def sb(name, shape, dt=F32):
            return ph.enter_context(nc.sbuf_tensor("n0_" + name, shape, dt))
        idx_s = [sb(f"idx{i}", [P, U], I32) for i in range(2)]
        ga, gc = sb("ga", [P, U, AGG0]), sb("gc", [P, U, AGG0])
        ea, ec, mt = sb("ea", [P, U, H]), sb("ec", [P, U, H]), sb("mt", [P, U, H])
        aggn = sb("aggn", [P, U, D])
        turned = [sb(f"turned{i}", [P, 2 * P]) for i in range(2)]
        xk = [sb(f"xk{i}", [P, D]) for i in range(2)]
        tab = [sb(f"tab{i}", [P, D]) for i in range(2)]
        scr = sb("scr", [P, NK, D])
        (loaded, copied, gathered, exp_arg, exped, normed, T, T_out, proj, added, varred, rooted, ready,
         xcopied, T2, T2_out, proj2, tabbed) = (sem("n0_" + n) for n in (
             "loaded", "copied", "gathered", "exp_arg", "exped", "normed", "T", "T_out", "proj", "added",
             "varred", "rooted", "ready", "xcopied", "T2", "T2_out", "proj2", "tabbed"))
        tab_out = [sem(f"n0_tab_out{i}") for i in range(2)]
        conv_v = conv_table.rearrange("(p k) d -> p k d", k=NK)

        def pairs(eng, body):
            for k in range(2):
                body(k, k)
            with eng.Fori(1, NK // 2, 1) as i:
                for u in range(2):
                    body(i * 2 + u, u)

        with nc.Block() as block:
            @block.sync
            def _(sp):
                sp.dma_start(X1[:, :, :], ins["x"].rearrange("(p k) d -> p k d", k=NK)).then_inc(loaded, 16)

                def store(k, q):
                    hold(sp, tabbed, k + 1)
                    sp.dma_start(conv_v[:, bass.ds(k, 1), :].squeeze(1), tab[q][:, :]).then_inc(tab_out[q], 16)
                pairs(sp, store)
                for q in range(2):
                    hold(sp, tab_out[q], 16 * (NK // 2))

            @block.gpsimd
            def _(pool):
                gather_batches(pool, NB, row_idx, carry_idx, idx_s, agg0, carry0, ga, gc, copied, normed, gathered)

            @block.vector
            def _(dve):
                own, den = sem("n0_chain"), sem("n0_den")
                dve.wait_ge(loaded, 16)
                LINKS = 7 + 4 * U + 3 + 2 * U

                def batch(b):
                    ch = Chain(dve, own)
                    ch.count = b * LINKS
                    cols = bass.ds(b * U, U)
                    dve.wait_ge(gathered, b * (32 * U) + 32 * U)
                    fa, fc = has_row[:, cols], has_carry[:, cols]
                    ch.link(dve.tensor_scalar(ea[:, :, 0], fa, -1.0, OFF, ALU.add, ALU.mult))
                    ch.link(dve.tensor_scalar(ec[:, :, 0], fc, -1.0, OFF, ALU.add, ALU.mult)); ch.wait()
                    ch.link(dve.tensor_tensor(ga[:, :, R:], ga[:, :, R:], rep(ea[:, :, 0], 2, H), ALU.add))
                    ch.link(dve.tensor_tensor(gc[:, :, R:], gc[:, :, R:], rep(ec[:, :, 0], 2, H), ALU.add)); ch.wait()
                    ch.link(dve.tensor_tensor(mt[:, :, :], ga[:, :, R:], gc[:, :, R:], ALU.max)); ch.wait()
                    dve.tensor_tensor(ea[:, :, :], ga[:, :, R:], mt[:, :, :], ALU.subtract).then_inc(exp_arg, 1)
                    dve.tensor_tensor(ec[:, :, :], gc[:, :, R:], mt[:, :, :], ALU.subtract).then_inc(exp_arg, 1)
                    dve.wait_ge(exped, b + 1)
                    ch.link(dve.tensor_tensor(ea[:, :, :], ea[:, :, :], rep(fa, 2, H), ALU.mult))
                    ch.link(dve.tensor_tensor(ec[:, :, :], ec[:, :, :], rep(fc, 2, H), ALU.mult)); ch.wait()

                    def by_head(buf, t, f):
                        ch.link(dve.tensor_tensor(buf[:, t, 0:S].rearrange("p (h c) -> p h c", h=H),
                                                  buf[:, t, 0:S].rearrange("p (h c) -> p h c", h=H),
                                                  rep(f[:, t, :], 2, 16), ALU.mult))
                        ch.link(dve.tensor_tensor(buf[:, t, S:D].rearrange("p (x h c) -> p x h c", h=H, c=8),
                                                  buf[:, t, S:D].rearrange("p (x h c) -> p x h c", h=H, c=8),
                                                  rep(rep(f[:, t, :], 2, 8), 1, 3), ALU.mult))
                    for t in range(U):
                        by_head(ga, t, ea)
                        by_head(gc, t, ec)
                    ch.link(dve.tensor_tensor(ga[:, :, D:R], ga[:, :, D:R], ea[:, :, :], ALU.mult))
                    ch.link(dve.tensor_tensor(gc[:, :, D:R], gc[:, :, D:R], ec[:, :, :], ALU.mult)); ch.wait()
                    ch.link(dve.tensor_tensor(ga[:, :, 0:R], ga[:, :, 0:R], gc[:, :, 0:R], ALU.add)); ch.wait()
                    dve.tensor_scalar(mt[:, :, :], ga[:, :, D:R], 1e-16, None, ALU.add).then_inc(den, 1)
                    dve.wait_ge(den, b * 2 + 1)
                    dve.reciprocal(mt[:, :, :], mt[:, :, :]).then_inc(den, 1)
                    dve.wait_ge(den, b * 2 + 2)
                    for t in range(U):
                        by_head(ga, t, mt)
                    ch.wait()
                    if not (isinstance(b, int) and b == 0):
                        dve.wait_ge(T, b * U)
                    dve.tensor_copy(aggn[:, :, :], ga[:, :, 0:D]).then_inc(normed, 1)
                    dve.wait_ge(normed, b + 1)
                    for t in range(U):
                        xt = X1[:, bass.ds(b * U + t, 1), :].squeeze(1)
                        dve.wait_ge(proj, b * U + (t + 1))
                        dve.scalar_tensor_tensor(out=xt, in0=xt, scalar=2.0, in1=banks[4 + t % 2][:, 0:D],
                                                 op0=ALU.mult, op1=ALU.add).then_inc(added, 1)
                run_batches(dve, NB, batch)
                dve.wait_ge(added, NK)
                ch = Chain(dve, sem("n0_norm_chain"))
                layer_norm(dve, ch, X1, scr, stat, varred, rooted)
                dve.tensor_tensor(X1[:, :, :], X1[:, :, :], rep(stat[:, :], 2, D), ALU.mult).then_inc(ready, 1)

                def body(k, q):
                    dve.wait_ge(proj2, k + 1)
                    if not (isinstance(k, int) and k < 2):
                        dve.wait_ge(tab_out[q], k * 8 - 8 * q)
                    a = node_a[:, bass.ds(k, 1)]
                    xt = X1[:, bass.ds(k, 1), :].squeeze(1)
                    o = banks[2 * q + 1]
                    dve.tensor_scalar(tab[q][:, :], o[:, 0:D], a, None, ALU.mult)
                    dve.scalar_tensor_tensor(out=xt, in0=o[:, D:2 * D], scalar=a, in1=xt, op0=ALU.mult,
                                             op1=ALU.add).then_inc(tabbed, 1)
                pairs(dve, body)

            @block.scalar
            def _(act):
                def batch(b):
                    act.wait_ge(exp_arg, b * 2 + 2)
                    act.activation(ea[:, :, :], ea[:, :, :], ACT.Exp)
                    act.activation(ec[:, :, :], ec[:, :, :], ACT.Exp).then_inc(exped, 1)
                    for t in range(U):
                        act.wait_ge(T, b * U + (t + 1))
                        if not (isinstance(b, int) and b * U + t < 2):
                            act.wait_ge(proj, b * U + (t - 1))
                        q = t % 2
                        act.activation(turned[q][:, 0:P], banks[t % 2][:, 0:P], ACT.Copy)
                        act.activation(turned[q][0:C, P:], banks[t % 2][0:C, P:2 * P], ACT.Copy).then_inc(T_out, 1)
                run_batches(act, NB, batch)
                act.wait_ge(varred, 1)
                act.activation(stat[:, :], stat[:, :], ACT.Sqrt).then_inc(rooted, 1)
                act.wait_ge(ready, 1)

                def body(k, q):
                    need(act, T2, k - 1)
                    act.activation(xk[q][:, :], X1[:, bass.ds(k, 1), :].squeeze(1), ACT.Copy).then_inc(xcopied, 1)
                    act.wait_ge(T2, k + 1)
                    need(act, proj2, k - 1)
                    act.activation(turned[q][:, 0:P], banks[2 * q][:, 0:P], ACT.Copy)
                    act.activation(turned[q][0:C, P:], banks[2 * q][0:C, P:2 * P], ACT.Copy).then_inc(T2_out, 1)
                pairs(act, body)

            @block.tensor
            def _(pe):
                def batch(b):
                    pe.wait_ge(normed, b + 1)

                    def turn(t):
                        if not (isinstance(b, int) and b * U + t < 2):
                            pe.wait_ge(T_out, b * U + (t - 1))
                        pe.transpose(banks[t % 2][:, 0:P], aggn[:, t, 0:P], ident[:, :])
                        pe.transpose(banks[t % 2][0:C, P:2 * P], aggn[:, t, P:D], ident[:, :]).then_inc(T, 1)
                    turn(0)
                    for t in range(U):
                        if t + 1 < U:
                            turn(t + 1)
                        pe.wait_ge(T_out, b * U + (t + 1))
                        if not (isinstance(b, int) and b * U + t < 2):
                            pe.wait_ge(added, b * U + (t - 1))
                        q = t % 2
                        pe.matmul(banks[4 + q][:, 0:D], turned[q][:, 0:P], wt("Wpa"), start=True, stop=False)
                        pe.matmul(banks[4 + q][:, 0:D], turned[q][0:C, P:], wt("Wpb"), start=False, stop=True)\
                            .then_inc(proj, 1)
                run_batches(pe, NB, batch)

                def body(k, q):
                    pe.wait_ge(xcopied, k + 1)
                    need(pe, T2_out, k - 1)
                    pe.transpose(banks[2 * q][:, 0:P], xk[q][:, 0:P], ident[:, :])
                    pe.transpose(banks[2 * q][0:C, P:2 * P], xk[q][:, P:D], ident[:, :]).then_inc(T2, 1)
                    pe.wait_ge(T2_out, k + 1)
                    need(pe, tabbed, k - 1)
                    pe.matmul(banks[2 * q + 1][:, 0:2 * D], turned[q][:, 0:P], wt("W3a"), start=True, stop=False)
                    pe.matmul(banks[2 * q + 1][:, 0:2 * D], turned[q][0:C, P:], wt("W3b"), start=False, stop=True)\
                        .then_inc(proj2, 1)
                pairs(pe, body)


def edge_loop_1(nc, ctx, sem, banks, wt, rbf_w, ins, rbf_parts, conv_table, agg1, NG):
    with ExitStack() as ph:
        def sb(name, shape, dt=F32):
            return ph.enter_context(nc.sbuf_tensor("m_" + name, shape, dt))
        pack = [sb(f"pack{i}", [P, 32], I32) for i in range(4)]
        idx = [p[:, 0:8] for p in pack]
        Y = [p[:, 8:32].bitcast(F32).rearrange("p (t c) -> p t c", t=TG) for p in pack]
        xs = [sb(f"xs{i}", [P, 512], BF16) for i in range(4)]
        drow = [sb(f"drow{i}", [P, 512], I32) for i in range(4)]
        gs = [sb(f"gs{i}", [P, TG, D]) for i in range(4)]
        tanh = sb("tanh", [S, 512])
        hid = [sb(f"hid{i}", [S, 512]) for i in range(2)]
        u = sb("u", [P, TG, P])
        tt = sb("tt", [P, TG, V])
        dot = sb("dot", [P, TG, C])
        w2y = sb("w2y", [P, TG, C])
        mid_ = [sb(f"mid{i}", [P, TG, 3 * P]) for i in range(2)]
        eq = [sb(f"eq{i}", [P, TG, P]) for i in range(4)]
        sums = [sb(f"sums{k}", [P, 512]) for k in range(3)]
        orow = [sb(f"orow{i}", [P, TG, AGG1]) for i in range(2)]
        ones = sb("ones", [P, 1])
        small_in = [sem(f"l1_small_in{i}") for i in range(4)]
        big_in = [sem(f"l1_big_in{i}") for i in range(4)]
        gathered = [sem(f"l1_gathered{i}") for i in range(4)]
        out_done = [sem(f"l1_out_done{i}") for i in range(2)]
        (hid_mm, tanhed, hid_made, weights, mids, eq_made, summed, sums_out, mapped, row_out, ones_made) = (
            sem("l1_" + n) for n in ("hid_mm", "tanhed", "hid_made", "weights", "mids", "eq_made", "summed",
                                     "sums_out", "mapped", "row_out", "ones_made"))
        agg_v = agg1.rearrange("(g j p) c -> g p j c", j=TG, p=P)
        xs_v = rbf_parts.rearrange("s c (g n) -> s g c n", n=512)
        drow_v = ins["dst_flat"].rearrange("(g n) -> g n", n=512)

        with nc.Block() as block:
            @block.sync
            def _(sp):
                def step(g, front, mid, tail):
                    if front:
                        s, n = g.slot, g.n
                        hold(sp, hid_mm, n - 3)
                        hold(sp, mids, n - 3)
                        hold(sp, eq_made, n - 3)
                        if not (isinstance(g.base, int) and g.base == 0):
                            hold(sp, gathered[s], g.base * 16)
                        at = bass.ds(n, 1)
                        sp.dma_start(pack[s][:, :], ins["edge_pack"][at].squeeze(0)).then_inc(small_in[s], 16)
                        c0 = 0
                        for part, copies in ((0, 3), (1, 3), (2, 2)):
                            sp.dma_start(xs[s][c0:c0 + 16 * copies, :], rep(xs_v[part, at], 0, copies).squeeze(1))\
                                .then_inc(big_in[s], 16)
                            c0 += 16 * copies
                        sp.dma_start(drow[s][:, :], drow_v[at].broadcast_to([P, 512])).then_inc(big_in[s], 16)
                steps(sp, NG, step)

            @block.gpsimd
            def _(pool):
                def step(g, front, mid, tail):
                    if not front:
                        return
                    s = g.slot
                    need(pool, mids, g.n - 3)
                    pool.wait_ge(small_in[s], g.loads(16))
                    settle(pool)
                    for j in range(TG):
                        pool.indirect_dma_start(
                            out=gs[s][:, j, :], out_offset=None, in_=conv_table,
                            in_offset=bass.IndirectOffsetOnAxis(ap=idx[s][:, j:j + 1], axis=0)
                        ).then_inc(gathered[s], 16)
                steps(pool, NG, step)

            @block.vector
            def _(dve):
                ch = Chain(dve, sem("l1_vector_chain"))
                dve.memset(ones[:, :], 1.0).then_inc(ones_made, 1)

                def x3(ap, c0, w):
                    return ap[:, :, c0:c0 + 3 * w].rearrange("p t (x c) -> p t x c", c=w)

                def step(g, front, mid, tail):
                    if mid:
                        m = g.back(1)
                        s, q, y, e = m.slot, m.slot % 2, Y[m.slot], gs[m.slot]
                        dve.wait_ge(gathered[s], m.loads(64))
                        need(dve, mids, m.n)
                        a = ch.link(dve.tensor_tensor(x3(tt, 0, C), x3(e, S, C), rep(y[:, :, 1:4], 3, C), ALU.mult))
                        need(dve, summed, 3 * (m.n - 1))
                        ch.wait(a)
                        a = ch.link(dve.tensor_tensor(dot[:, :, :], tt[:, :, 0:C], tt[:, :, C:2 * C], ALU.add))
                        for b in range(2):
                            dve.wait_ge(weights, 2 * m.n + (b + 1))
                            o = banks[1 + b][:, 0:384].rearrange("p (t c) -> p t c", t=2)
                            ts2 = slice(2 * b, 2 * b + 2)
                            bu = ch.link(dve.tensor_tensor(
                                u[:, ts2, :].rearrange("p t (r c) -> p t r c", c=S),
                                o[:, :, 0:P].rearrange("p t (r c) -> p t r c", c=S), rep(e[:, ts2, 0:S], 2, 2), ALU.mult))
                            bw = ch.link(dve.tensor_tensor(w2y[:, ts2, :], o[:, :, 128:160], rep(y[:, ts2, 0], 2, C),
                                                           ALU.mult))
                            if b == 0:
                                ch.wait(a)
                                a = ch.link(dve.tensor_tensor(dot[:, :, :], dot[:, :, :], tt[:, :, 2 * C:V], ALU.add))
                                ch.wait(a)
                            ch.link(dve.tensor_tensor(mid_[q][:, ts2, S:V], o[:, :, 160:192], dot[:, ts2, :], ALU.mult))
                        ch.wait(bw)
                        ch.link(dve.tensor_tensor(mid_[q][:, :, 0:S], u[:, :, 0:S], rep(y[:, :, 0], 2, S), ALU.mult))
                        ch.link(dve.tensor_tensor(x3(mid_[q], V, C), x3(e, S, C), rep(w2y[:, :, :], 2, 3), ALU.mult))
                        dve.tensor_tensor(x3(mid_[q], 2 * V, S), rep(u[:, :, S:P], 2, 3), rep(y[:, :, 1:4], 3, S),
                                          ALU.mult).then_inc(mids, 1)
                        dve.wait_ge(big_in[s], m.loads(64))
                        need(dve, mapped, 2 * (m.n - 1))
                        dve.tensor_tensor(eq[q][:, :, :], drow[s][:, :].rearrange("p (t e) -> p t e", t=TG),
                                          rep(idx[s][:, 4:8], 2, P), ALU.is_equal).then_inc(eq_made, 1)
                    if front:
                        n = g.n
                        dve.wait_ge(tanhed, n + 1)
                        need(dve, weights, 2 * (n - 1))
                        dve.scalar_tensor_tensor(out=hid[g.slot % 2][:, :], in0=tanh[:, :], scalar=1.0,
                                                 in1=banks[0][0:S, :], op0=ALU.add, op1=ALU.mult)\
                            .then_inc(hid_made, 1)
                chain_steps(dve, NG, step, ch)

            @block.scalar
            def _(act):
                def step(g, front, mid, tail):
                    n = g.n
                    if front:
                        act.wait_ge(hid_mm, n + 1)
                        need(act, hid_made, n)
                        act.activation(tanh[:, :], banks[0][0:S, :], ACT.Tanh, scale=0.125).then_inc(tanhed, 1)
                    if tail:
                        t = g.back(2)
                        q = t.slot % 2
                        for k in range(3):
                            act.wait_ge(summed, 3 * t.n + (k + 1))
                            need(act, mapped, 2 * t.n)
                            act.activation(sums[k][:, :], banks[3 + k][:, :], ACT.Copy).then_inc(sums_out, 1)
                        if not (isinstance(t.base, int) and t.base == 0 and t.slot < 2):
                            act.wait_ge(out_done[q], t.base * 8 + 16 * (t.slot // 2))
                        for b in range(2):
                            act.wait_ge(mapped, 2 * t.n + (b + 1))
                            act.activation(orow[q][:, 2 * b:2 * b + 2, :],
                                           banks[6 + b][:, 0:2 * AGG1].rearrange("p (t c) -> p t c", t=2), ACT.Copy)\
                                .then_inc(row_out, 1)
                        act.wait_ge(row_out, 2 * (t.n + 1))
                        act.dma_start(agg_v[bass.ds(t.n, 1)].squeeze(0), orow[q][:, :, :])\
                            .then_inc(out_done[q], 16)
                steps(act, NG, step)
                for i in range(2):
                    act.wait_ge(out_done[i], 16 * (NG // 2))

            @block.tensor
            def _(pe):
                pe.wait_ge(ones_made, 1)

                def step(g, front, mid, tail):
                    n = g.n
                    if front:
                        pe.wait_ge(big_in[g.slot], g.loads(64))
                        need(pe, hid_made, n)
                        pe.matmul(banks[0][0:S, :], rbf_w[:, 352:416], xs[g.slot][:, :], start=True, stop=True)\
                            .then_inc(hid_mm, 1)
                    if tail:
                        t = g.back(2)
                        q = t.slot % 2
                        pe.wait_ge(mids, t.n + 1)
                        pe.wait_ge(eq_made, t.n + 1)
                        for k in range(3):
                            need(pe, sums_out, 3 * t.n - 2 + k)
                            for j in range(TG):
                                mm = pe.matmul(banks[3 + k][:, P * j:P * j + P], mid_[q][:, j, P * k:P * k + P],
                                               eq[q][:, j, :], start=True, stop=True)
                            mm.then_inc(summed, 1)
                    if mid:
                        m = g.back(1)
                        pe.wait_ge(hid_made, m.n + 1)
                        need(pe, mids, m.n)
                        for j in range(TG):
                            c = 192 * (j % 2)
                            mm = pe.matmul(banks[1 + j // 2][:, c:c + 192], hid[m.slot % 2][:, P * j:P * j + P],
                                           wt("Wfc2"), start=True, stop=True)
                            if j % 2:
                                mm.then_inc(weights, 1)
                    if tail:
                        pe.wait_ge(sums_out, 3 * t.n + 3)
                        for j in range(TG):
                            if j % 2 == 0:
                                need(pe, row_out, 2 * t.n - 1 + j // 2)
                            c, e = AGG1 * (j % 2), slice(P * j, P * j + P)
                            o = banks[6 + j // 2]
                            pe.matmul(o[:, c + 161:c + 162], eq[q][:, j, :], ones[:, :], start=True, stop=True)
                            pe.matmul(o[:, c:c + 161], sums[0][:, e], wt("W4a"), start=True, stop=False)
                            pe.matmul(o[:, c + 65:c + 161], sums[1][:, e], wt("W4b"), start=False, stop=False)
                            mm = pe.matmul(o[:, c + 97:c + 161], sums[2][:, e], wt("W4c"), start=False, stop=True)
                            if j % 2:
                                mm.then_inc(mapped, 1)
                steps(pe, NG, step)


def node_step_1(nc, ctx, sem, banks, agg1, carry1, out, X1, row_idx, carry_idx, has_row, has_carry, node_a,
                stat, NK):
    NB, U = NK // NODE_BATCH, NODE_BATCH
    with ExitStack() as ph:
        def sb(name, shape, dt=F32):
            return ph.enter_context(nc.sbuf_tensor("n1_" + name, shape, dt))
        idx_s = [sb(f"idx{i}", [P, U], I32) for i in range(2)]
        ga, gc = sb("ga", [P, U, AGG1]), sb("gc", [P, U, AGG1])
        cnt = sb("cnt", [P, U])
        scr = sb("scr", [P, NK, D])
        copied, used, gathered, varred, rooted, done, stored = (
            sem("n1_" + n) for n in ("copied", "used", "gathered", "varred", "rooted", "done", "stored"))
        with nc.Block() as block:
            @block.sync
            def _(sp):
                hold(sp, done, 1)
                sp.dma_start(out.rearrange("(p k) d -> p k d", k=NK), X1[:, :, :]).then_inc(stored, 16)
                hold(sp, stored, 16)

            @block.gpsimd
            def _(pool):
                gather_batches(pool, NB, row_idx, carry_idx, idx_s, agg1, carry1, ga, gc, copied, used, gathered)

            @block.scalar
            def _(act):
                act.wait_ge(varred, 1)
                act.activation(stat[:, :], stat[:, :], ACT.Sqrt).then_inc(rooted, 1)

            @block.vector
            def _(dve):
                own = sem("n1_chain")
                LINKS = 10

                def batch(b):
                    ch = Chain(dve, own)
                    ch.count = b * LINKS
                    cols = bass.ds(b * U, U)
                    dve.wait_ge(gathered, b * (32 * U) + 32 * U)
                    ch.link(dve.tensor_tensor(ga[:, :, :], ga[:, :, :], rep(has_row[:, cols], 2, AGG1), ALU.mult))
                    ch.link(dve.tensor_tensor(gc[:, :, :], gc[:, :, :], rep(has_carry[:, cols], 2, AGG1), ALU.mult))
                    ch.wait()
                    ch.link(dve.tensor_tensor(ga[:, :, :], ga[:, :, :], gc[:, :, :], ALU.add)); ch.wait()
                    ch.link(dve.tensor_scalar(cnt[:, :], ga[:, :, 161], 1.0, None, ALU.max)); ch.wait()
                    ch.link(dve.reciprocal(cnt[:, :], cnt[:, :])); ch.wait()
                    ch.link(dve.tensor_tensor(cnt[:, :], cnt[:, :], node_a[:, cols], ALU.mult)); ch.wait()
                    ch.link(dve.tensor_tensor(cnt[:, :], cnt[:, :], cnt[:, :], ALU.mult)); ch.wait()
                    ch.link(dve.tensor_tensor(cnt[:, :], cnt[:, :], ga[:, :, 0], ALU.mult)); ch.wait()
                    ch.link(dve.tensor_tensor(ga[:, :, 1:161], ga[:, :, 1:161], rep(cnt[:, :], 2, D), ALU.mult))
                    ch.wait()
                    xs, xv = X1[:, cols, 0:S], X1[:, cols, S:D].rearrange("p k (c x) -> p k x c", x=3)
                    ch.link(dve.tensor_tensor(xs, xs, ga[:, :, 1:65], ALU.add))
                    ch.wait()
                    dve.tensor_tensor(xv, xv, ga[:, :, 65:161].rearrange("p k (x c) -> p k x c", x=3),
                                      ALU.add).then_inc(used, 1)
                run_batches(dve, NB, batch)
                dve.wait_ge(used, NB)
                ch = Chain(dve, sem("n1_norm_chain"))
                layer_norm(dve, ch, X1, scr, stat, varred, rooted)
                dve.tensor_tensor(X1[:, :, :], X1[:, :, :], rep(stat[:, :], 2, D), ALU.mult).then_inc(done, 1)


def kernel(**inputs):
    import numpy as np
    import concourse.bacc as bacc
    from concourse.bass_utils import run_bass_kernel_spmd

    g = {k: np.ascontiguousarray(v) for k, v in inputs.items()}
    f32 = np.float32
    N, E = g["x"].shape[0], g["src"].shape[0]
    SB = -(-E // (P * P))
    NT = SB * P
    EP, NG = NT * P, NT // TG
    NK = 2 * NODE_BATCH * -(-(N + 1) // (2 * NODE_BATCH * P))

    def padded(a, n, fill=0):
        out = np.full((n,) + a.shape[1:], fill, a.dtype)
        out[:a.shape[0]] = a
        return out

    src, dst = padded(g["src"], EP), padded(g["dst"], EP, N)

    def columns(a):
        return a.reshape(NG, TG, P, -1).transpose(0, 2, 1, 3)
    y = padded(g["edge_attr_4"], EP)
    before = np.concatenate([np.full(1, -1, dst.dtype), dst[:-1]])
    arrays = {
        "x": padded(g["x"], NK * P),
        "edge_pack": np.concatenate([columns(src)[..., 0], columns(dst)[..., 0], np.ascontiguousarray(
            columns(y[:, [0, 1, 2, 3, 1, 2]]).reshape(NG, P, TG * 6)).view(src.dtype)], axis=2),
        "rbf_t": padded(g["edge_attr_16"], EP).T,
        "dst_flat": dst,
        "dst_rows": np.concatenate([before.reshape(NT, P)[:, :1], dst.reshape(NT, P)], axis=1),
        "first": dst.reshape(NT, P)[:, 0], "last": dst.reshape(NT, P)[:, -1],
        "before": before.reshape(NT, P)[:, 0], "sup": dst.reshape(SB, P * P)[:, -1],
        "node_a": padded(g["node_vec1"], NK * P).reshape(P, NK),
    }

    L0 = {k[7:]: v for k, v in g.items() if k.startswith("L0_gnn_")}
    L1 = {k[7:]: v for k, v in g.items() if k.startswith("L1_gnn_")}
    c3 = 3 * np.arange(C)

    def blocks(w):
        o = np.zeros((V, V), f32)
        for x in range(3):
            o[C * x:C * x + C, C * x:C * x + C] = w
        return o

    def node_rows(w, x_major_cols=True):
        o = np.zeros((V, V), f32)
        for x in range(3):
            o[np.ix_(c3 + x, C * x + np.arange(C) if x_major_cols else c3 + x)] = w
        return o
    wr = L0["W_rbf"]
    ss, sv, vs, vv0, vv1 = wr[:, :64], wr[:, 64:128], wr[:, 128:160], wr[:, 160:192], wr[:, 192:224]
    arrays["rbf_w"] = np.concatenate([sv, ss, vs, vs, vs, vv0, vv1, vv1, vv1, L1["Wfc1"]], axis=1)
    z = lambda r, c: np.zeros((r, c), f32)
    Wal, Wsv, Wvv = L0["W_alpha"], L0["Ws_val"], L0["Wv_val"]
    Wsl, Wvl = L0["Ws_vlin"], L0["Wv_vlin"]
    parts = {}
    parts["WsSD"] = np.concatenate([L0["Ws_src"], L0["Ws_dst"]], axis=1)
    parts["WvSD"] = np.concatenate([node_rows(L0["Wv_src"]), node_rows(L0["Wv_dst"])], axis=1)
    parts["gs"], parts["bs"] = L0["gamma_s"][:, None], L0["beta_s"][:, None]
    parts["gv"] = np.repeat(L0["gamma_v"], 3)[:, None]
    parts["WvT1"], parts["WvT2"] = z(64, 128), z(64, 128)
    parts["WvT1"][:, 64:] = Wsv.T[:, :64]
    parts["WvT2"][:, 96:] = Wsv.T[:, 64:]
    parts["Wg"] = L0["Wg"]
    parts["W1a"] = z(128, 192)
    parts["W1a"][:64, 160:] = Wvv[:64]
    parts["W1a"][64:, :64], parts["W1a"][64:, 96:160] = Wsv[:64], Wal[:64]
    parts["W1b"] = z(128, 288)
    parts["W1b"][:96, 192:] = blocks(Wvv[64:96])
    parts["W1b"][96:, :64], parts["W1b"][96:, 96:160] = Wsv[64:], Wal[64:]
    parts["W1c"] = blocks(Wvv[96:])
    parts["W2a"] = z(128, 96)
    parts["W2a"][:64, 64:] = Wvl[:64]
    parts["W2a"][64:, :64] = Wsl[:64]
    parts["W2b"] = z(128, 192)
    parts["W2b"][:96, 96:] = blocks(Wvl[64:96])
    parts["W2b"][96:, :64] = Wsl[64:]
    parts["W2c"] = blocks(Wvl[96:])
    parts["r2"] = z(128, 3)
    parts["r2"][:, 0] = np.concatenate([L0["w2_sv"], L0["w2_ss"]])
    parts["r2"][:, 1] = np.concatenate([L0["w2_vs"]] * 3 + [L0["w2_vv0"]])
    parts["r2"][:96, 2] = np.concatenate([L0["w2_vv1"]] * 3)
    parts["adot"] = np.broadcast_to(L0["alpha_dot"].reshape(1, 64), (P, 64))
    po = z(160, 160)
    po[:64, :64] = L0["Wps"]
    for x in range(3):
        po[np.ix_(64 + C * x + np.arange(C), 64 + c3 + x)] = L0["Wpv"]
    parts["Wpa"], parts["Wpb"] = po[:P], po[P:]
    w3 = z(160, 320)
    w3[:64, :64], w3[:64, 160:224] = L1["Wl1_0"], L1["Wsc0"]
    w3[64:, 64:160], w3[64:, 224:] = node_rows(L1["Wl1_1"]), node_rows(L1["Wsc1"], False)
    parts["W3a"], parts["W3b"] = w3[:P], w3[P:]
    parts["Wfc2"] = L1["Wfc2"]
    w4 = z(384, 161)
    w4[:96, 0:1], w4[:96, 1:65] = L1["Wa"], L1["Wl2_s"]
    for x in range(3):
        w4[96 + C * x:96 + C * x + C, 65 + C * x:97 + C * x] = L1["Wl2_v"][64:]
        w4[192 + S * x:192 + S * x + S, 65 + C * x:97 + C * x] = L1["Wl2_v"][:64]
    parts["W4a"], parts["W4b"], parts["W4c"] = w4[:128], w4[128:256, 65:], w4[256:, 97:]
    at, cols = {}, 0
    for n, w in parts.items():
        at[n] = (cols, w.shape[0], w.shape[1])
        cols += w.shape[1]
    at["_width"] = cols
    arrays["weights"] = z(P, cols)
    for n, w in parts.items():
        arrays["weights"][:w.shape[0], at[n][0]:at[n][0] + w.shape[1]] = w

    nc = bacc.Bacc("TRN2", target_bir_lowering=False, num_devices=1)
    arrays = {"in_" + k: np.ascontiguousarray(v) for k, v in arrays.items()}
    ins = {k[3:]: nc.dram_tensor(k, v.shape, mybir.dt.from_np(v.dtype), kind="ExternalInput").ap()
           for k, v in arrays.items()}
    out = nc.dram_tensor("out_nodes", (NK * P, D), F32, kind="ExternalOutput").ap()
    build(nc, ins, out, at, NT, NK)
    r = run_bass_kernel_spmd(nc, [arrays], core_ids=[0])
    return r.results[0]["out_nodes"][:N]
```

```python
import concourse.bass as bass
from concourse import mybir
from contextlib import ExitStack

P = 128
TG = 4
S, V, C = 64, 96, 32
D = S + V
H = 4
AGG0 = D + 2 * H
AGG1 = D + 1
OFF = 3.0e38
NODE_BATCH = 7
F32, BF16, I32 = mybir.dt.float32, mybir.dt.bfloat16, mybir.dt.int32
ALU, ACT, AX = mybir.AluOpType, mybir.ActivationFunctionType, mybir.AxisListType.X


def rep(ap, axis, n):
    ap = ap.unsqueeze(axis)
    shape = list(ap.shape)
    shape[axis] = n
    return ap.broadcast_to(shape)


def need(eng, sem, value):
    if isinstance(value, int) and value <= 0:
        return
    eng.wait_ge(sem, value)


def settle(eng):
    eng.nop(nofuse=True)


def hold(sp, sem, value):
    need(sp, sem, value)
    if not isinstance(value, int):
        settle(sp)


class Chain:

    def __init__(self, eng, sem):
        self.eng, self.sem, self.count = eng, sem, 0

    def link(self, ins):
        ins.then_inc(self.sem, 1)
        self.count = self.count + 1
        return self.count

    def on(self, eng):
        self.eng = eng
        return self

    def wait(self, mark=None):
        self.eng.wait_ge(self.sem, self.count if mark is None else mark)


class Group:

    def __init__(self, base, slot):
        self.base, self.slot, self.n = base, slot, base + slot

    def back(self, k):
        if self.slot >= k:
            return Group(self.base, self.slot - k)
        return Group(self.base - 4, self.slot - k + 4)

    def loads(self, unit):
        return self.base * (unit // 4) + unit


def steps(eng, groups, step, stages=3, ch=None):
    for n in range(4):
        before = ch.count if ch else 0
        step(Group(0, n), *(n >= k for k in range(stages)))
    entry = ch.count if ch else 0
    full = entry - before
    with eng.Fori(1, groups // 4, 1) as i:
        if ch:
            ch.count = i * (4 * full) + (entry - 4 * full)
        for u in range(4):
            step(Group(i * 4, u), *(True for _ in range(stages)))
    if ch:
        ch.count = entry + (groups - 4) * full
    for u in range(stages - 1):
        step(Group(groups, u), *(k > u for k in range(stages)))


def build(nc, ins, out, weights_at, NT, NK):
    NG = NT // TG
    SB = NT // P
    EP = NT * P
    NB = NK // NODE_BATCH
    ctx = ExitStack()
    with ctx:
        def dram(name, shape, dt=F32):
            return nc.dram_tensor(name, shape, dt, kind="Internal").ap()

        def sem(name):
            return ctx.enter_context(nc.semaphore(name))

        def sb(name, shape, dt=F32, where=ctx):
            return where.enter_context(nc.sbuf_tensor(name, shape, dt))

        rbf_parts = dram("rbf_parts", (3, 16, EP), BF16)
        edge_cut = dram("edge_cut", (NG, TG * H, P + 1))
        src_table = dram("src_table", (NK * P, D))
        dst_table = dram("dst_table", (NK * P, D))
        conv_table = dram("conv_table", (NK * P, D))
        agg0 = dram("agg0", (EP, AGG0))
        agg1 = dram("agg1", (EP, AGG1))
        carry0 = dram("carry0", (NT + 1, AGG0))
        carry1 = dram("carry1", (NT + 1, AGG1))

        banks = [ctx.enter_context(nc.psum_tensor(f"bank{i}", [P, 512], F32)) for i in range(8)]
        W = sb("W", [P, weights_at["_width"]])

        def wt(name, rows=None, c0=0, c1=None):
            at, r, c = weights_at[name]
            return W[0:r, at + c0:at + (c if c1 is None else c1)]

        ident = sb("ident", [P, P])
        rbf_w = sb("rbf_w", [P, 416], BF16)
        row_idx = sb("row_idx", [P, NK], I32)
        carry_idx = sb("carry_idx", [P, NK], I32)
        has_row = sb("has_row", [P, NK])
        has_carry = sb("has_carry", [P, NK])
        node_a = sb("node_a", [P, NK])
        degree = sb("degree", [P, NK])
        before_run = sb("before_run", [P, 1])
        chain = Chain(None, sem("vector_chain"))
        stat = sb("stat", [P, NK])
        stat2 = sb("stat2", [P, NK])

        with ExitStack() as ph:
            wload, split_load, cut_load = sem("wload"), sem("split_load"), sem("cut_load")
            stored, eye, prod, made, dma_w = (sem("prep_stored"), sem("eye"), sem("gate_product"),
                                              sem("prep_vector"), sem("prep_moved"))
            hi_done, mid_done, rest_done, low_done = (sem("split_hi"), sem("split_mid"), sem("split_rest"),
                                                      sem("split_low"))
            wr = sb("wr", [P, 416], F32, ph)
            wparts = [sb(f"wpart{i}", [P, 416], BF16, ph) for i in range(3)]
            xin = sb("xin", [P, 2048], F32, ph)
            xrest = sb("xrest", [P, 2048], F32, ph)
            xp = [sb(f"xp{i}", [P, 2048], BF16, ph) for i in range(3)]
            dsts = sb("dsts", [P, SB, P + 1], I32, ph)
            cut = sb("cut", [P, SB, P + 1], F32, ph)
            zrow = sb("zrow", [P, AGG0], F32, ph)
            rbf_v = ins["rbf_t"].rearrange("c (h n) -> (c h) n", h=8)
            parts_v = [rbf_parts[i].rearrange("c (h n) -> (c h) n", h=8) for i in range(3)]

            with nc.Block() as block:
                @block.sync
                def _(sp):
                    sp.dma_start(W[:, :], ins["weights"]).then_inc(wload, 16)
                    for c in range(8):
                        sp.dma_start(wr[16 * c:16 * c + 16, :], ins["rbf_w"]).then_inc(wload, 16)
                    sp.dma_start(dsts[:, :, :], ins["dst_rows"].rearrange("(b t) e -> t b e", t=P))\
                        .then_inc(cut_load, 16)
                    sp.dma_start(node_a[:, :], ins["node_a"]).then_inc(wload, 16)
                    hold(sp, made, 3)
                    for c, wp in enumerate((0, 1, 2, 0, 1, 2, 0, 1)):
                        sp.dma_start(rbf_w[16 * c:16 * c + 16, :], wparts[wp][16 * c:16 * c + 16, :])\
                            .then_inc(dma_w, 16)
                    hold(sp, dma_w, 128)
                    for b in range(SB):
                        if b >= 1:
                            hold(sp, stored, 48 * b)
                        sp.dma_start(xin[:, :], rbf_v[:, 2048 * b:2048 * b + 2048]).then_inc(split_load, 16)
                        hold(sp, hi_done, b + 1)
                        sp.dma_start(parts_v[0][:, 2048 * b:2048 * b + 2048], xp[0][:, :]).then_inc(stored, 16)
                        hold(sp, mid_done, b + 1)
                        sp.dma_start(parts_v[1][:, 2048 * b:2048 * b + 2048], xp[1][:, :]).then_inc(stored, 16)
                        hold(sp, low_done, b + 1)
                        sp.dma_start(parts_v[2][:, 2048 * b:2048 * b + 2048], xp[2][:, :]).then_inc(stored, 16)
                    hold(sp, stored, 48 * SB)
                    hold(sp, made, 6)
                    for h in range(H):
                        sp.dma_start(edge_cut.rearrange("g (j h) e -> h (g j) e", h=H)[h]
                                     .rearrange("(b t) e -> t b e", t=P), cut[:, :, :]).then_inc(dma_w, 16)
                    sp.dma_start(carry0[0:1, :], zrow[0:1, :]).then_inc(dma_w, 16)
                    sp.dma_start(carry1[0:1, :], zrow[0:1, 0:AGG1]).then_inc(dma_w, 16)
                    hold(sp, dma_w, 128 + 16 * (H + 2))

                @block.gpsimd
                def _(pool):
                    pool.memset(ident[:, :], 0.0).then_inc(eye, 1)
                    pool.wait_ge(eye, 1)
                    pool.affine_select(out=ident[:, :], in_=ident[:, :], compare_op=ALU.not_equal, fill=1.0,
                                       base=0, pattern=[[-1, P]], channel_multiplier=1).then_inc(eye, 1)

                @block.scalar
                def _(act):
                    for b in range(SB):
                        act.wait_ge(split_load, 16 * b + 16)
                        act.activation(xp[0][:, :], xin[:, :], ACT.Copy).then_inc(hi_done, 1)
                        act.wait_ge(rest_done, b + 1)
                        act.activation(xp[1][:, :], xrest[:, :], ACT.Copy).then_inc(mid_done, 1)

                @block.vector
                def _(dve):
                    ch = chain.on(dve)
                    dve.wait_ge(wload, 160)
                    dve.tensor_copy(wparts[0][:, :], wr[:, :]).then_inc(made, 1)
                    dve.wait_ge(made, 1)
                    ch.link(dve.tensor_tensor(wr[:, :], wr[:, :], wparts[0][:, :], ALU.subtract))
                    ch.wait()
                    dve.tensor_copy(wparts[1][:, :], wr[:, :]).then_inc(made, 1)
                    dve.wait_ge(made, 2)
                    dve.tensor_tensor(wparts[2][:, :], wr[:, :], wparts[1][:, :], ALU.subtract).then_inc(made, 1)
                    dve.wait_ge(cut_load, 16)
                    ch.link(dve.tensor_tensor(cut[:, :, 1:P], dsts[:, :, 2:P + 1], dsts[:, :, 1:P], ALU.not_equal))
                    ch.wait()
                    dve.tensor_scalar(cut[:, :, 1:P], cut[:, :, 1:P], -OFF, None, ALU.mult).then_inc(made, 1)
                    dve.memset(cut[:, :, 0:P + 1:P], -OFF).then_inc(made, 1)
                    dve.memset(zrow[:, :], 0.0).then_inc(made, 1)
                    r3, r2 = 3.0 ** -0.5, 2.0 ** -0.5
                    dve.wait_ge(prod, 1)
                    ch.link(dve.tensor_copy(wt("W1a", c0=64, c1=96)[64:128], banks[0][64:128, 0:C]))
                    ch.link(dve.tensor_copy(wt("W1b", c0=64, c1=96)[96:128], banks[1][96:128, 0:C]))
                    ch.wait()
                    ch.link(dve.tensor_scalar(wt("W1b")[96:128], wt("W1b")[96:128], r3, None, ALU.mult))
                    ch.link(dve.tensor_scalar(wt("W1c"), wt("W1c"), r2, None, ALU.mult))
                    for k, (n, f) in enumerate((("W2a", 0.5), ("W2b", 0.5), ("W2c", 0.5 * r2))):
                        r = weights_at[n][1]
                        ch.link(dve.tensor_scalar(wt(n), wt(n), wt("r2")[0:r, k:k + 1], f, ALU.mult, ALU.mult))
                    ch.wait()
                    ch.link(dve.tensor_scalar(wt("W2b")[96:128], wt("W2b")[96:128], r3, None, ALU.mult))
                    ch.link(dve.tensor_scalar(wt("W3a")[0:64], wt("W3a")[0:64], 0.125, None, ALU.mult))
                    ch.link(dve.tensor_scalar(wt("W3a")[64:128], wt("W3a")[64:128], 32.0 ** -0.5, None, ALU.mult))
                    ch.link(dve.tensor_scalar(wt("W3b"), wt("W3b"), 32.0 ** -0.5, None, ALU.mult))
                    ch.link(dve.tensor_scalar(wt("Wfc2"), wt("Wfc2"), 0.125 * 0.125, None, ALU.mult))
                    for n in ("W4a", "W4b", "W4c"):
                        ch.link(dve.tensor_scalar(wt(n), wt(n), 96.0 ** -0.5, None, ALU.mult))
                    ch.wait()
                    ch.link(dve.tensor_scalar(wt("W4a")[64:96], wt("W4a")[64:96], r3, None, ALU.mult))
                    ch.wait()
                    for b in range(SB):
                        dve.wait_ge(hi_done, b + 1)
                        dve.tensor_tensor(xrest[:, :], xin[:, :], xp[0][:, :], ALU.subtract).then_inc(rest_done, 1)
                        dve.wait_ge(mid_done, b + 1)
                        dve.tensor_tensor(xp[2][:, :], xrest[:, :], xp[1][:, :], ALU.subtract).then_inc(low_done, 1)

                @block.tensor
                def _(pe):
                    pe.wait_ge(wload, 160)
                    pe.matmul(banks[0][:, 0:C], wt("WvT1"), wt("Wg"), start=True, stop=True)
                    pe.matmul(banks[1][:, 0:C], wt("WvT2"), wt("Wg"), start=True, stop=True).then_inc(prod, 1)

        with ExitStack() as ph:
            X = sb("X", [P, NK, D], F32, ph)
            scr = sb("scr", [P, NK, V], F32, ph)
            nf = sb("nf", [P, NK], F32, ph)
            n_int = sb("n_int", [P, NK], I32, ph)
            level = sb("level", [P, NK], F32, ph)
            found = sb("found", [P, NK], F32, ph)
            level_i = sb("level_i", [P, NK], I32, ph)
            idx_s = sb("idx_s", [P, NODE_BATCH], I32, ph)
            sup = sb("sup", [P, SB], I32, ph)
            rows = sb("rows", [P, NODE_BATCH, P + 1], I32, ph)
            cmp = sb("cmp", [P, NODE_BATCH, P], F32, ph)
            xk = [sb(f"xk{i}", [P, D], F32, ph) for i in range(2)]
            xts = [sb(f"xts{i}", [S, P], F32, ph) for i in range(2)]
            xtv = [sb(f"xtv{i}", [V, P], F32, ph) for i in range(2)]
            tab = [sb(f"ntab{i}", [P, 2 * D], F32, ph) for i in range(2)]
            xload, normed, copied, xT, evacT, projd, tabbed, rooted, varred = (
                sem("xload"), sem("node_normed"), sem("node_copied"), sem("node_T"), sem("node_T_out"),
                sem("node_projected"), sem("node_tab"), sem("node_rooted"), sem("node_var"))
            tab_out = [sem(f"node_tab_stored{i}") for i in range(2)]
            iota_done, lvl_idx, idx_copied, batch_done, ends_made, before_in = (
                sem("iota"), sem("level_index"), sem("index_copied"), sem("batch_compared"), sem("ends_made"),
                sem("before_run_in"))
            rows_in = [sem(f"rows_in{i}") for i in range(2)]
            src_v = src_table.rearrange("(p k) d -> p k d", k=NK)
            dst_v = dst_table.rearrange("(p k) d -> p k d", k=NK)
            last_rows = ins["last"].rearrange("(b t) -> b t", t=P)

            def node_loop(eng, body):
                for k in range(2):
                    body(k, k)
                with eng.Fori(1, NK // 2, 1) as i:
                    for u in range(2):
                        body(i * 2 + u, u)

            def batch_loop(eng, body):
                body(0)
                if NB > 1:
                    with eng.Fori(1, NB, 1) as b:
                        body(b)

            with nc.Block() as block:
                @block.sync
                def _(sp):
                    sp.dma_start(X[:, :, :], ins["x"].rearrange("(p k) d -> p k d", k=NK)).then_inc(xload, 16)
                    sp.dma_start(sup[:, :], ins["sup"].partition_broadcast(P)).then_inc(xload, 16)

                    def store(k, q):
                        hold(sp, tabbed, k + 1)
                        sp.dma_start(src_v[:, bass.ds(k, 1), :].squeeze(1), tab[q][:, 0:D]).then_inc(tab_out[q], 16)
                        sp.dma_start(dst_v[:, bass.ds(k, 1), :].squeeze(1), tab[q][:, D:2 * D])\
                            .then_inc(tab_out[q], 16)
                    node_loop(sp, store)
                    for q in range(2):
                        hold(sp, tab_out[q], 32 * (NK // 2))
                @block.gpsimd
                def _(pool):
                    pool.iota(n_int[:, :], pattern=[[1, NK]], base=0, channel_multiplier=NK).then_inc(iota_done, 1)
                    for lvl in range(2):
                        table = last_rows if lvl == 0 else ins["dst_rows"]
                        width = P if lvl == 0 else P + 1

                        def batch(b):
                            if isinstance(b, int) and b == 0:
                                pool.wait_ge(lvl_idx, lvl + 1)
                                need(pool, batch_done, lvl * NB)
                            else:
                                pool.wait_ge(batch_done, b + lvl * NB)
                            pool.tensor_copy(idx_s[:, :], level_i[:, bass.ds(b * NODE_BATCH, NODE_BATCH)])\
                                .then_inc(idx_copied, 1)
                            pool.wait_ge(idx_copied, b + (lvl * NB + 1))
                            settle(pool)
                            for j in range(NODE_BATCH):
                                pool.indirect_dma_start(
                                    out=rows[:, j, 0:width], out_offset=None, in_=table,
                                    in_offset=bass.IndirectOffsetOnAxis(ap=idx_s[:, j:j + 1], axis=0)
                                ).then_inc(rows_in[lvl], 16)
                        batch_loop(pool, batch)
                    pool.wait_ge(ends_made, 2)
                    pool.dma_start(before_run[1:P, :], nf[0:P - 1, NK - 1:NK]).then_inc(before_in, 16)

                @block.scalar
                def _(act):
                    act.wait_ge(varred, 2)
                    act.activation(stat[:, :], stat[:, :], ACT.Sqrt).then_inc(rooted, 1)
                    act.activation(stat2[:, :], stat2[:, :], ACT.Sqrt).then_inc(rooted, 1)
                    act.wait_ge(normed, 2)

                    def body(k, q):
                        need(act, xT, k - 1)
                        act.activation(xk[q][:, :], X[:, bass.ds(k, 1), :].squeeze(1), ACT.Copy).then_inc(copied, 1)
                        act.wait_ge(xT, k + 1)
                        need(act, projd, k - 1)
                        act.activation(xts[q][:, :], banks[2 * q][0:S, 0:P], ACT.Identity,
                                       scale=wt("gs"), bias=wt("bs"))
                        act.activation(xtv[q][:, :], banks[2 * q][0:V, P:2 * P], ACT.Copy,
                                       scale=wt("gv")).then_inc(evacT, 1)
                        act.wait_ge(projd, k + 1)
                        if not (isinstance(k, int) and k < 2):
                            act.wait_ge(tab_out[q], k * 16 - 16 * q)
                        act.activation(tab[q][:, :], banks[2 * q + 1][:, 0:2 * D], ACT.Copy).then_inc(tabbed, 1)
                    node_loop(act, body)

                @block.tensor
                def _(pe):
                    def body(k, q):
                        pe.wait_ge(copied, k + 1)
                        need(pe, evacT, k - 1)
                        settle(pe)
                        pe.transpose(banks[2 * q][0:S, 0:P], xk[q][:, 0:S], ident[:, :])
                        pe.transpose(banks[2 * q][0:V, P:2 * P], xk[q][:, S:D], ident[:, :]).then_inc(xT, 1)
                        pe.wait_ge(evacT, k + 1)
                        need(pe, tabbed, k - 1)
                        o = banks[2 * q + 1]
                        for t in range(2):
                            pe.matmul(o[:, D * t:D * t + S], xts[q][:, :], wt("WsSD", c0=S * t, c1=S * t + S),
                                      start=True, stop=True)
                            mm = pe.matmul(o[:, D * t + S:D * t + D], xtv[q][:, :],
                                           wt("WvSD", c0=V * t, c1=V * t + V), start=True, stop=True)
                        mm.then_inc(projd, 1)
                    node_loop(pe, body)

                @block.vector
                def _(dve):
                    ch = chain.on(dve)
                    dve.wait_ge(xload, 32)
                    Xs, Xv = X[:, :, 0:S], X[:, :, S:D]
                    ch.link(dve.tensor_reduce(stat[:, :], Xs, AX, ALU.add)); ch.wait()
                    ch.link(dve.tensor_scalar(stat[:, :], stat[:, :], 1.0 / S, None, ALU.mult)); ch.wait()
                    ch.link(dve.tensor_tensor(Xs, Xs, rep(stat[:, :], 2, S), ALU.subtract)); ch.wait()
                    ch.link(dve.tensor_tensor(scr[:, :, 0:S], Xs, Xs, ALU.mult)); ch.wait()
                    ch.link(dve.tensor_reduce(stat[:, :], scr[:, :, 0:S], AX, ALU.add)); ch.wait()
                    dve.tensor_scalar(stat[:, :], stat[:, :], 1.0 / S, 1e-5, ALU.mult, ALU.add).then_inc(varred, 1)
                    ch.link(dve.tensor_tensor(scr[:, :, :], Xv, Xv, ALU.mult)); ch.wait()
                    ch.link(dve.tensor_reduce(stat2[:, :], scr[:, :, :], AX, ALU.add)); ch.wait()
                    dve.tensor_scalar(stat2[:, :], stat2[:, :], 1.0 / C, 1e-5, ALU.mult, ALU.add).then_inc(varred, 1)
                    dve.wait_ge(rooted, 2)
                    ch.link(dve.reciprocal(stat[:, :], stat[:, :]))
                    ch.link(dve.reciprocal(stat2[:, :], stat2[:, :])); ch.wait()
                    dve.tensor_tensor(Xs, Xs, rep(stat[:, :], 2, S), ALU.mult).then_inc(normed, 1)
                    dve.tensor_tensor(Xv, Xv, rep(stat2[:, :], 2, V), ALU.mult).then_inc(normed, 1)
                    dve.wait_ge(iota_done, 1)
                    ch.link(dve.tensor_copy(nf[:, :], n_int[:, :])); ch.wait()
                    ch.link(dve.tensor_tensor(scr[:, :, 0:SB], rep(sup[:, :], 1, NK), rep(nf[:, :], 2, SB),
                                              ALU.is_le)); ch.wait()
                    ch.link(dve.tensor_reduce(level[:, :], scr[:, :, 0:SB], AX, ALU.add)); ch.wait()
                    ch.link(dve.tensor_scalar(level[:, :], level[:, :], float(SB - 1), None, ALU.min)); ch.wait()
                    dve.tensor_copy(level_i[:, :], level[:, :]).then_inc(lvl_idx, 1)

                    def count(lvl, first):
                        def batch(b):
                            dve.wait_ge(rows_in[lvl], b * (16 * NODE_BATCH) + 16 * NODE_BATCH)
                            cols = bass.ds(b * NODE_BATCH, NODE_BATCH)
                            e0 = 0 if lvl == 0 else 1
                            dve.tensor_tensor(cmp[:, :, :], rows[:, :, e0:e0 + P], rep(nf[:, cols], 2, P), ALU.is_le)\
                                .then_inc(cmp_step, 1)
                            s = 1 if lvl == 0 else 4
                            dve.wait_ge(cmp_step, b * s + (first + 1))
                            if lvl == 0:
                                dve.tensor_reduce(found[:, cols], cmp[:, :, :], AX, ALU.add).then_inc(batch_done, 1)
                                return
                            dve.tensor_reduce(found[:, cols], cmp[:, :, :], AX, ALU.add).then_inc(cmp_step, 1)
                            dve.wait_ge(cmp_step, b * 4 + (first + 2))
                            dve.tensor_tensor(cmp[:, :, :], rows[:, :, 1:P + 1], rep(nf[:, cols], 2, P),
                                              ALU.is_equal).then_inc(cmp_step, 1)
                            dve.wait_ge(cmp_step, b * 4 + (first + 3))
                            dve.tensor_reduce(has_row[:, cols], cmp[:, :, :], AX, ALU.max).then_inc(cmp_step, 1)
                            dve.tensor_tensor(has_carry[:, cols], rows[:, :, 0], nf[:, cols], ALU.is_equal)\
                                .then_inc(batch_done, 1)
                        return batch
                    cmp_step = sem("compare_step")
                    batch_loop(dve, count(0, 0))
                    dve.wait_ge(batch_done, NB)
                    ch.link(dve.scalar_tensor_tensor(out=level[:, :], in0=level[:, :], scalar=float(P),
                                                     in1=found[:, :], op0=ALU.mult, op1=ALU.add)); ch.wait()
                    ch.link(dve.tensor_scalar(level[:, :], level[:, :], float(NT - 1), None, ALU.min)); ch.wait()
                    dve.tensor_copy(level_i[:, :], level[:, :]).then_inc(lvl_idx, 1)
                    dve.wait_ge(lvl_idx, 2)
                    ch.link(dve.tensor_copy(carry_idx[:, :], level_i[:, :]))
                    batch_loop(dve, count(1, NB))
                    dve.wait_ge(batch_done, 2 * NB)
                    ends = nf
                    dve.scalar_tensor_tensor(out=ends[:, :], in0=level[:, :], scalar=float(P), in1=found[:, :],
                                             op0=ALU.mult, op1=ALU.add).then_inc(ends_made, 1)
                    dve.memset(before_run[0:1, :], 0.0).then_inc(ends_made, 1)
                    dve.wait_ge(ends_made, 2)
                    ch.link(dve.tensor_scalar(found[:, :], found[:, :], -1.0, 0.0, ALU.add, ALU.max)); ch.wait()
                    ch.link(dve.scalar_tensor_tensor(out=level[:, :], in0=level[:, :], scalar=float(P),
                                                     in1=found[:, :], op0=ALU.mult, op1=ALU.add)); ch.wait()
                    ch.link(dve.tensor_copy(row_idx[:, :], level[:, :]))
                    ch.link(dve.tensor_tensor(degree[:, 1:NK], ends[:, 1:NK], ends[:, 0:NK - 1], ALU.subtract))
                    dve.wait_ge(before_in, 16)
                    ch.link(dve.tensor_tensor(degree[:, 0:1], ends[:, 0:1], before_run[:, :], ALU.subtract))
                    ch.wait()

        edge_loop_0(nc, ctx, sem, banks, W, wt, ident, rbf_w, ins, rbf_parts, edge_cut, src_table, dst_table,
                    agg0, NG)
        carry_scan(nc, ctx, sem, banks, ident, ins, agg0, carry0, NT, AGG0, True)

        X1 = sb("X1", [P, NK, D])
        node_step_0(nc, ctx, sem, banks, wt, ident, ins, agg0, carry0, conv_table, X1, row_idx, carry_idx,
                    has_row, has_carry, node_a, stat, stat2, chain, NK)
        edge_loop_1(nc, ctx, sem, banks, wt, rbf_w, ins, rbf_parts, conv_table, agg1, NG)
        carry_scan(nc, ctx, sem, banks, ident, ins, agg1, carry1, NT, AGG1, False)
        node_step_1(nc, ctx, sem, banks, agg1, carry1, out, X1, row_idx, carry_idx, has_row, has_carry,
                    node_a, stat, degree, chain, NK)


def edge_loop_0(nc, ctx, sem, banks, W, wt, ident, rbf_w, ins, rbf_parts, edge_cut, src_table, dst_table,
                agg0, NG):
    with ExitStack() as ph:
        def sb(name, shape, dt=F32):
            return ph.enter_context(nc.sbuf_tensor(name, shape, dt))
        pack = [sb(f"e_pack{i}", [P, 32], I32) for i in range(4)]
        idx = [p[:, 0:8] for p in pack]
        Y = [p[:, 8:32].bitcast(F32).rearrange("p (t c) -> p t c", t=TG) for p in pack]
        xs = [sb(f"e_xs{i}", [P, 512], BF16) for i in range(4)]
        drow = [sb(f"e_drow{i}", [P, 512], I32) for i in range(4)]
        cut = [sb(f"e_cut{i}", [16, P + 1]) for i in range(4)]
        feat = [sb(f"feat{i}", [P, TG, D + 64]) for i in range(4)]
        stg = [sb(f"stg{i}", [P, TG, 352]) for i in range(2)]
        feat2 = sb("mid_feat", [P, TG, D + 64])
        tmp = [sb(f"tmp{i}", [P, TG, V]) for i in range(6)]
        vlin = sb("vlin", [P, TG, V])
        tabs = [sb(f"tabs{k}", [P, 512]) for k in range(3)]
        prods = [sb(f"prods{k}", [P, 512]) for k in range(3)]
        st2 = [sb(f"st2_{k}", [P, 512]) for k in range(3)]
        lg = sb("lg", [P, TG, S])
        th = [sb(f"th{i}", [P, TG, V]) for i in range(2)]
        av = [sb(f"av{i}", [P, TG, 192]) for i in range(2)]
        gate = sb("gate", [P, TG, C])
        a_e = [sb(f"a_e{i}", [P, 16]) for i in range(2)]
        late_Y = [sb(f"late_Y{i}", [P, TG, 6]) for i in range(4)]
        one = sb("one", [P, 1])
        run_max = sb("run_max", [16, P])
        seg_max = sb("seg_max", [16, P])
        diff = sb("diff", [P, 16])
        ex8 = sb("ex8", [P, TG, C])
        ha = [sb(f"ha{i}", [P, TG, D + H]) for i in range(2)]
        hv = sb("hv", [P, TG, V])
        eq = [sb(f"eq{i}", [P, TG, P]) for i in range(4)]
        orow = [sb(f"orow{i}", [P, TG, AGG0]) for i in range(2)]

        small_in = [sem(f"l0_small_in{i}") for i in range(4)]

        big_in = [sem(f"l0_big_in{i}") for i in range(4)]
        gathered = [sem(f"l0_gathered{i}") for i in range(4)]
        out_done = [sem(f"l0_out_done{i}") for i in range(2)]
        (table_mm, table_out, v_dup, scaled1, v2_done, v2_dup, scaled2, gated, staged1, staged1_T, product,
         stage1, stage1_out, logit, logit_T, logit_read, maxed, max_T, diffed, exped, max_out, staged2,
         staged2_T, st2_out, stage2, eq_made, ha_made, agg, agg_out) = (sem("l0_" + n) for n in (
             "table_mm", "table_out", "v_dup", "scaled1", "v2_done", "v2_dup", "scaled2", "gated", "staged1",
             "staged1_T", "product", "stage1", "stage1_out", "logit", "logit_T", "logit_read", "maxed", "max_T",
             "diffed", "exped", "max_out", "staged2", "staged2_T", "st2_out", "stage2", "eq_made", "ha_made",
             "agg", "agg_out"))
        own, one_made = sem("l0_vector_chain"), sem("l0_one_made")
        agg_v = agg0.rearrange("(g j p) c -> g p j c", j=TG, p=P)
        xs_v = rbf_parts.rearrange("s c (g n) -> s g c n", n=512)
        drow_v = ins["dst_flat"].rearrange("(g n) -> g n", n=512)
        PARTS = ((0, 3), (1, 3), (2, 2))

        with nc.Block() as block:
            @block.sync
            def _(sp):
                def step(g, early, front, mid, tail):
                    if not early:
                        return
                    s, n = g.slot, g.n
                    hold(sp, table_mm, 3 * (n - 3))
                    hold(sp, eq_made, n - 3)
                    hold(sp, scaled1, n - 3)
                    hold(sp, staged1, n - 3)
                    if not (isinstance(g.base, int) and g.base == 0):
                        hold(sp, gathered[s], g.base * 32)
                    at = bass.ds(n, 1)
                    sp.dma_start(pack[s][:, :], ins["edge_pack"][at].squeeze(0)).then_inc(small_in[s], 16)
                    c0 = 0
                    for part, copies in PARTS:
                        sp.dma_start(xs[s][c0:c0 + 16 * copies, :], rep(xs_v[part, at], 0, copies).squeeze(1))\
                            .then_inc(big_in[s], 16)
                        c0 += 16 * copies
                    sp.dma_start(drow[s][:, :], drow_v[at].broadcast_to([P, 512])).then_inc(big_in[s], 16)
                    hold(sp, maxed, n - 3)
                    sp.dma_start(cut[s][:, :], edge_cut[at].squeeze(0)).then_inc(big_in[s], 16)
                steps(sp, NG, step, 4)

            @block.gpsimd
            def _(pool):
                def gather(table, s, col, j, op):
                    pool.indirect_dma_start(
                        out=feat[s][:, j, 0:D], out_offset=None, in_=table,
                        in_offset=bass.IndirectOffsetOnAxis(ap=idx[s][:, col + j:col + j + 1], axis=0),
                        compute_op=op).then_inc(gathered[s], 16)

                def step(g, early, front, mid, tail):
                    if front:
                        f = g.back(1)
                        pool.wait_ge(gathered[f.slot], f.base * 32 + 64)
                        settle(pool)
                        for j in range(TG):
                            gather(dst_table, f.slot, 4, j, ALU.add)
                    if early:
                        s = g.slot
                        need(pool, staged1, g.n - 3)
                        need(pool, scaled1, g.n - 3)
                        pool.wait_ge(small_in[s], g.loads(16))
                        settle(pool)
                        for j in range(TG):
                            gather(src_table, s, 0, j, ALU.bypass)
                steps(pool, NG, step, 4)

            @block.vector
            def _(dve):
                ch = Chain(dve, own)

                def comp(ap, c0, n=3, w=C):
                    return ap[:, :, c0:c0 + n * w].rearrange("p t (x c) -> p t x c", c=w)

                def yx(y, c0, w=C):
                    return rep(y[:, :, c0:c0 + 3], 3, w)

                def products_with_y(st, f, tmp, y, dup_sem, dup_at, last_sem):
                    a = ch.link(dve.tensor_tensor(comp(tmp[0], 0), comp(f, S), yx(y, 1), ALU.mult))
                    dve.wait_ge(dup_sem, dup_at)
                    b = ch.link(dve.tensor_tensor(comp(tmp[1], 0), comp(f, S + C), yx(y, 3), ALU.mult))
                    ch.wait(a)
                    a = ch.link(dve.tensor_tensor(st[:, :, 224:256], tmp[0][:, :, 0:C], tmp[0][:, :, C:2 * C],
                                                  ALU.add))
                    c = ch.link(dve.tensor_tensor(comp(tmp[2], 0), comp(f, S + 2 * C), yx(y, 2), ALU.mult))
                    ch.wait(a)
                    ch.link(dve.tensor_tensor(st[:, :, 224:256], st[:, :, 224:256], tmp[0][:, :, 2 * C:V],
                                              ALU.add))
                    ch.wait(c)
                    dve.tensor_tensor(st[:, :, 256:352], tmp[1][:, :, :], tmp[2][:, :, :], ALU.subtract)\
                        .then_inc(last_sem, 1)

                def gated_values(m):
                    q, y = m.slot % 2, late_Y[m.slot]
                    dve.wait_ge(stage1_out, 4 * (m.n + 1))
                    dve.wait_ge(v_dup, 2 * m.n + 1)
                    need(dve, diffed, m.n - 1)
                    need(dve, staged2, m.n)
                    need(dve, scaled2, m.n)
                    b = ch.link(dve.tensor_tensor(comp(vlin, 0), rep(av[q][:, :, S:V], 2, 3), yx(y, 1), ALU.mult))
                    a = ch.link(dve.scalar_tensor_tensor(out=lg[:, :, :], in0=av[q][:, :, 0:S], scalar=0.2,
                                                         in1=av[q][:, :, 0:S], op0=ALU.mult, op1=ALU.max))
                    ch.wait(b)
                    b = ch.link(dve.tensor_tensor(vlin[:, :, :], vlin[:, :, :], av[q][:, :, V:192], ALU.add))
                    ch.wait(a)
                    a = ch.link(dve.tensor_tensor(lg[:, :, :], lg[:, :, :], rep(wt("adot"), 1, TG), ALU.mult))
                    dve.wait_ge(gated, m.n + 1)
                    ch.wait(b)
                    dve.tensor_tensor(comp(feat2, S), comp(vlin, 0), rep(gate[:, :, :], 2, 3), ALU.mult)\
                        .then_inc(v2_done, 1)
                    ch.wait(a)
                    dve.tensor_reduce(a_e[q][:, :], lg[:, :, :].rearrange("p t (h c) -> p (t h) c", h=H), AX,
                                      ALU.add).then_inc(logit, 1)

                def half(t, q, y, b):
                    ts2, o = slice(2 * b, 2 * b + 2), banks[5 + b][:, 0:384].rearrange("p (t c) -> p t c", t=2)
                    dve.wait_ge(stage2, 2 * t.n + (b + 1))
                    a = ch.link(dve.tensor_tensor(
                        hv[:, ts2, :].rearrange("p t (x c) -> p t x c", c=C), rep(o[:, :, 64:96], 2, 3),
                        rep(y[:, ts2, 1:4], 3, C), ALU.mult))
                    ch.link(dve.tensor_tensor(
                        ha[q][:, ts2, 0:S].rearrange("p t (h c) -> p t h c", h=H),
                        o[:, :, 0:64].rearrange("p t (h c) -> p t h c", h=H),
                        rep(ha[q][:, ts2, D:D + H], 3, 16), ALU.mult))
                    ch.wait(a)
                    return ch.link(dve.tensor_tensor(hv[:, ts2, :], hv[:, ts2, :], o[:, :, 96:192], ALU.add))

                def step(g, early, front, mid, tail):
                    f, m, t = (g.back(k) for k in (1, 2, 3))
                    if mid:
                        gated_values(m)
                    if early:
                        s, n = g.slot, g.n
                        dve.wait_ge(big_in[s], g.loads(80))
                        dve.wait_ge(small_in[s], g.loads(16))
                        need(dve, agg, 2 * (n - 3))
                        dve.tensor_tensor(eq[s][:, :, :], drow[s][:, :].rearrange("p (t e) -> p t e", t=TG),
                                          rep(idx[s][:, 4:8], 2, P), ALU.is_equal).then_inc(eq_made, 1)
                    if front:
                        for k, r in enumerate((P, P, V)):
                            dve.wait_ge(staged1_T, 3 * f.n + (k + 1))
                            dve.wait_ge(table_out, 3 * f.n + (k + 1))
                            if k == 0:
                                need(dve, stage1, 4 * f.n)
                            dve.tensor_tensor(prods[k][0:r, :], tabs[k][0:r, :], banks[k][0:r, :], ALU.mult)\
                                .then_inc(product, 1)
                    if tail:
                        y, q = late_Y[t.slot], t.slot % 2
                        dve.wait_ge(max_T, t.n + 1)
                        need(dve, exped, t.n)
                        dve.tensor_tensor(diff[:, :], a_e[q][:, :], banks[7][:, 328:344], ALU.subtract)\
                            .then_inc(diffed, 1)
                    if early:
                        dve.wait_ge(gathered[s], g.loads(128))
                        need(dve, staged1_T, 3 * n)
                        need(dve, staged1, n)
                        products_with_y(stg[0], feat[s], tmp[0:3], Y[s], v_dup, 2 * (n + 1), staged1)
                    if tail:
                        need(dve, ha_made, t.n)
                    if mid:
                        dve.wait_ge(logit_T, m.n + 1)
                    if tail:
                        dve.wait_ge(exped, t.n + 1)
                        half(t, q, y, 0)
                    if mid:
                        dve.wait_ge(big_in[m.slot], m.loads(80))
                        dve.tensor_tensor_scan(run_max[:, :], cut[m.slot][:, 0:P], banks[5][0:16, 384:512], -OFF,
                                               ALU.add, ALU.max).then_inc(logit_read, 1)
                    if tail:
                        last = half(t, q, y, 1)
                        ch.wait(last)
                        dve.tensor_tensor(comp(ha[q], S), comp(hv, 0), rep(ex8[:, :, :], 2, 3), ALU.mult)\
                            .then_inc(ha_made, 1)
                    if mid:
                        need(dve, staged2_T, 3 * m.n)
                        dve.wait_ge(v2_done, m.n + 1)
                        products_with_y(stg[1], feat2, tmp[3:6], late_Y[m.slot], v2_dup, 2 * (m.n + 1), staged2)
                        dve.wait_ge(logit_read, m.n + 1)
                        need(dve, max_T, m.n)
                        dve.tensor_tensor_scan(seg_max[:, ::-1], cut[m.slot][:, P:0:-1], run_max[:, ::-1], -OFF,
                                               ALU.add, ALU.max).then_inc(maxed, 1)
                dve.memset(one[:, :], 1.0).then_inc(one_made, 1)
                steps(dve, NG, step, 4, ch)

            @block.scalar
            def _(act):
                def scaled_by_y0(st, f, y, done):
                    for j in range(TG):
                        last = act.activation(st[:, j, S:S + D], f[:, j, 0:D], ACT.Copy, scale=y[:, j, 0:1])
                    last.then_inc(done, 1)

                def step(g, early, front, mid, tail):
                    f, m, t = (g.back(k) for k in (1, 2, 3))
                    if early:
                        e = feat[g.slot]
                        act.wait_ge(small_in[g.slot], g.loads(16))
                        need(act, ha_made, g.n - 3)
                        need(act, staged2, g.n - 3)
                        need(act, scaled2, g.n - 3)
                        act.activation(late_Y[g.slot][:, :, :], Y[g.slot][:, :, :], ACT.Copy).then_inc(v_dup, 1)
                        act.wait_ge(gathered[g.slot], g.loads(128))
                        act.activation(e[:, :, D:D + 64], e[:, :, S:S + 64], ACT.Copy).then_inc(v_dup, 1)
                    if mid:
                        act.wait_ge(stage1_out, 4 * (m.n + 1))
                        need(act, scaled2, m.n)
                        need(act, staged2_T, 3 * m.n)
                        q = m.slot % 2
                        act.activation(stg[1][:, :, 0:S], th[q][:, :, 0:S], ACT.Identity, bias=one[:, 0:1])
                        act.activation(feat2[:, :, 0:S], th[q][:, :, 0:S], ACT.Identity, bias=one[:, 0:1])\
                            .then_inc(v2_dup, 1)
                        act.wait_ge(v2_done, m.n + 1)
                        act.activation(feat2[:, :, D:D + 64], feat2[:, :, S:S + 64], ACT.Copy).then_inc(v2_dup, 1)
                        act.wait_ge(v2_dup, 2 * m.n + 1)
                        scaled_by_y0(stg[1], feat2, late_Y[m.slot], scaled2)
                    if tail:
                        q = t.slot % 2
                        if not (isinstance(t.base, int) and t.base == 0 and t.slot < 2):
                            act.wait_ge(out_done[q], t.base * 8 + 16 * (t.slot // 2))
                        act.wait_ge(diffed, t.n + 1)
                        need(act, ha_made, t.n)
                        act.activation(ha[q][:, :, D:D + H], diff[:, :].rearrange("p (t h) -> p t h", t=TG), ACT.Exp)
                        act.activation(ex8[:, :, :].rearrange("p t (h c) -> p (t h) c", h=H), rep(diff[:, :], 2, 8),
                                       ACT.Exp).then_inc(exped, 1)
                        act.activation(orow[q][:, :, D + H:AGG0],
                                       banks[7][:, 328:344].rearrange("p (t h) -> p t h", t=TG), ACT.Copy)\
                            .then_inc(max_out, 1)
                    if early:
                        need(act, staged1_T, 3 * g.n)
                        act.activation(stg[0][:, :, 0:S], e[:, :, 0:S], ACT.Copy)
                        scaled_by_y0(stg[0], e, Y[g.slot], scaled1)
                    if front:
                        q = f.slot % 2
                        need(act, v2_done, f.n - 1)
                        need(act, logit, f.n - 1)
                        for j in range(TG):
                            act.wait_ge(stage1, 4 * f.n + (j + 1))
                            o = banks[3 + j % 2]
                            act.activation(th[q][:, j, :], o[:, 0:V], ACT.Tanh, scale=0.5)
                            act.activation(av[q][:, j, :], o[:, V:288], ACT.Copy).then_inc(stage1_out, 1)
                        act.wait_ge(stage1_out, 4 * (f.n + 1))
                        need(act, v2_done, f.n)
                        act.activation(gate[:, :, :], th[q][:, :, S:V], ACT.Identity, bias=one[:, 0:1])\
                            .then_inc(gated, 1)
                    if tail:
                        agg_evac(t, 0)
                        agg_evac(t, 1)
                        act.wait_ge(agg_out, 2 * (t.n + 1))
                        act.dma_start(agg_v[bass.ds(t.n, 1)].squeeze(0), orow[t.slot % 2][:, :, :])\
                            .then_inc(out_done[t.slot % 2], 16)
                    if mid:
                        for k, r in enumerate((P, P, V)):
                            act.wait_ge(staged2_T, 3 * m.n + (k + 1))
                            need(act, stage2, 2 * m.n)
                            act.activation(st2[k][0:r, :], banks[k][0:r, :], ACT.Copy).then_inc(st2_out, 1)
                    if early:
                        n = g.n
                        for k, r in enumerate((P, P, V)):
                            act.wait_ge(table_mm, 3 * n + (k + 1))
                            need(act, product, 3 * n - 2 + k)
                            act.activation(tabs[k][0:r, :], banks[(5, 3, 4)[k]][0:r, :], ACT.Copy).then_inc(table_out, 1)

                def agg_evac(t, b):
                    q = t.slot % 2
                    act.wait_ge(agg, 2 * t.n + (b + 1))
                    act.activation(orow[q][:, 2 * b:2 * b + 2, 0:D + H],
                                   banks[7 - b][:, 0:2 * (D + H)].rearrange("p (t c) -> p t c", t=2), ACT.Copy)\
                        .then_inc(agg_out, 1)
                act.wait_ge(one_made, 1)
                steps(act, NG, step, 4)
                for i in range(2):
                    act.wait_ge(out_done[i], 16 * (NG // 2))

            @block.tensor
            def _(pe):
                def sums(t, b):
                    q, e = t.slot % 2, t.slot
                    need(pe, agg_out, 2 * t.n - 1 + b)
                    for j in (2 * b, 2 * b + 1):
                        mm = pe.matmul(banks[7 - b][:, (j % 2) * (D + H):(j % 2 + 1) * (D + H)], eq[e][:, j, :],
                                       ha[q][:, j, :], start=True, stop=True)
                    mm.then_inc(agg, 1)

                def tables(g):
                    pe.wait_ge(big_in[g.slot], g.loads(80))
                    need(pe, stage1_out, 4 * g.n)
                    for k, r in enumerate((P, P, V)):
                        if k == 0:
                            need(pe, ha_made, g.n - 2)
                            need(pe, logit_read, g.n - 1)
                        pe.matmul(banks[(5, 3, 4)[k]][0:r, :], rbf_w[:, P * k:P * k + r], xs[g.slot][:, :],
                                  start=True, stop=True).then_inc(table_mm, 1)

                def step(g, early, front, mid, tail):
                    f, m, t = (g.back(k) for k in (1, 2, 3))
                    if front:
                        pe.wait_ge(staged1, f.n + 1)
                        pe.wait_ge(scaled1, f.n + 1)
                        for k, r in enumerate((P, P, V)):
                            need(pe, st2_out, 3 * f.n - 5 + k)
                            for j in range(TG):
                                mm = pe.transpose(banks[k][0:r, P * j:P * j + P], stg[0][:, j, P * k:P * k + r],
                                                  ident[:, :])
                            mm.then_inc(staged1_T, 1)
                    if front:
                        pe.wait_ge(table_out, 3 * f.n + 1)
                    if mid:
                        pe.wait_ge(logit, m.n + 1)
                        need(pe, logit_read, m.n)
                        need(pe, ha_made, m.n - 1)
                        pe.transpose(banks[5][0:16, 384:512], a_e[m.slot % 2][:, :], ident[:, :])\
                            .then_inc(logit_T, 1)
                    if tail:
                        pe.wait_ge(st2_out, 3 * t.n + 3)
                        need(pe, ha_made, t.n)
                        need(pe, agg_out, 2 * t.n)
                        pe.wait_ge(logit_read, t.n + 1)
                        for j in range(TG):
                            o = banks[5 + j // 2]
                            c = 192 * (j % 2)
                            e = slice(P * j, P * j + P)
                            pe.matmul(o[:, c:c + 192], st2[1][:, e], wt("W2b"), start=True, stop=False)
                            pe.matmul(o[:, c:c + 96], st2[0][:, e], wt("W2a"), start=False, stop=False)
                            mm = pe.matmul(o[:, c + 96:c + 192], st2[2][0:V, e], wt("W2c"), start=False, stop=True)
                            if j % 2:
                                mm.then_inc(stage2, 1)
                    if front:
                        pe.wait_ge(product, 3 * f.n + 3)
                        pe.wait_ge(table_out, 3 * f.n + 3)
                        for j in range(TG):
                            need(pe, stage1_out, 4 * f.n + j - 1)
                            o = banks[3 + j % 2]
                            e = slice(P * j, P * j + P)
                            pe.matmul(o[:, 0:288], prods[1][:, e], wt("W1b"), start=True, stop=False)
                            pe.matmul(o[:, 0:192], prods[0][:, e], wt("W1a"), start=False, stop=False)
                            pe.matmul(o[:, 192:288], prods[2][0:V, e], wt("W1c"), start=False, stop=True)\
                                .then_inc(stage1, 1)
                    if tail:
                        pe.wait_ge(eq_made, t.n + 1)
                        pe.wait_ge(ha_made, t.n + 1)
                        pe.wait_ge(max_out, t.n + 1)
                        sums(t, 0)
                        sums(t, 1)
                    if mid:
                        pe.wait_ge(staged2, m.n + 1)
                        pe.wait_ge(scaled2, m.n + 1)
                        for k, r in enumerate((P, P, V)):
                            if front:
                                pe.wait_ge(product, 3 * f.n + (k + 1))
                            for j in range(TG):
                                mm = pe.transpose(banks[k][0:r, P * j:P * j + P], stg[1][:, j, P * k:P * k + r],
                                                  ident[:, :])
                            mm.then_inc(staged2_T, 1)
                    if early:
                        tables(g)
                    if mid:
                        pe.wait_ge(maxed, m.n + 1)
                        need(pe, agg_out, 2 * m.n)
                        need(pe, diffed, m.n)
                        need(pe, max_out, m.n)
                        settle(pe)
                        pe.transpose(banks[7][:, 328:344], seg_max[:, :], ident[0:16, 0:16]).then_inc(max_T, 1)
                steps(pe, NG, step, 4)


def carry_scan(nc, ctx, sem, banks, ident, ins, agg, carry, NT, width, softmax):
    SB = NT // P
    tag = "c0_" if softmax else "c1_"
    R = D + H if softmax else width
    parts = ((0, P), (P, R - P))
    with ExitStack() as ph:
        def sb(name, shape, dt=F32):
            return ph.enter_context(nc.sbuf_tensor(tag + name, shape, dt))
        last = sb("last", [P, SB, width])
        mrep = sb("mrep", [P, SB, R]) if softmax else None
        edges = [sb(f"edge{i}", [P, NT], I32) for i in range(3)]
        go_on = sb("go_on", [P, NT])
        cut = sb("cut", [P, NT])
        val = [sb(f"val{i}", [P, NT]) for i in range(2)]
        mx = [sb(f"mx{i}", [P, NT]) for i in range(2)] if softmax else None
        mtop = [sb(f"mtop{i}", [P, NT]) for i in range(2)] if softmax else None
        keep = sb("keep", [P, NT])
        gain = sb("gain", [P, NT])
        back = sb("back", [P, SB, width])
        loaded, rep_done, turned, turned_out, scanned, back_T, back_out, stored, arg_done, exp_done = (
            sem(tag + n) for n in ("loaded", "rep_done", "turned", "turned_out", "scanned", "back_T", "back_out",
                                   "stored", "arg_done", "exp_done"))
        with nc.Block() as block:
            @block.sync
            def _(sp):
                sp.dma_start(last[:, :, :], agg.rearrange("(b t e) c -> e t b c", t=P, e=P)[P - 1])\
                    .then_inc(loaded, 16)
                for i, n in enumerate(("first", "last", "before")):
                    sp.dma_start(edges[i][:, :], ins[n].partition_broadcast(P)).then_inc(loaded, 16)
                hold(sp, back_out, SB)
                sp.dma_start(carry[1:NT + 1].rearrange("(b t) c -> t b c", t=P), back[:, :, :]).then_inc(stored, 16)
                hold(sp, stored, 16)

            @block.tensor
            def _(pe):
                pe.wait_ge(loaded, 64)
                if softmax:
                    pe.wait_ge(rep_done, 3)
                k = 0
                for b in range(SB):
                    for i, (c, r) in enumerate(parts):
                        for src in ((last, mrep) if softmax else (last,)):
                            if k >= 4:
                                pe.wait_ge(turned_out, k - 3)
                            pe.transpose(banks[k % 4][0:r, 0:P], src[:, b, c:c + r], ident[:, :]).then_inc(turned, 1)
                            k += 1
                pe.wait_ge(scanned, 2)
                k = 0
                for b in range(SB):
                    if k >= 4:
                        pe.wait_ge(back_out, b - 3)
                    o = banks[4 + b % 4]
                    e = slice(b * P, b * P + P)
                    for i, (c, r) in enumerate(parts):
                        mm = pe.transpose(o[:, c:c + r], val[i][0:r, e], ident[0:r, 0:r])
                    if softmax:
                        mm = pe.transpose(o[:, 256:256 + R - P], mtop[1][0:R - P, e], ident[0:R - P, 0:R - P])
                    mm.then_inc(back_T, 1)
                    k += 1

            @block.scalar
            def _(act):
                k = 0
                for b in range(SB):
                    for i, (c, r) in enumerate(parts):
                        for dst in ((val, mx) if softmax else (val,)):
                            act.wait_ge(turned, k + 1)
                            act.activation(dst[i][0:r, b * P:b * P + P], banks[k % 4][0:r, 0:P], ACT.Copy)\
                                .then_inc(turned_out, 1)
                            k += 1
                if softmax:
                    for i, (c, r) in enumerate(parts):
                        act.wait_ge(arg_done, 2 * i + 2)
                        act.activation(keep[0:r, :], keep[0:r, :], ACT.Exp)
                        act.activation(gain[0:r, :], gain[0:r, :], ACT.Exp).then_inc(exp_done, 1)
                for b in range(SB):
                    act.wait_ge(back_T, b + 1)
                    o = banks[4 + b % 4]
                    if softmax:
                        act.activation(back[:, b, D + H:], o[:, 256 + R - P - H:256 + R - P], ACT.Copy)
                    act.activation(back[:, b, 0:R], o[:, 0:R], ACT.Copy).then_inc(back_out, 1)

            @block.vector
            def _(dve):
                ch = Chain(dve, sem(tag + "chain"))
                dve.wait_ge(loaded, 64)
                if softmax:
                    m = last[:, :, D + H:]
                    dve.tensor_copy(mrep[:, :, 0:S].rearrange("p b (h c) -> p b h c", h=H), rep(m, 3, 16))\
                        .then_inc(rep_done, 1)
                    for x in range(3):
                        ins_ = dve.tensor_copy(
                            mrep[:, :, S + C * x:S + C * x + C].rearrange("p b (h c) -> p b h c", h=H), rep(m, 3, 8))
                    ins_.then_inc(rep_done, 1)
                    dve.tensor_copy(mrep[:, :, D:R], m).then_inc(rep_done, 1)
                ch.link(dve.tensor_tensor(go_on[:, :], edges[0][:, :], edges[1][:, :], ALU.is_equal))
                ch.link(dve.tensor_tensor(cut[:, :], edges[0][:, :], edges[2][:, :], ALU.is_equal))
                ch.wait()
                ch.link(dve.tensor_tensor(go_on[:, :], go_on[:, :], cut[:, :], ALU.mult))
                ch.wait()
                dve.wait_ge(turned_out, SB * len(parts) * (2 if softmax else 1))
                if not softmax:
                    for i, (c, r) in enumerate(parts):
                        dve.tensor_tensor_scan(val[i][0:r, :], go_on[0:r, :], val[i][0:r, :], 0.0, ALU.mult, ALU.add)\
                            .then_inc(scanned, 1)
                    return
                ch.link(dve.tensor_scalar(cut[:, :], go_on[:, :], -1.0, OFF, ALU.add, ALU.mult))
                ch.wait()
                for i, (c, r) in enumerate(parts):
                    if i >= 1:
                        dve.wait_ge(scanned, i)
                    top = mtop[i]
                    ch.link(dve.tensor_tensor_scan(top[0:r, :], cut[0:r, :], mx[i][0:r, :], -OFF, ALU.add, ALU.max))
                    ch.wait()
                    ch.link(dve.memset(keep[0:r, 0:1], 0.0))
                    ch.link(dve.tensor_tensor(keep[0:r, 1:NT], top[0:r, 0:NT - 1], top[0:r, 1:NT], ALU.subtract))
                    ch.wait()
                    dve.tensor_scalar(keep[0:r, :], keep[0:r, :], 0.0, None, ALU.min).then_inc(arg_done, 1)
                    dve.tensor_tensor(gain[0:r, :], mx[i][0:r, :], top[0:r, :], ALU.subtract).then_inc(arg_done, 1)
                    dve.wait_ge(exp_done, i + 1)
                    ch.link(dve.tensor_tensor(keep[0:r, :], keep[0:r, :], go_on[0:r, :], ALU.mult))
                    ch.link(dve.tensor_tensor(gain[0:r, :], gain[0:r, :], val[i][0:r, :], ALU.mult))
                    ch.wait()
                    dve.tensor_tensor_scan(val[i][0:r, :], keep[0:r, :], gain[0:r, :], 0.0, ALU.mult, ALU.add)\
                        .then_inc(scanned, 1)


def layer_norm(dve, ch, X, scr, stat, varred, rooted):
    ch.link(dve.tensor_reduce(stat[:, :], X[:, :, :], AX, ALU.add)); ch.wait()
    ch.link(dve.tensor_scalar(stat[:, :], stat[:, :], 1.0 / D, None, ALU.mult)); ch.wait()
    ch.link(dve.tensor_tensor(X[:, :, :], X[:, :, :], rep(stat[:, :], 2, D), ALU.subtract)); ch.wait()
    ch.link(dve.tensor_tensor(scr[:, :, :], X[:, :, :], X[:, :, :], ALU.mult)); ch.wait()
    ch.link(dve.tensor_reduce(stat[:, :], scr[:, :, :], AX, ALU.add)); ch.wait()
    dve.tensor_scalar(stat[:, :], stat[:, :], 1.0 / D, 1e-5, ALU.mult, ALU.add).then_inc(varred, 1)
    dve.wait_ge(rooted, 1)
    ch.link(dve.reciprocal(stat[:, :], stat[:, :])); ch.wait()


def gather_batches(pool, NB, row_idx, carry_idx, idx_s, agg, carry, ga, gc, copied, used, gathered):
    def batch(b):
        if not (isinstance(b, int) and b == 0):
            pool.wait_ge(gathered, b * (32 * NODE_BATCH))
            pool.wait_ge(used, b)
        cols = bass.ds(b * NODE_BATCH, NODE_BATCH)
        pool.tensor_copy(idx_s[0][:, :], row_idx[:, cols]).then_inc(copied, 1)
        pool.tensor_copy(idx_s[1][:, :], carry_idx[:, cols]).then_inc(copied, 1)
        pool.wait_ge(copied, b * 2 + 2)
        settle(pool)
        for j in range(NODE_BATCH):
            for i, (table, dst) in enumerate(((agg, ga), (carry, gc))):
                pool.indirect_dma_start(out=dst[:, j, :], out_offset=None, in_=table,
                                        in_offset=bass.IndirectOffsetOnAxis(ap=idx_s[i][:, j:j + 1], axis=0))\
                    .then_inc(gathered, 16)
    run_batches(pool, NB, batch)


def run_batches(eng, NB, batch):
    batch(0)
    if NB > 1:
        with eng.Fori(1, NB, 1) as b:
            batch(b)


def node_step_0(nc, ctx, sem, banks, wt, ident, ins, agg0, carry0, conv_table, X1, row_idx, carry_idx,
                has_row, has_carry, node_a, stat, stat2, chain, NK):
    NB = NK // NODE_BATCH
    U = NODE_BATCH
    R = D + H
    with ExitStack() as ph:
        def sb(name, shape, dt=F32):
            return ph.enter_context(nc.sbuf_tensor("n0_" + name, shape, dt))
        idx_s = [sb(f"idx{i}", [P, U], I32) for i in range(2)]
        ga, gc = sb("ga", [P, U, AGG0]), sb("gc", [P, U, AGG0])
        ea, ec, mt = sb("ea", [P, U, H]), sb("ec", [P, U, H]), sb("mt", [P, U, H])
        aggn = sb("aggn", [P, U, D])
        turned = [sb(f"turned{i}", [P, 2 * P]) for i in range(2)]
        xk = [sb(f"xk{i}", [P, D]) for i in range(2)]
        tab = [sb(f"tab{i}", [P, D]) for i in range(2)]
        scr = sb("scr", [P, NK, D])
        (loaded, copied, gathered, exp_arg, exped, normed, T, T_out, proj, added, varred, rooted, ready,
         xcopied, T2, T2_out, proj2, tabbed) = (sem("n0_" + n) for n in (
             "loaded", "copied", "gathered", "exp_arg", "exped", "normed", "T", "T_out", "proj", "added",
             "varred", "rooted", "ready", "xcopied", "T2", "T2_out", "proj2", "tabbed"))
        tab_out = [sem(f"n0_tab_out{i}") for i in range(2)]
        conv_v = conv_table.rearrange("(p k) d -> p k d", k=NK)

        def pairs(eng, body):
            for k in range(2):
                body(k, k)
            with eng.Fori(1, NK // 2, 1) as i:
                for u in range(2):
                    body(i * 2 + u, u)

        with nc.Block() as block:
            @block.sync
            def _(sp):
                sp.dma_start(X1[:, :, :], ins["x"].rearrange("(p k) d -> p k d", k=NK)).then_inc(loaded, 16)

                def store(k, q):
                    hold(sp, tabbed, k + 1)
                    sp.dma_start(conv_v[:, bass.ds(k, 1), :].squeeze(1), tab[q][:, :]).then_inc(tab_out[q], 16)
                pairs(sp, store)
                for q in range(2):
                    hold(sp, tab_out[q], 16 * (NK // 2))

            @block.gpsimd
            def _(pool):
                gather_batches(pool, NB, row_idx, carry_idx, idx_s, agg0, carry0, ga, gc, copied, normed, gathered)

            @block.vector
            def _(dve):
                own, den = sem("n0_chain"), sem("n0_den")
                dve.wait_ge(loaded, 16)
                LINKS = 7 + 4 * U + 3 + 2 * U

                def batch(b):
                    ch = Chain(dve, own)
                    ch.count = b * LINKS
                    cols = bass.ds(b * U, U)
                    dve.wait_ge(gathered, b * (32 * U) + 32 * U)
                    fa, fc = has_row[:, cols], has_carry[:, cols]
                    ch.link(dve.tensor_scalar(ea[:, :, 0], fa, -1.0, OFF, ALU.add, ALU.mult))
                    ch.link(dve.tensor_scalar(ec[:, :, 0], fc, -1.0, OFF, ALU.add, ALU.mult)); ch.wait()
                    ch.link(dve.tensor_tensor(ga[:, :, R:], ga[:, :, R:], rep(ea[:, :, 0], 2, H), ALU.add))
                    ch.link(dve.tensor_tensor(gc[:, :, R:], gc[:, :, R:], rep(ec[:, :, 0], 2, H), ALU.add)); ch.wait()
                    ch.link(dve.tensor_tensor(mt[:, :, :], ga[:, :, R:], gc[:, :, R:], ALU.max)); ch.wait()
                    dve.tensor_tensor(ea[:, :, :], ga[:, :, R:], mt[:, :, :], ALU.subtract).then_inc(exp_arg, 1)
                    dve.tensor_tensor(ec[:, :, :], gc[:, :, R:], mt[:, :, :], ALU.subtract).then_inc(exp_arg, 1)
                    dve.wait_ge(exped, b + 1)
                    ch.link(dve.tensor_tensor(ea[:, :, :], ea[:, :, :], rep(fa, 2, H), ALU.mult))
                    ch.link(dve.tensor_tensor(ec[:, :, :], ec[:, :, :], rep(fc, 2, H), ALU.mult)); ch.wait()

                    def by_head(buf, t, f):
                        ch.link(dve.tensor_tensor(buf[:, t, 0:S].rearrange("p (h c) -> p h c", h=H),
                                                  buf[:, t, 0:S].rearrange("p (h c) -> p h c", h=H),
                                                  rep(f[:, t, :], 2, 16), ALU.mult))
                        ch.link(dve.tensor_tensor(buf[:, t, S:D].rearrange("p (x h c) -> p x h c", h=H, c=8),
                                                  buf[:, t, S:D].rearrange("p (x h c) -> p x h c", h=H, c=8),
                                                  rep(rep(f[:, t, :], 2, 8), 1, 3), ALU.mult))
                    for t in range(U):
                        by_head(ga, t, ea)
                        by_head(gc, t, ec)
                    ch.link(dve.tensor_tensor(ga[:, :, D:R], ga[:, :, D:R], ea[:, :, :], ALU.mult))
                    ch.link(dve.tensor_tensor(gc[:, :, D:R], gc[:, :, D:R], ec[:, :, :], ALU.mult)); ch.wait()
                    ch.link(dve.tensor_tensor(ga[:, :, 0:R], ga[:, :, 0:R], gc[:, :, 0:R], ALU.add)); ch.wait()
                    dve.tensor_scalar(mt[:, :, :], ga[:, :, D:R], 1e-16, None, ALU.add).then_inc(den, 1)
                    dve.wait_ge(den, b * 2 + 1)
                    dve.reciprocal(mt[:, :, :], mt[:, :, :]).then_inc(den, 1)
                    dve.wait_ge(den, b * 2 + 2)
                    for t in range(U):
                        by_head(ga, t, mt)
                    ch.wait()
                    if not (isinstance(b, int) and b == 0):
                        dve.wait_ge(T, b * U)
                    dve.tensor_copy(aggn[:, :, :], ga[:, :, 0:D]).then_inc(normed, 1)
                    dve.wait_ge(normed, b + 1)
                    for t in range(U):
                        xt = X1[:, bass.ds(b * U + t, 1), :].squeeze(1)
                        dve.wait_ge(proj, b * U + (t + 1))
                        dve.scalar_tensor_tensor(out=xt, in0=xt, scalar=2.0, in1=banks[4 + t % 2][:, 0:D],
                                                 op0=ALU.mult, op1=ALU.add).then_inc(added, 1)
                run_batches(dve, NB, batch)
                dve.wait_ge(added, NK)
                ch = chain.on(dve)
                layer_norm(dve, ch, X1, scr, stat, varred, rooted)
                dve.tensor_tensor(X1[:, :, :], X1[:, :, :], rep(stat[:, :], 2, D), ALU.mult).then_inc(ready, 1)

                def body(k, q):
                    dve.wait_ge(proj2, k + 1)
                    if not (isinstance(k, int) and k < 2):
                        dve.wait_ge(tab_out[q], k * 8 - 8 * q)
                    a = node_a[:, bass.ds(k, 1)]
                    xt = X1[:, bass.ds(k, 1), :].squeeze(1)
                    o = banks[2 * q + 1]
                    dve.tensor_scalar(tab[q][:, :], o[:, 0:D], a, None, ALU.mult)
                    dve.scalar_tensor_tensor(out=xt, in0=o[:, D:2 * D], scalar=a, in1=xt, op0=ALU.mult,
                                             op1=ALU.add).then_inc(tabbed, 1)
                pairs(dve, body)

            @block.scalar
            def _(act):
                def batch(b):
                    act.wait_ge(exp_arg, b * 2 + 2)
                    act.activation(ea[:, :, :], ea[:, :, :], ACT.Exp)
                    act.activation(ec[:, :, :], ec[:, :, :], ACT.Exp).then_inc(exped, 1)
                    for t in range(U):
                        act.wait_ge(T, b * U + (t + 1))
                        if not (isinstance(b, int) and b * U + t < 2):
                            act.wait_ge(proj, b * U + (t - 1))
                        q = t % 2
                        act.activation(turned[q][:, 0:P], banks[t % 2][:, 0:P], ACT.Copy)
                        act.activation(turned[q][0:C, P:], banks[t % 2][0:C, P:2 * P], ACT.Copy).then_inc(T_out, 1)
                run_batches(act, NB, batch)
                act.wait_ge(varred, 1)
                act.activation(stat[:, :], stat[:, :], ACT.Sqrt).then_inc(rooted, 1)
                act.wait_ge(ready, 1)

                def body(k, q):
                    need(act, T2, k - 1)
                    act.activation(xk[q][:, :], X1[:, bass.ds(k, 1), :].squeeze(1), ACT.Copy).then_inc(xcopied, 1)
                    act.wait_ge(T2, k + 1)
                    need(act, proj2, k - 1)
                    act.activation(turned[q][:, 0:P], banks[2 * q][:, 0:P], ACT.Copy)
                    act.activation(turned[q][0:C, P:], banks[2 * q][0:C, P:2 * P], ACT.Copy).then_inc(T2_out, 1)
                pairs(act, body)

            @block.tensor
            def _(pe):
                def batch(b):
                    pe.wait_ge(normed, b + 1)

                    def turn(t):
                        if not (isinstance(b, int) and b * U + t < 2):
                            pe.wait_ge(T_out, b * U + (t - 1))
                        pe.transpose(banks[t % 2][:, 0:P], aggn[:, t, 0:P], ident[:, :])
                        pe.transpose(banks[t % 2][0:C, P:2 * P], aggn[:, t, P:D], ident[:, :]).then_inc(T, 1)
                    turn(0)
                    for t in range(U):
                        if t + 1 < U:
                            turn(t + 1)
                        pe.wait_ge(T_out, b * U + (t + 1))
                        if not (isinstance(b, int) and b * U + t < 2):
                            pe.wait_ge(added, b * U + (t - 1))
                        q = t % 2
                        pe.matmul(banks[4 + q][:, 0:D], turned[q][:, 0:P], wt("Wpa"), start=True, stop=False)
                        pe.matmul(banks[4 + q][:, 0:D], turned[q][0:C, P:], wt("Wpb"), start=False, stop=True)\
                            .then_inc(proj, 1)
                run_batches(pe, NB, batch)

                def body(k, q):
                    pe.wait_ge(xcopied, k + 1)
                    need(pe, T2_out, k - 1)
                    pe.transpose(banks[2 * q][:, 0:P], xk[q][:, 0:P], ident[:, :])
                    pe.transpose(banks[2 * q][0:C, P:2 * P], xk[q][:, P:D], ident[:, :]).then_inc(T2, 1)
                    pe.wait_ge(T2_out, k + 1)
                    need(pe, tabbed, k - 1)
                    pe.matmul(banks[2 * q + 1][:, 0:2 * D], turned[q][:, 0:P], wt("W3a"), start=True, stop=False)
                    pe.matmul(banks[2 * q + 1][:, 0:2 * D], turned[q][0:C, P:], wt("W3b"), start=False, stop=True)\
                        .then_inc(proj2, 1)
                pairs(pe, body)


def edge_loop_1(nc, ctx, sem, banks, wt, rbf_w, ins, rbf_parts, conv_table, agg1, NG):
    with ExitStack() as ph:
        def sb(name, shape, dt=F32):
            return ph.enter_context(nc.sbuf_tensor("m_" + name, shape, dt))
        pack = [sb(f"pack{i}", [P, 32], I32) for i in range(4)]
        idx = [p[:, 0:8] for p in pack]
        Y = [p[:, 8:32].bitcast(F32).rearrange("p (t c) -> p t c", t=TG) for p in pack]
        xs = [sb(f"xs{i}", [P, 512], BF16) for i in range(4)]
        drow = [sb(f"drow{i}", [P, 512], I32) for i in range(4)]
        gs = [sb(f"gs{i}", [P, TG, D]) for i in range(4)]
        tanh = sb("tanh", [S, 512])
        hid = [sb(f"hid{i}", [S, 512]) for i in range(2)]
        u = sb("u", [P, TG, P])
        tt = sb("tt", [P, TG, V])
        dot = sb("dot", [P, TG, C])
        w2y = sb("w2y", [P, TG, C])
        mid_ = [sb(f"mid{i}", [P, TG, 3 * P]) for i in range(4)]
        eq = [sb(f"eq{i}", [P, TG, P]) for i in range(4)]
        sums = [sb(f"sums{k}", [P, 512]) for k in range(3)]
        orow = [sb(f"orow{i}", [P, TG, AGG1]) for i in range(2)]
        small_in = [sem(f"l1_small_in{i}") for i in range(4)]
        big_in = [sem(f"l1_big_in{i}") for i in range(4)]
        gathered = [sem(f"l1_gathered{i}") for i in range(4)]
        out_done = [sem(f"l1_out_done{i}") for i in range(2)]
        (hid_mm, tanhed, hid_made, weights, mids, eq_made, summed, sums_out, mapped, row_out, u_made, scaled) = (
            sem("l1_" + n) for n in ("hid_mm", "tanhed", "hid_made", "weights", "mids", "eq_made", "summed",
                                     "sums_out", "mapped", "row_out", "u_made", "scaled"))
        agg_v = agg1.rearrange("(g j p) c -> g p j c", j=TG, p=P)
        xs_v = rbf_parts.rearrange("s c (g n) -> s g c n", n=512)
        drow_v = ins["dst_flat"].rearrange("(g n) -> g n", n=512)

        with nc.Block() as block:
            @block.sync
            def _(sp):
                def step(g, front, mid, late, tail):
                    if front:
                        s, n = g.slot, g.n
                        hold(sp, hid_mm, n - 3)
                        hold(sp, mids, n - 3)
                        hold(sp, scaled, n - 3)
                        hold(sp, eq_made, n - 3)
                        if not (isinstance(g.base, int) and g.base == 0):
                            hold(sp, gathered[s], g.base * 16)
                        at = bass.ds(n, 1)
                        sp.dma_start(pack[s][:, :], ins["edge_pack"][at].squeeze(0)).then_inc(small_in[s], 16)
                        c0 = 0
                        for part, copies in ((0, 3), (1, 3), (2, 2)):
                            sp.dma_start(xs[s][c0:c0 + 16 * copies, :], rep(xs_v[part, at], 0, copies).squeeze(1))\
                                .then_inc(big_in[s], 16)
                            c0 += 16 * copies
                        sp.dma_start(drow[s][:, :], drow_v[at].broadcast_to([P, 512])).then_inc(big_in[s], 16)
                steps(sp, NG, step, 4)

            @block.gpsimd
            def _(pool):
                def step(g, front, mid, late, tail):
                    if not front:
                        return
                    s = g.slot
                    need(pool, mids, g.n - 3)
                    pool.wait_ge(small_in[s], g.loads(16))
                    settle(pool)
                    for j in range(TG):
                        pool.indirect_dma_start(
                            out=gs[s][:, j, :], out_offset=None, in_=conv_table,
                            in_offset=bass.IndirectOffsetOnAxis(ap=idx[s][:, j:j + 1], axis=0)
                        ).then_inc(gathered[s], 16)
                steps(pool, NG, step, 4)

            @block.vector
            def _(dve):
                ch = Chain(dve, sem("l1_vector_chain"))

                def x3(ap, c0, w):
                    return ap[:, :, c0:c0 + 3 * w].rearrange("p t (x c) -> p t x c", c=w)

                def step(g, front, mid, late, tail):
                    if mid:
                        m = g.back(1)
                        s, y, e = m.slot, Y[m.slot], gs[m.slot]
                        dve.wait_ge(gathered[s], m.loads(64))
                        need(dve, mids, m.n)
                        a = ch.link(dve.tensor_tensor(x3(tt, 0, C), x3(e, S, C), rep(y[:, :, 1:4], 3, C), ALU.mult))
                        need(dve, summed, 3 * (m.n - 2))
                        ch.wait(a)
                        a = ch.link(dve.tensor_tensor(dot[:, :, :], tt[:, :, 0:C], tt[:, :, C:2 * C], ALU.add))
                        dve.wait_ge(big_in[s], m.loads(64))
                        need(dve, summed, 3 * (m.n - 2))
                        dve.tensor_tensor(eq[s][:, :, :], drow[s][:, :].rearrange("p (t e) -> p t e", t=TG),
                                          rep(idx[s][:, 4:8], 2, P), ALU.is_equal).then_inc(eq_made, 1)
                    if front:
                        n = g.n
                        dve.wait_ge(tanhed, n + 1)
                        need(dve, weights, 2 * (n - 1))
                        dve.scalar_tensor_tensor(out=hid[g.slot % 2][:, :], in0=tanh[:, :], scalar=1.0,
                                                 in1=banks[0][0:S, :], op0=ALU.add, op1=ALU.mult)\
                            .then_inc(hid_made, 1)
                    if mid:
                        need(dve, scaled, m.n)
                        for b in range(2):
                            dve.wait_ge(weights, 2 * m.n + (b + 1))
                            o = banks[1 + b][:, 0:384].rearrange("p (t c) -> p t c", t=2)
                            ts2 = slice(2 * b, 2 * b + 2)
                            dve.tensor_tensor(
                                u[:, ts2, :].rearrange("p t (r c) -> p t r c", c=S),
                                o[:, :, 0:P].rearrange("p t (r c) -> p t r c", c=S), rep(e[:, ts2, 0:S], 2, 2),
                                ALU.mult).then_inc(u_made, 1)
                            bw = ch.link(dve.tensor_tensor(w2y[:, ts2, :], o[:, :, 128:160], rep(y[:, ts2, 0], 2, C),
                                                           ALU.mult))
                            if b == 0:
                                ch.wait(a)
                                a = ch.link(dve.tensor_tensor(dot[:, :, :], dot[:, :, :], tt[:, :, 2 * C:V], ALU.add))
                                ch.wait(a)
                            ch.link(dve.tensor_tensor(mid_[s][:, ts2, S:V], o[:, :, 160:192], dot[:, ts2, :], ALU.mult))
                        ch.wait(bw)
                        ch.link(dve.tensor_tensor(x3(mid_[s], V, C), x3(e, S, C), rep(w2y[:, :, :], 2, 3), ALU.mult))
                        dve.wait_ge(u_made, 2 * (m.n + 1))
                        dve.tensor_tensor(x3(mid_[s], 2 * V, S), rep(u[:, :, S:P], 2, 3), rep(y[:, :, 1:4], 3, S),
                                          ALU.mult).then_inc(mids, 1)
                steps(dve, NG, step, 4, ch)

            @block.scalar
            def _(act):
                def step(g, front, mid, late, tail):
                    n = g.n
                    if front:
                        act.wait_ge(hid_mm, n + 1)
                        need(act, hid_made, n)
                        act.activation(tanh[:, :], banks[0][0:S, :], ACT.Tanh, scale=0.125).then_inc(tanhed, 1)
                    if tail:
                        t = g.back(3)
                        q = t.slot % 2
                        for k in range(3):
                            act.wait_ge(summed, 3 * t.n + (k + 1))
                            need(act, mapped, 2 * t.n)
                            act.activation(sums[k][:, :], banks[3 + k][:, :], ACT.Copy).then_inc(sums_out, 1)
                        if not (isinstance(t.base, int) and t.base == 0 and t.slot < 2):
                            act.wait_ge(out_done[q], t.base * 8 + 16 * (t.slot // 2))
                        for b in range(2):
                            act.wait_ge(mapped, 2 * t.n + (b + 1))
                            act.activation(orow[q][:, 2 * b:2 * b + 2, :],
                                           banks[6 + b][:, 0:2 * AGG1].rearrange("p (t c) -> p t c", t=2), ACT.Copy)\
                                .then_inc(row_out, 1)
                        act.wait_ge(row_out, 2 * (t.n + 1))
                        act.dma_start(agg_v[bass.ds(t.n, 1)].squeeze(0), orow[q][:, :, :])\
                            .then_inc(out_done[q], 16)
                    if mid:
                        m = g.back(1)
                        act.wait_ge(u_made, 2 * (m.n + 1))
                        need(act, summed, 3 * (m.n - 2))
                        for j in range(TG):
                            last = act.activation(mid_[m.slot][:, j, 0:S], u[:, j, 0:S], ACT.Copy,
                                                  scale=Y[m.slot][:, j, 0:1])
                        last.then_inc(scaled, 1)
                steps(act, NG, step, 4)
                for i in range(2):
                    act.wait_ge(out_done[i], 16 * (NG // 2))

            @block.tensor
            def _(pe):
                def step(g, front, mid, late, tail):
                    n = g.n
                    if front:
                        pe.wait_ge(big_in[g.slot], g.loads(64))
                        need(pe, hid_made, n)
                        pe.matmul(banks[0][0:S, :], rbf_w[:, 352:416], xs[g.slot][:, :], start=True, stop=True)\
                            .then_inc(hid_mm, 1)
                    if tail:
                        t = g.back(3)
                        pe.wait_ge(mids, t.n + 1)
                        pe.wait_ge(scaled, t.n + 1)
                        pe.wait_ge(eq_made, t.n + 1)
                        for k in range(3):
                            need(pe, sums_out, 3 * t.n - 2 + k)
                            for j in range(TG):
                                mm = pe.matmul(banks[3 + k][:, P * j:P * j + P], mid_[t.slot][:, j, P * k:P * k + P],
                                               eq[t.slot][:, j, :], start=True, stop=True)
                            mm.then_inc(summed, 1)
                    if mid:
                        m = g.back(1)
                        pe.wait_ge(hid_made, m.n + 1)
                        need(pe, mids, m.n)
                        for j in range(TG):
                            c = 192 * (j % 2)
                            mm = pe.matmul(banks[1 + j // 2][:, c:c + 192], hid[m.slot % 2][:, P * j:P * j + P],
                                           wt("Wfc2"), start=True, stop=True)
                            if j % 2:
                                mm.then_inc(weights, 1)
                    if tail:
                        pe.wait_ge(sums_out, 3 * t.n + 3)
                        for j in range(TG):
                            if j % 2 == 0:
                                need(pe, row_out, 2 * t.n - 1 + j // 2)
                            c, e = AGG1 * (j % 2), slice(P * j, P * j + P)
                            o = banks[6 + j // 2]
                            pe.matmul(o[:, c:c + 161], sums[0][:, e], wt("W4a"), start=True, stop=False)
                            pe.matmul(o[:, c + 65:c + 161], sums[1][:, e], wt("W4b"), start=False, stop=False)
                            mm = pe.matmul(o[:, c + 97:c + 161], sums[2][:, e], wt("W4c"), start=False, stop=True)
                            if j % 2:
                                mm.then_inc(mapped, 1)
                steps(pe, NG, step, 4)


def node_step_1(nc, ctx, sem, banks, agg1, carry1, out, X1, row_idx, carry_idx, has_row, has_carry, node_a,
                stat, degree, chain, NK):
    NB, U = NK // NODE_BATCH, NODE_BATCH
    with ExitStack() as ph:
        def sb(name, shape, dt=F32):
            return ph.enter_context(nc.sbuf_tensor("n1_" + name, shape, dt))
        idx_s = [sb(f"idx{i}", [P, U], I32) for i in range(2)]
        ga, gc = sb("ga", [P, U, AGG1]), sb("gc", [P, U, AGG1])
        cnt = sb("cnt", [P, U])
        scr = sb("scr", [P, NK, D])
        copied, used, gathered, varred, rooted, done, stored = (
            sem("n1_" + n) for n in ("copied", "used", "gathered", "varred", "rooted", "done", "stored"))
        with nc.Block() as block:
            @block.sync
            def _(sp):
                hold(sp, done, 1)
                sp.dma_start(out.rearrange("(p k) d -> p k d", k=NK), X1[:, :, :]).then_inc(stored, 16)
                hold(sp, stored, 16)

            @block.gpsimd
            def _(pool):
                gather_batches(pool, NB, row_idx, carry_idx, idx_s, agg1, carry1, ga, gc, copied, used, gathered)

            @block.scalar
            def _(act):
                act.wait_ge(varred, 1)
                act.activation(stat[:, :], stat[:, :], ACT.Sqrt).then_inc(rooted, 1)

            @block.vector
            def _(dve):
                own = sem("n1_chain")
                LINKS = 10

                def batch(b):
                    ch = Chain(dve, own)
                    ch.count = b * LINKS
                    cols = bass.ds(b * U, U)
                    dve.wait_ge(gathered, b * (32 * U) + 32 * U)
                    ch.link(dve.tensor_tensor(ga[:, :, :], ga[:, :, :], rep(has_row[:, cols], 2, AGG1), ALU.mult))
                    ch.link(dve.tensor_tensor(gc[:, :, :], gc[:, :, :], rep(has_carry[:, cols], 2, AGG1), ALU.mult))
                    ch.wait()
                    ch.link(dve.tensor_tensor(ga[:, :, :], ga[:, :, :], gc[:, :, :], ALU.add)); ch.wait()
                    ch.link(dve.tensor_scalar(cnt[:, :], degree[:, cols], 1.0, None, ALU.max)); ch.wait()
                    ch.link(dve.reciprocal(cnt[:, :], cnt[:, :])); ch.wait()
                    ch.link(dve.tensor_tensor(cnt[:, :], cnt[:, :], node_a[:, cols], ALU.mult)); ch.wait()
                    ch.link(dve.tensor_tensor(cnt[:, :], cnt[:, :], cnt[:, :], ALU.mult)); ch.wait()
                    ch.link(dve.tensor_tensor(cnt[:, :], cnt[:, :], ga[:, :, 0], ALU.mult)); ch.wait()
                    ch.link(dve.tensor_tensor(ga[:, :, 1:161], ga[:, :, 1:161], rep(cnt[:, :], 2, D), ALU.mult))
                    ch.wait()
                    xs, xv = X1[:, cols, 0:S], X1[:, cols, S:D].rearrange("p k (c x) -> p k x c", x=3)
                    ch.link(dve.tensor_tensor(xs, xs, ga[:, :, 1:65], ALU.add))
                    ch.wait()
                    dve.tensor_tensor(xv, xv, ga[:, :, 65:161].rearrange("p k (x c) -> p k x c", x=3),
                                      ALU.add).then_inc(used, 1)
                run_batches(dve, NB, batch)
                dve.wait_ge(used, NB)
                ch = chain.on(dve)
                layer_norm(dve, ch, X1, scr, stat, varred, rooted)
                dve.tensor_tensor(X1[:, :, :], X1[:, :, :], rep(stat[:, :], 2, D), ALU.mult).then_inc(done, 1)


def kernel(**inputs):
    import numpy as np
    import concourse.bacc as bacc
    from concourse.bass_utils import run_bass_kernel_spmd

    g = {k: np.ascontiguousarray(v) for k, v in inputs.items()}
    f32 = np.float32
    N, E = g["x"].shape[0], g["src"].shape[0]
    SB = -(-E // (P * P))
    NT = SB * P
    EP, NG = NT * P, NT // TG
    NK = 2 * NODE_BATCH * -(-(N + 1) // (2 * NODE_BATCH * P))

    def padded(a, n, fill=0):
        out = np.full((n,) + a.shape[1:], fill, a.dtype)
        out[:a.shape[0]] = a
        return out

    src, dst = padded(g["src"], EP), padded(g["dst"], EP, N)

    def columns(a):
        return a.reshape(NG, TG, P, -1).transpose(0, 2, 1, 3)
    y = padded(g["edge_attr_4"], EP)
    before = np.concatenate([np.full(1, -1, dst.dtype), dst[:-1]])
    arrays = {
        "x": padded(g["x"], NK * P),
        "edge_pack": np.concatenate([columns(src)[..., 0], columns(dst)[..., 0], np.ascontiguousarray(
            columns(y[:, [0, 1, 2, 3, 1, 2]]).reshape(NG, P, TG * 6)).view(src.dtype)], axis=2),
        "rbf_t": padded(g["edge_attr_16"], EP).T,
        "dst_flat": dst,
        "dst_rows": np.concatenate([before.reshape(NT, P)[:, :1], dst.reshape(NT, P)], axis=1),
        "first": dst.reshape(NT, P)[:, 0], "last": dst.reshape(NT, P)[:, -1],
        "before": before.reshape(NT, P)[:, 0], "sup": dst.reshape(SB, P * P)[:, -1],
        "node_a": padded(g["node_vec1"], NK * P).reshape(P, NK),
    }

    L0 = {k[7:]: v for k, v in g.items() if k.startswith("L0_gnn_")}
    L1 = {k[7:]: v for k, v in g.items() if k.startswith("L1_gnn_")}
    c3 = 3 * np.arange(C)

    def blocks(w):
        o = np.zeros((V, V), f32)
        for x in range(3):
            o[C * x:C * x + C, C * x:C * x + C] = w
        return o

    def node_rows(w, x_major_cols=True):
        o = np.zeros((V, V), f32)
        for x in range(3):
            o[np.ix_(c3 + x, C * x + np.arange(C) if x_major_cols else c3 + x)] = w
        return o
    wr = L0["W_rbf"]
    ss, sv, vs, vv0, vv1 = wr[:, :64], wr[:, 64:128], wr[:, 128:160], wr[:, 160:192], wr[:, 192:224]
    arrays["rbf_w"] = np.concatenate([sv, ss, vs, vs, vs, vv0, vv1, vv1, vv1, L1["Wfc1"]], axis=1)
    z = lambda r, c: np.zeros((r, c), f32)
    Wal, Wsv, Wvv = L0["W_alpha"], L0["Ws_val"], L0["Wv_val"]
    Wsl, Wvl = L0["Ws_vlin"], L0["Wv_vlin"]
    parts = {}
    parts["WsSD"] = np.concatenate([L0["Ws_src"], L0["Ws_dst"]], axis=1)
    parts["WvSD"] = np.concatenate([node_rows(L0["Wv_src"]), node_rows(L0["Wv_dst"])], axis=1)
    parts["gs"], parts["bs"] = L0["gamma_s"][:, None], L0["beta_s"][:, None]
    parts["gv"] = np.repeat(L0["gamma_v"], 3)[:, None]
    parts["WvT1"], parts["WvT2"] = z(64, 128), z(64, 128)
    parts["WvT1"][:, 64:] = Wsv.T[:, :64]
    parts["WvT2"][:, 96:] = Wsv.T[:, 64:]
    parts["Wg"] = L0["Wg"]
    parts["W1a"] = z(128, 192)
    parts["W1a"][:64, 160:] = Wvv[:64]
    parts["W1a"][64:, :64], parts["W1a"][64:, 96:160] = Wsv[:64], Wal[:64]
    parts["W1b"] = z(128, 288)
    parts["W1b"][:96, 192:] = blocks(Wvv[64:96])
    parts["W1b"][96:, :64], parts["W1b"][96:, 96:160] = Wsv[64:], Wal[64:]
    parts["W1c"] = blocks(Wvv[96:])
    parts["W2a"] = z(128, 96)
    parts["W2a"][:64, 64:] = Wvl[:64]
    parts["W2a"][64:, :64] = Wsl[:64]
    parts["W2b"] = z(128, 192)
    parts["W2b"][:96, 96:] = blocks(Wvl[64:96])
    parts["W2b"][96:, :64] = Wsl[64:]
    parts["W2c"] = blocks(Wvl[96:])
    parts["r2"] = z(128, 3)
    parts["r2"][:, 0] = np.concatenate([L0["w2_sv"], L0["w2_ss"]])
    parts["r2"][:, 1] = np.concatenate([L0["w2_vs"]] * 3 + [L0["w2_vv0"]])
    parts["r2"][:96, 2] = np.concatenate([L0["w2_vv1"]] * 3)
    parts["adot"] = np.broadcast_to(L0["alpha_dot"].reshape(1, 64), (P, 64))
    po = z(160, 160)
    po[:64, :64] = L0["Wps"]
    for x in range(3):
        po[np.ix_(64 + C * x + np.arange(C), 64 + c3 + x)] = L0["Wpv"]
    parts["Wpa"], parts["Wpb"] = po[:P], po[P:]
    w3 = z(160, 320)
    w3[:64, :64], w3[:64, 160:224] = L1["Wl1_0"], L1["Wsc0"]
    w3[64:, 64:160], w3[64:, 224:] = node_rows(L1["Wl1_1"]), node_rows(L1["Wsc1"], False)
    parts["W3a"], parts["W3b"] = w3[:P], w3[P:]
    parts["Wfc2"] = L1["Wfc2"]
    w4 = z(384, 161)
    w4[:96, 0:1], w4[:96, 1:65] = L1["Wa"], L1["Wl2_s"]
    for x in range(3):
        w4[96 + C * x:96 + C * x + C, 65 + C * x:97 + C * x] = L1["Wl2_v"][64:]
        w4[192 + S * x:192 + S * x + S, 65 + C * x:97 + C * x] = L1["Wl2_v"][:64]
    parts["W4a"], parts["W4b"], parts["W4c"] = w4[:128], w4[128:256, 65:], w4[256:, 97:]
    at, cols = {}, 0
    for n, w in parts.items():
        at[n] = (cols, w.shape[0], w.shape[1])
        cols += w.shape[1]
    at["_width"] = cols
    arrays["weights"] = z(P, cols)
    for n, w in parts.items():
        arrays["weights"][:w.shape[0], at[n][0]:at[n][0] + w.shape[1]] = w

    nc = bacc.Bacc("TRN2", target_bir_lowering=False, num_devices=1)
    arrays = {"in_" + k: np.ascontiguousarray(v) for k, v in arrays.items()}
    ins = {k[3:]: nc.dram_tensor(k, v.shape, mybir.dt.from_np(v.dtype), kind="ExternalInput").ap()
           for k, v in arrays.items()}
    out = nc.dram_tensor("out_nodes", (NK * P, D), F32, kind="ExternalOutput").ap()
    build(nc, ins, out, at, NT, NK)
    r = run_bass_kernel_spmd(nc, [arrays], core_ids=[0])
    return r.results[0]["out_nodes"][:N]
```

```python
import concourse.bass as bass
from concourse import mybir
from contextlib import ExitStack

P = 128
TG = 4
S, V, C = 64, 96, 32
D = S + V
H = 4
AGG0 = D + 2 * H
AGG1 = D + 1
OFF = 3.0e38
NODE_BATCH = 7
F32, BF16, I32 = mybir.dt.float32, mybir.dt.bfloat16, mybir.dt.int32
ALU, ACT, AX = mybir.AluOpType, mybir.ActivationFunctionType, mybir.AxisListType.X


def rep(ap, axis, n):
    ap = ap.unsqueeze(axis)
    shape = list(ap.shape)
    shape[axis] = n
    return ap.broadcast_to(shape)


def need(eng, sem, value):
    if isinstance(value, int) and value <= 0:
        return
    eng.wait_ge(sem, value)


def settle(eng):
    eng.nop(nofuse=True)


def hold(sp, sem, value):
    need(sp, sem, value)
    if not isinstance(value, int):
        settle(sp)


class Chain:

    def __init__(self, eng, sem):
        self.eng, self.sem, self.count = eng, sem, 0

    def link(self, ins):
        ins.then_inc(self.sem, 1)
        self.count = self.count + 1
        return self.count

    def on(self, eng):
        self.eng = eng
        return self

    def wait(self, mark=None):
        self.eng.wait_ge(self.sem, self.count if mark is None else mark)


class Group:

    def __init__(self, base, slot):
        self.base, self.slot, self.n = base, slot, base + slot

    def back(self, k):
        if self.slot >= k:
            return Group(self.base, self.slot - k)
        return Group(self.base - 4, self.slot - k + 4)

    def loads(self, unit):
        return self.base * (unit // 4) + unit


def steps(eng, groups, step, stages=3, ch=None):
    for n in range(4):
        before = ch.count if ch else 0
        step(Group(0, n), *(n >= k for k in range(stages)))
    entry = ch.count if ch else 0
    full = entry - before
    with eng.Fori(1, groups // 4, 1) as i:
        if ch:
            ch.count = i * (4 * full) + (entry - 4 * full)
        for u in range(4):
            step(Group(i * 4, u), *(True for _ in range(stages)))
    if ch:
        ch.count = entry + (groups - 4) * full
    for u in range(stages - 1):
        step(Group(groups, u), *(k > u for k in range(stages)))


class Batch:

    def __init__(self, n, q):
        self.n, self.q = n, q
        self.cols = bass.ds(n * NODE_BATCH, NODE_BATCH)

    def tiles(self, t, count=1):
        return bass.ds(self.n * NODE_BATCH + t, count)

    def of_parity(self, unit):
        return (self.n - self.q) * (unit // 2) + unit


def batches(eng, NB, step):
    for n in range(min(4, NB)):
        step(*(Batch(n - k, (n - k) % 2) if n >= k else None for k in range(3)))
    if NB > 4:
        with eng.Fori(2, NB // 2, 1) as i:
            for u in range(2):
                n = i * 2 + u
                step(Batch(n, u), Batch(n - 1, 1 - u), Batch(n - 2, u))
    step(None, Batch(NB - 1, 1), Batch(NB - 2, 0))
    step(None, None, Batch(NB - 1, 1))


def build(nc, ins, out, weights_at, NT, NK):
    NG = NT // TG
    SB = NT // P
    EP = NT * P
    NB = NK // NODE_BATCH
    ctx = ExitStack()
    with ctx:
        def dram(name, shape, dt=F32):
            return nc.dram_tensor(name, shape, dt, kind="Internal").ap()

        def sem(name):
            return ctx.enter_context(nc.semaphore(name))

        def sb(name, shape, dt=F32, where=ctx):
            return where.enter_context(nc.sbuf_tensor(name, shape, dt))

        rbf_parts = dram("rbf_parts", (3, 16, EP), BF16)
        edge_cut = dram("edge_cut", (NG, TG * H, P + 1))
        src_table = dram("src_table", (NK * P, D))
        dst_table = dram("dst_table", (NK * P, D))
        conv_table = dram("conv_table", (NK * P, D))
        agg0 = dram("agg0", (EP, AGG0))
        agg1 = dram("agg1", (EP, AGG1))
        carry0 = dram("carry0", (NT + 1, AGG0))
        carry1 = dram("carry1", (NT + 1, AGG1))

        banks = [ctx.enter_context(nc.psum_tensor(f"bank{i}", [P, 512], F32)) for i in range(8)]
        W = sb("W", [P, weights_at["_width"]])

        def wt(name, rows=None, c0=0, c1=None):
            at, r, c = weights_at[name]
            return W[0:r, at + c0:at + (c if c1 is None else c1)]

        ident = sb("ident", [P, P])
        rbf_w = sb("rbf_w", [P, 416], BF16)
        row_idx = sb("row_idx", [P, NK], I32)
        carry_idx = sb("carry_idx", [P, NK], I32)
        has_row = sb("has_row", [P, NK])
        has_carry = sb("has_carry", [P, NK])
        node_a = sb("node_a", [P, NK])
        degree = sb("degree", [P, NK])
        before_run = sb("before_run", [P, 1])
        chain = Chain(None, sem("vector_chain"))

        with ExitStack() as ph:
            wload, cut_load = sem("wload"), sem("cut_load")
            split_load = [sem(f"split_load{i}") for i in range(2)]
            stored, eye, prod, made, dma_w = (sem("prep_stored"), sem("eye"), sem("gate_product"),
                                              sem("prep_vector"), sem("prep_moved"))
            hi_done, mid_done, rest_done, low_done = (sem("split_hi"), sem("split_mid"), sem("split_rest"),
                                                      sem("split_low"))
            wr = sb("wr", [P, 416], F32, ph)
            wparts = [sb(f"wpart{i}", [P, 416], BF16, ph) for i in range(3)]
            xin = [sb(f"xin{i}", [P, 2048], F32, ph) for i in range(2)]
            xrest = [sb(f"xrest{i}", [P, 2048], F32, ph) for i in range(2)]
            xp = [[sb(f"xp{i}_{q}", [P, 2048], BF16, ph) for i in range(3)] for q in range(2)]
            dsts = sb("dsts", [P, SB, P + 1], I32, ph)
            cut = sb("cut", [P, SB, P + 1], F32, ph)
            zrow = sb("zrow", [P, AGG0], F32, ph)
            rbf_v = ins["rbf_t"].rearrange("c (h n) -> (c h) n", h=8)
            parts_v = [rbf_parts[i].rearrange("c (h n) -> (c h) n", h=8) for i in range(3)]

            with nc.Block() as block:
                @block.sync
                def _(sp):
                    sp.dma_start(W[:, :], ins["weights"]).then_inc(wload, 16)
                    for c in range(8):
                        sp.dma_start(wr[16 * c:16 * c + 16, :], ins["rbf_w"]).then_inc(wload, 16)
                    sp.dma_start(dsts[:, :, :], ins["dst_rows"].rearrange("(b t) e -> t b e", t=P))\
                        .then_inc(cut_load, 16)
                    sp.dma_start(node_a[:, :], ins["node_a"]).then_inc(wload, 16)
                    hold(sp, made, 3)
                    for c, wp in enumerate((0, 1, 2, 0, 1, 2, 0, 1)):
                        sp.dma_start(rbf_w[16 * c:16 * c + 16, :], wparts[wp][16 * c:16 * c + 16, :])\
                            .then_inc(dma_w, 16)
                    hold(sp, dma_w, 128)
                    for b in range(SB + 1):
                        if b < SB:
                            hold(sp, stored, 48 * (b - 1))
                            sp.dma_start(xin[b % 2][:, :], rbf_v[:, 2048 * b:2048 * b + 2048])\
                                .then_inc(split_load[b % 2], 16)
                        if b >= 1:
                            c = slice(2048 * b - 2048, 2048 * b)
                            for i, part_done in enumerate((hi_done, mid_done, low_done)):
                                hold(sp, part_done, b)
                                sp.dma_start(parts_v[i][:, c], xp[(b - 1) % 2][i][:, :]).then_inc(stored, 16)
                    hold(sp, stored, 48 * SB)
                    hold(sp, made, 6)
                    for h in range(H):
                        sp.dma_start(edge_cut.rearrange("g (j h) e -> h (g j) e", h=H)[h]
                                     .rearrange("(b t) e -> t b e", t=P), cut[:, :, :]).then_inc(dma_w, 16)
                    sp.dma_start(carry0[0:1, :], zrow[0:1, :]).then_inc(dma_w, 16)
                    sp.dma_start(carry1[0:1, :], zrow[0:1, 0:AGG1]).then_inc(dma_w, 16)
                    hold(sp, dma_w, 128 + 16 * (H + 2))

                @block.gpsimd
                def _(pool):
                    pool.memset(ident[:, :], 0.0).then_inc(eye, 1)
                    pool.wait_ge(eye, 1)
                    pool.affine_select(out=ident[:, :], in_=ident[:, :], compare_op=ALU.not_equal, fill=1.0,
                                       base=0, pattern=[[-1, P]], channel_multiplier=1).then_inc(eye, 1)

                @block.scalar
                def _(act):
                    for b in range(SB + 1):
                        if b < SB:
                            act.wait_ge(split_load[b % 2], 16 * (b // 2) + 16)
                            need(act, stored, 48 * (b - 1))
                            act.activation(xp[b % 2][0][:, :], xin[b % 2][:, :], ACT.Copy).then_inc(hi_done, 1)
                        if b >= 1:
                            act.wait_ge(rest_done, b)
                            act.activation(xp[(b - 1) % 2][1][:, :], xrest[(b - 1) % 2][:, :], ACT.Copy)\
                                .then_inc(mid_done, 1)

                @block.vector
                def _(dve):
                    ch = chain.on(dve)
                    dve.wait_ge(wload, 160)
                    dve.tensor_copy(wparts[0][:, :], wr[:, :]).then_inc(made, 1)
                    dve.wait_ge(made, 1)
                    ch.link(dve.tensor_tensor(wr[:, :], wr[:, :], wparts[0][:, :], ALU.subtract))
                    ch.wait()
                    dve.tensor_copy(wparts[1][:, :], wr[:, :]).then_inc(made, 1)
                    dve.wait_ge(made, 2)
                    dve.tensor_tensor(wparts[2][:, :], wr[:, :], wparts[1][:, :], ALU.subtract).then_inc(made, 1)
                    dve.wait_ge(cut_load, 16)
                    ch.link(dve.tensor_tensor(cut[:, :, 1:P], dsts[:, :, 2:P + 1], dsts[:, :, 1:P], ALU.not_equal))
                    ch.wait()
                    dve.tensor_scalar(cut[:, :, 1:P], cut[:, :, 1:P], -OFF, None, ALU.mult).then_inc(made, 1)
                    dve.memset(cut[:, :, 0:P + 1:P], -OFF).then_inc(made, 1)
                    dve.memset(zrow[:, :], 0.0).then_inc(made, 1)
                    r3, r2 = 3.0 ** -0.5, 2.0 ** -0.5
                    dve.wait_ge(prod, 1)
                    ch.link(dve.tensor_copy(wt("W1a", c0=64, c1=96)[64:128], banks[0][64:128, 0:C]))
                    ch.link(dve.tensor_copy(wt("W1b", c0=64, c1=96)[96:128], banks[1][96:128, 0:C]))
                    ch.wait()
                    ch.link(dve.tensor_scalar(wt("W1b")[96:128], wt("W1b")[96:128], r3, None, ALU.mult))
                    ch.link(dve.tensor_scalar(wt("W1c"), wt("W1c"), r2, None, ALU.mult))
                    for k, (n, f) in enumerate((("W2a", 0.5), ("W2b", 0.5), ("W2c", 0.5 * r2))):
                        r = weights_at[n][1]
                        ch.link(dve.tensor_scalar(wt(n), wt(n), wt("r2")[0:r, k:k + 1], f, ALU.mult, ALU.mult))
                    ch.wait()
                    ch.link(dve.tensor_scalar(wt("W2b")[96:128], wt("W2b")[96:128], r3, None, ALU.mult))
                    ch.link(dve.tensor_scalar(wt("W3a")[0:64], wt("W3a")[0:64], 0.125, None, ALU.mult))
                    ch.link(dve.tensor_scalar(wt("W3a")[64:128], wt("W3a")[64:128], 32.0 ** -0.5, None, ALU.mult))
                    ch.link(dve.tensor_scalar(wt("W3b"), wt("W3b"), 32.0 ** -0.5, None, ALU.mult))
                    ch.link(dve.tensor_scalar(wt("Wfc2"), wt("Wfc2"), 0.125 * 0.125, None, ALU.mult))
                    for n in ("W4a", "W4b", "W4c"):
                        ch.link(dve.tensor_scalar(wt(n), wt(n), 96.0 ** -0.5, None, ALU.mult))
                    ch.wait()
                    ch.link(dve.tensor_scalar(wt("W4a")[64:96], wt("W4a")[64:96], r3, None, ALU.mult))
                    ch.wait()
                    for b in range(SB + 1):
                        if b < SB:
                            dve.wait_ge(hi_done, b + 1)
                            need(dve, low_done, b - 1)
                            dve.tensor_tensor(xrest[b % 2][:, :], xin[b % 2][:, :], xp[b % 2][0][:, :], ALU.subtract)\
                                .then_inc(rest_done, 1)
                        if b >= 1:
                            q = (b - 1) % 2
                            dve.wait_ge(mid_done, b)
                            dve.tensor_tensor(xp[q][2][:, :], xrest[q][:, :], xp[q][1][:, :], ALU.subtract)\
                                .then_inc(low_done, 1)

                @block.tensor
                def _(pe):
                    pe.wait_ge(wload, 160)
                    pe.matmul(banks[0][:, 0:C], wt("WvT1"), wt("Wg"), start=True, stop=True)
                    pe.matmul(banks[1][:, 0:C], wt("WvT2"), wt("Wg"), start=True, stop=True).then_inc(prod, 1)

        with ExitStack() as ph:
            U = NODE_BATCH
            X = sb("X", [P, NK, D], F32, ph)
            scr = sb("scr", [P, U, V], F32, ph)
            below = sb("below", [P, NK, SB], F32, ph)
            nf = sb("nf", [P, NK], F32, ph)
            n_int = sb("n_int", [P, NK], I32, ph)
            level = sb("level", [P, NK], F32, ph)
            found = sb("found", [P, NK], F32, ph)
            level_i = sb("level_i", [P, NK], I32, ph)
            idx_s = [sb(f"idx_s{i}", [P, U], I32, ph) for i in range(2)]
            sup = sb("sup", [P, SB], I32, ph)
            rows = [sb(f"rows{i}", [P, U, P + 1], I32, ph) for i in range(2)]
            cmp = sb("cmp", [P, U, P], F32, ph)
            stat_s, stat_v = sb("stat_s", [P, U], F32, ph), sb("stat_v", [P, U], F32, ph)
            xn = [sb(f"node_xn{i}", [P, U, D], F32, ph) for i in range(2)]
            xts = [sb(f"xts{i}", [S, P], F32, ph) for i in range(2)]
            xtv = [sb(f"xtv{i}", [V, P], F32, ph) for i in range(2)]
            tab = [sb(f"ntab{i}", [P, U, 2 * D], F32, ph) for i in range(2)]
            xload, normed, xT, evacT, projd, tabbed, rooted, varred = (
                sem("xload"), sem("node_normed"), sem("node_T"), sem("node_T_out"),
                sem("node_projected"), sem("node_tab"), sem("node_rooted"), sem("node_var"))
            tab_out = [sem(f"node_tab_stored{i}") for i in range(2)]
            iota_done, lvl_idx, idx_copied, batch_done, ends_made, before_in = (
                sem("iota"), sem("level_index"), sem("index_copied"), sem("batch_compared"), sem("ends_made"),
                sem("before_run_in"))
            rows_in = [sem(f"rows_in{i}") for i in range(2)]
            src_v = src_table.rearrange("(p k) d -> p k d", k=NK)
            dst_v = dst_table.rearrange("(p k) d -> p k d", k=NK)
            last_rows = ins["last"].rearrange("(b t) -> b t", t=P)

            with nc.Block() as block:
                @block.sync
                def _(sp):
                    sp.dma_start(sup[:, :], ins["sup"].partition_broadcast(P)).then_inc(xload, 16)
                    sp.dma_start(X[:, :, :], ins["x"].rearrange("(p k) d -> p k d", k=NK)).then_inc(xload, 16)

                    def step(_, a, __):
                        if a is not None:
                            hold(sp, tabbed, a.n * U + U)
                            sp.dma_start(src_v[:, a.cols, :], tab[a.q][:, :, 0:D]).then_inc(tab_out[a.q], 16)
                            sp.dma_start(dst_v[:, a.cols, :], tab[a.q][:, :, D:2 * D]).then_inc(tab_out[a.q], 16)
                    batches(sp, NB, step)
                    for q in range(2):
                        hold(sp, tab_out[q], 32 * (NB // 2))

                @block.gpsimd
                def _(pool):
                    pool.iota(n_int[:, :], pattern=[[1, NK]], base=0, channel_multiplier=NK).then_inc(iota_done, 1)
                    for lvl in range(2):
                        table = last_rows if lvl == 0 else ins["dst_rows"]
                        width = P if lvl == 0 else P + 1
                        pool.wait_ge(lvl_idx, lvl + 1)

                        def step(m, *_):
                            if m is None:
                                return
                            need(pool, batch_done, m.n + (lvl * NB - 1))
                            pool.tensor_copy(idx_s[m.q][:, :], level_i[:, m.cols]).then_inc(idx_copied, 1)
                            pool.wait_ge(idx_copied, m.n + (lvl * NB + 1))
                            settle(pool)
                            for j in range(U):
                                pool.indirect_dma_start(
                                    out=rows[m.q][:, j, 0:width], out_offset=None, in_=table,
                                    in_offset=bass.IndirectOffsetOnAxis(ap=idx_s[m.q][:, j:j + 1], axis=0)
                                ).then_inc(rows_in[m.q], 16)
                        batches(pool, NB, step)
                    pool.wait_ge(ends_made, 2)
                    pool.dma_start(before_run[1:P, :], nf[0:P - 1, NK - 1:NK]).then_inc(before_in, 16)

                @block.scalar
                def _(act):
                    def step(m, a, _):
                        if m is not None:
                            act.wait_ge(varred, m.n * 2 + 2)
                            act.activation(stat_s[:, :], stat_s[:, :], ACT.Sqrt)
                            act.activation(stat_v[:, :], stat_v[:, :], ACT.Sqrt).then_inc(rooted, 1)
                        if a is None:
                            return
                        if not (isinstance(a.n, int) and a.n < 2):
                            act.wait_ge(tab_out[a.q], (a.n - a.q) * 16)
                        for t in range(U + 1):
                            if t < U:
                                q = t % 2
                                act.wait_ge(xT, a.n * U + (t + 1))
                                need(act, projd, a.n * U + max(t - 1, 0))
                                act.activation(xts[q][:, :], banks[q][0:S, 0:P], ACT.Identity,
                                               scale=wt("gs"), bias=wt("bs"))
                                act.activation(xtv[q][:, :], banks[q][0:V, P:2 * P], ACT.Copy,
                                               scale=wt("gv")).then_inc(evacT, 1)
                            if t >= 1:
                                act.wait_ge(projd, a.n * U + t)
                                act.activation(tab[a.q][:, t - 1, :], banks[2 + (t - 1) % 2][:, 0:2 * D], ACT.Copy)\
                                    .then_inc(tabbed, 1)
                    batches(act, NB, step)

                @block.tensor
                def _(pe):
                    def step(_, a, __):
                        if a is None:
                            return
                        pe.wait_ge(normed, a.n * 2 + 2)
                        need(pe, evacT, a.n * U)
                        for t in range(U + 1):
                            if t < U:
                                if t >= 2:
                                    pe.wait_ge(evacT, a.n * U + (t - 1))
                                settle(pe)
                                pe.transpose(banks[t % 2][0:S, 0:P], xn[a.q][:, t, 0:S], ident[:, :])
                                pe.transpose(banks[t % 2][0:V, P:2 * P], xn[a.q][:, t, S:D], ident[:, :])\
                                    .then_inc(xT, 1)
                            if t >= 1:
                                k = t - 1
                                pe.wait_ge(evacT, a.n * U + t)
                                need(pe, tabbed, a.n * U + max(k - 1, 0))
                                o = banks[2 + k % 2][:, 0:2 * D].rearrange("p (i d) -> p i d", d=D)
                                pe.matmul(o[:, :, 0:S], xts[k % 2][:, :],
                                          wt("WsSD").rearrange("p (i d) -> p i d", d=S), start=True, stop=True)
                                pe.matmul(o[:, :, S:D], xtv[k % 2][:, :],
                                          wt("WvSD").rearrange("p (i d) -> p i d", d=V), start=True, stop=True)\
                                    .then_inc(projd, 1)
                    batches(pe, NB, step)

                @block.vector
                def _(dve):
                    ch = chain.on(dve)
                    dve.wait_ge(xload, 32)
                    dve.wait_ge(iota_done, 1)
                    ch.link(dve.tensor_copy(nf[:, :], n_int[:, :])); ch.wait()
                    ch.link(dve.tensor_tensor(below[:, :, :], rep(sup[:, :], 1, NK), rep(nf[:, :], 2, SB),
                                              ALU.is_le)); ch.wait()
                    ch.link(dve.tensor_reduce(level[:, :], below[:, :, :], AX, ALU.add)); ch.wait()
                    ch.link(dve.tensor_scalar(level[:, :], level[:, :], float(SB - 1), None, ALU.min)); ch.wait()
                    dve.tensor_copy(level_i[:, :], level[:, :]).then_inc(lvl_idx, 1)
                    norm_ch = Chain(dve, sem("node_norm_chain"))
                    NORM_LINKS = 9

                    def norm(m):
                        ch = norm_ch
                        ch.count = m.n * NORM_LINKS
                        Xs, Xv, ns, nv = X[:, m.cols, 0:S], X[:, m.cols, S:D], xn[m.q][:, :, 0:S], xn[m.q][:, :, S:D]
                        ch.link(dve.tensor_reduce(stat_s[:, :], Xs, AX, ALU.add))
                        ch.link(dve.tensor_tensor(scr[:, :, :], Xv, Xv, ALU.mult)); ch.wait()
                        ch.link(dve.tensor_scalar(stat_s[:, :], stat_s[:, :], 1.0 / S, None, ALU.mult))
                        ch.link(dve.tensor_reduce(stat_v[:, :], scr[:, :, :], AX, ALU.add)); ch.wait()
                        need(dve, xT, (m.n - 1) * U)
                        ch.link(dve.tensor_tensor(ns, Xs, rep(stat_s[:, :], 2, S), ALU.subtract))
                        dve.tensor_scalar(stat_v[:, :], stat_v[:, :], 1.0 / C, 1e-5, ALU.mult, ALU.add)\
                            .then_inc(varred, 1)
                        ch.wait()
                        ch.link(dve.tensor_tensor(scr[:, :, 0:S], ns, ns, ALU.mult)); ch.wait()
                        ch.link(dve.tensor_reduce(stat_s[:, :], scr[:, :, 0:S], AX, ALU.add)); ch.wait()
                        dve.tensor_scalar(stat_s[:, :], stat_s[:, :], 1.0 / S, 1e-5, ALU.mult, ALU.add)\
                            .then_inc(varred, 1)
                        dve.wait_ge(rooted, m.n + 1)
                        ch.link(dve.reciprocal(stat_s[:, :], stat_s[:, :]))
                        ch.link(dve.reciprocal(stat_v[:, :], stat_v[:, :])); ch.wait()
                        dve.tensor_tensor(ns, ns, rep(stat_s[:, :], 2, S), ALU.mult).then_inc(normed, 1)
                        dve.tensor_tensor(nv, Xv, rep(stat_v[:, :], 2, V), ALU.mult).then_inc(normed, 1)

                    def first_level(m, *_):
                        if m is None:
                            return
                        norm(m)
                        dve.wait_ge(rows_in[m.q], m.of_parity(16 * U))
                        need(dve, batch_done, m.n)
                        dve.tensor_tensor(cmp[:, :, :], rows[m.q][:, :, 0:P], rep(nf[:, m.cols], 2, P), ALU.is_le)\
                            .then_inc(cmp_step, 1)
                        dve.wait_ge(cmp_step, m.n + 1)
                        settle(dve)
                        dve.tensor_reduce(found[:, m.cols], cmp[:, :, :], AX, ALU.add).then_inc(batch_done, 1)

                    def second_level(m, *_):
                        if m is None:
                            return
                        r = rows[m.q]
                        dve.wait_ge(rows_in[m.q], m.of_parity(16 * U) + (NB // 2) * 16 * U)
                        dve.wait_ge(cmp_step, m.n * 4 + NB)
                        dve.tensor_tensor(cmp[:, :, :], r[:, :, 1:P + 1], rep(nf[:, m.cols], 2, P), ALU.is_le)\
                            .then_inc(cmp_step, 1)
                        dve.wait_ge(cmp_step, m.n * 4 + (NB + 1))
                        settle(dve)
                        dve.tensor_reduce(found[:, m.cols], cmp[:, :, :], AX, ALU.add).then_inc(cmp_step, 1)
                        dve.wait_ge(cmp_step, m.n * 4 + (NB + 2))
                        dve.tensor_tensor(cmp[:, :, :], r[:, :, 1:P + 1], rep(nf[:, m.cols], 2, P),
                                          ALU.is_equal).then_inc(cmp_step, 1)
                        dve.wait_ge(cmp_step, m.n * 4 + (NB + 3))
                        settle(dve)
                        dve.tensor_reduce(has_row[:, m.cols], cmp[:, :, :], AX, ALU.max).then_inc(cmp_step, 1)
                        dve.tensor_tensor(has_carry[:, m.cols], r[:, :, 0], nf[:, m.cols], ALU.is_equal)\
                            .then_inc(batch_done, 1)
                    cmp_step = sem("compare_step")
                    batches(dve, NB, first_level)
                    dve.wait_ge(batch_done, NB)
                    ch.link(dve.scalar_tensor_tensor(out=level[:, :], in0=level[:, :], scalar=float(P),
                                                     in1=found[:, :], op0=ALU.mult, op1=ALU.add)); ch.wait()
                    ch.link(dve.tensor_scalar(level[:, :], level[:, :], float(NT - 1), None, ALU.min)); ch.wait()
                    dve.tensor_copy(level_i[:, :], level[:, :]).then_inc(lvl_idx, 1)
                    dve.wait_ge(lvl_idx, 2)
                    ch.link(dve.tensor_copy(carry_idx[:, :], level_i[:, :]))
                    batches(dve, NB, second_level)
                    dve.wait_ge(batch_done, 2 * NB)
                    ends = nf
                    dve.scalar_tensor_tensor(out=ends[:, :], in0=level[:, :], scalar=float(P), in1=found[:, :],
                                             op0=ALU.mult, op1=ALU.add).then_inc(ends_made, 1)
                    dve.memset(before_run[0:1, :], 0.0).then_inc(ends_made, 1)
                    dve.wait_ge(ends_made, 2)
                    ch.link(dve.tensor_scalar(found[:, :], found[:, :], -1.0, 0.0, ALU.add, ALU.max)); ch.wait()
                    ch.link(dve.scalar_tensor_tensor(out=level[:, :], in0=level[:, :], scalar=float(P),
                                                     in1=found[:, :], op0=ALU.mult, op1=ALU.add)); ch.wait()
                    ch.link(dve.tensor_copy(row_idx[:, :], level[:, :]))
                    ch.link(dve.tensor_tensor(degree[:, 1:NK], ends[:, 1:NK], ends[:, 0:NK - 1], ALU.subtract))
                    dve.wait_ge(before_in, 16)
                    ch.link(dve.tensor_tensor(degree[:, 0:1], ends[:, 0:1], before_run[:, :], ALU.subtract))
                    ch.wait()

        edge_loop_0(nc, ctx, sem, banks, W, wt, ident, rbf_w, ins, rbf_parts, edge_cut, src_table, dst_table,
                    agg0, NG)
        carry_scan(nc, ctx, sem, banks, ident, ins, agg0, carry0, NT, AGG0, True, chain)

        X1 = sb("X1", [P, NK, D])
        node_step_0(nc, ctx, sem, banks, wt, ident, ins, agg0, carry0, conv_table, X1, row_idx, carry_idx,
                    has_row, has_carry, node_a, NK)
        edge_loop_1(nc, ctx, sem, banks, wt, rbf_w, ins, rbf_parts, conv_table, agg1, NG)
        carry_scan(nc, ctx, sem, banks, ident, ins, agg1, carry1, NT, AGG1, False, chain)
        node_step_1(nc, ctx, sem, banks, agg1, carry1, out, X1, row_idx, carry_idx, has_row, has_carry,
                    node_a, degree, NK)


def edge_loop_0(nc, ctx, sem, banks, W, wt, ident, rbf_w, ins, rbf_parts, edge_cut, src_table, dst_table,
                agg0, NG):
    with ExitStack() as ph:
        def sb(name, shape, dt=F32):
            return ph.enter_context(nc.sbuf_tensor(name, shape, dt))
        pack = [sb(f"e_pack{i}", [P, 32], I32) for i in range(4)]
        idx = [p[:, 0:8] for p in pack]
        Y = [p[:, 8:32].bitcast(F32).rearrange("p (t c) -> p t c", t=TG) for p in pack]
        xs = [sb(f"e_xs{i}", [P, 512], BF16) for i in range(4)]
        drow = [sb(f"e_drow{i}", [P, 512], I32) for i in range(4)]
        cut = [sb(f"e_cut{i}", [16, P + 1]) for i in range(4)]
        feat = [sb(f"feat{i}", [P, TG, D + 64]) for i in range(4)]
        stg = [sb(f"stg{i}", [P, TG, 352]) for i in range(2)]
        feat2 = sb("mid_feat", [P, TG, D + 64])
        tmp = [sb(f"tmp{i}", [P, TG, V]) for i in range(6)]
        vlin = sb("vlin", [P, TG, V])
        tabs = [sb(f"tabs{k}", [P, 512]) for k in range(3)]
        prods = [sb(f"prods{k}", [P, 512]) for k in range(3)]
        st2 = [sb(f"st2_{k}", [P, 512]) for k in range(3)]
        lg = sb("lg", [P, TG, S])
        th = [sb(f"th{i}", [P, TG, V]) for i in range(2)]
        av = [sb(f"av{i}", [P, TG, 192]) for i in range(2)]
        gate = sb("gate", [P, TG, C])
        a_e = [sb(f"a_e{i}", [P, 16]) for i in range(2)]
        late_Y = [sb(f"late_Y{i}", [P, TG, 6]) for i in range(4)]
        one = sb("one", [P, 1])
        run_max = sb("run_max", [16, P])
        seg_max = sb("seg_max", [16, P])
        diff = sb("diff", [P, 16])
        ex8 = sb("ex8", [P, TG, C])
        ha = [sb(f"ha{i}", [P, TG, D + H]) for i in range(2)]
        hv = sb("hv", [P, TG, V])
        eq = [sb(f"eq{i}", [P, TG, P]) for i in range(4)]
        orow = [sb(f"orow{i}", [P, TG, AGG0]) for i in range(2)]

        small_in = [sem(f"l0_small_in{i}") for i in range(4)]

        big_in = [sem(f"l0_big_in{i}") for i in range(4)]
        gathered = [sem(f"l0_gathered{i}") for i in range(4)]
        out_done = [sem(f"l0_out_done{i}") for i in range(2)]
        (table_mm, table_out, v_dup, scaled1, v2_done, v2_dup, scaled2, gated, staged1, staged1_T, product,
         stage1, stage1_out, logit, logit_T, logit_read, maxed, max_T, diffed, exped, max_out, staged2,
         staged2_T, st2_out, stage2, eq_made, ha_made, agg, agg_out) = (sem("l0_" + n) for n in (
             "table_mm", "table_out", "v_dup", "scaled1", "v2_done", "v2_dup", "scaled2", "gated", "staged1",
             "staged1_T", "product", "stage1", "stage1_out", "logit", "logit_T", "logit_read", "maxed", "max_T",
             "diffed", "exped", "max_out", "staged2", "staged2_T", "st2_out", "stage2", "eq_made", "ha_made",
             "agg", "agg_out"))
        own, one_made = sem("l0_vector_chain"), sem("l0_one_made")
        agg_v = agg0.rearrange("(g j p) c -> g p j c", j=TG, p=P)
        xs_v = rbf_parts.rearrange("s c (g n) -> s g c n", n=512)
        drow_v = ins["dst_flat"].rearrange("(g n) -> g n", n=512)
        PARTS = ((0, 3), (1, 3), (2, 2))

        with nc.Block() as block:
            @block.sync
            def _(sp):
                def step(g, early, front, mid, tail):
                    if not early:
                        return
                    s, n = g.slot, g.n
                    hold(sp, table_mm, 3 * (n - 3))
                    hold(sp, eq_made, n - 3)
                    hold(sp, scaled1, n - 3)
                    hold(sp, staged1, n - 3)
                    if not (isinstance(g.base, int) and g.base == 0):
                        hold(sp, gathered[s], g.base * 32)
                    at = bass.ds(n, 1)
                    sp.dma_start(pack[s][:, :], ins["edge_pack"][at].squeeze(0)).then_inc(small_in[s], 16)
                    c0 = 0
                    for part, copies in PARTS:
                        sp.dma_start(xs[s][c0:c0 + 16 * copies, :], rep(xs_v[part, at], 0, copies).squeeze(1))\
                            .then_inc(big_in[s], 16)
                        c0 += 16 * copies
                    sp.dma_start(drow[s][:, :], drow_v[at].broadcast_to([P, 512])).then_inc(big_in[s], 16)
                    hold(sp, maxed, n - 3)
                    sp.dma_start(cut[s][:, :], edge_cut[at].squeeze(0)).then_inc(big_in[s], 16)
                steps(sp, NG, step, 4)

            @block.gpsimd
            def _(pool):
                def gather(table, s, col, j, op):
                    pool.indirect_dma_start(
                        out=feat[s][:, j, 0:D], out_offset=None, in_=table,
                        in_offset=bass.IndirectOffsetOnAxis(ap=idx[s][:, col + j:col + j + 1], axis=0),
                        compute_op=op).then_inc(gathered[s], 16)

                def step(g, early, front, mid, tail):
                    if front:
                        f = g.back(1)
                        pool.wait_ge(gathered[f.slot], f.base * 32 + 64)
                        settle(pool)
                        for j in range(TG):
                            gather(dst_table, f.slot, 4, j, ALU.add)
                    if early:
                        s = g.slot
                        need(pool, staged1, g.n - 3)
                        need(pool, scaled1, g.n - 3)
                        pool.wait_ge(small_in[s], g.loads(16))
                        settle(pool)
                        for j in range(TG):
                            gather(src_table, s, 0, j, ALU.bypass)
                steps(pool, NG, step, 4)

            @block.vector
            def _(dve):
                ch = Chain(dve, own)

                def comp(ap, c0, n=3, w=C):
                    return ap[:, :, c0:c0 + n * w].rearrange("p t (x c) -> p t x c", c=w)

                def yx(y, c0, w=C):
                    return rep(y[:, :, c0:c0 + 3], 3, w)

                def products_with_y(st, f, tmp, y, dup_sem, dup_at, last_sem):
                    a = ch.link(dve.tensor_tensor(comp(tmp[0], 0), comp(f, S), yx(y, 1), ALU.mult))
                    dve.wait_ge(dup_sem, dup_at)
                    b = ch.link(dve.tensor_tensor(comp(tmp[1], 0), comp(f, S + C), yx(y, 3), ALU.mult))
                    ch.wait(a)
                    a = ch.link(dve.tensor_tensor(st[:, :, 224:256], tmp[0][:, :, 0:C], tmp[0][:, :, C:2 * C],
                                                  ALU.add))
                    c = ch.link(dve.tensor_tensor(comp(tmp[2], 0), comp(f, S + 2 * C), yx(y, 2), ALU.mult))
                    ch.wait(a)
                    ch.link(dve.tensor_tensor(st[:, :, 224:256], st[:, :, 224:256], tmp[0][:, :, 2 * C:V],
                                              ALU.add))
                    ch.wait(c)
                    dve.tensor_tensor(st[:, :, 256:352], tmp[1][:, :, :], tmp[2][:, :, :], ALU.subtract)\
                        .then_inc(last_sem, 1)

                def gated_values(m):
                    q, y = m.slot % 2, late_Y[m.slot]
                    dve.wait_ge(stage1_out, 4 * (m.n + 1))
                    b = ch.link(dve.tensor_tensor(comp(vlin, 0), rep(av[q][:, :, S:V], 2, 3), yx(y, 1), ALU.mult))
                    a = ch.link(dve.scalar_tensor_tensor(out=lg[:, :, :], in0=av[q][:, :, 0:S], scalar=0.2,
                                                         in1=av[q][:, :, 0:S], op0=ALU.mult, op1=ALU.max))
                    ch.wait(b)
                    b = ch.link(dve.tensor_tensor(vlin[:, :, :], vlin[:, :, :], av[q][:, :, V:192], ALU.add))
                    ch.wait(a)
                    a = ch.link(dve.tensor_tensor(lg[:, :, :], lg[:, :, :], rep(wt("adot"), 1, TG), ALU.mult))
                    dve.wait_ge(gated, m.n + 1)
                    need(dve, staged2, m.n)
                    need(dve, scaled2, m.n)
                    ch.wait(b)
                    dve.tensor_tensor(comp(feat2, S), comp(vlin, 0), rep(gate[:, :, :], 2, 3), ALU.mult)\
                        .then_inc(v2_done, 1)
                    need(dve, diffed, m.n - 1)
                    ch.wait(a)
                    dve.tensor_reduce(a_e[q][:, :], lg[:, :, :].rearrange("p t (h c) -> p (t h) c", h=H), AX,
                                      ALU.add).then_inc(logit, 1)

                def half(t, q, y, b):
                    ts2, o = slice(2 * b, 2 * b + 2), banks[5 + b][:, 0:384].rearrange("p (t c) -> p t c", t=2)
                    dve.wait_ge(stage2, 2 * t.n + (b + 1))
                    a = ch.link(dve.tensor_tensor(
                        hv[:, ts2, :].rearrange("p t (x c) -> p t x c", c=C), rep(o[:, :, 64:96], 2, 3),
                        rep(y[:, ts2, 1:4], 3, C), ALU.mult))
                    ch.link(dve.tensor_tensor(
                        ha[q][:, ts2, 0:S].rearrange("p t (h c) -> p t h c", h=H),
                        o[:, :, 0:64].rearrange("p t (h c) -> p t h c", h=H),
                        rep(ha[q][:, ts2, D:D + H], 3, 16), ALU.mult))
                    ch.wait(a)
                    return ch.link(dve.tensor_tensor(hv[:, ts2, :], hv[:, ts2, :], o[:, :, 96:192], ALU.add))

                def step(g, early, front, mid, tail):
                    f, m, t = (g.back(k) for k in (1, 2, 3))
                    if mid:
                        gated_values(m)
                    if early:
                        s, n = g.slot, g.n
                        dve.wait_ge(big_in[s], g.loads(80))
                        dve.wait_ge(small_in[s], g.loads(16))
                        need(dve, agg, 2 * (n - 3))
                        dve.tensor_tensor(eq[s][:, :, :], drow[s][:, :].rearrange("p (t e) -> p t e", t=TG),
                                          rep(idx[s][:, 4:8], 2, P), ALU.is_equal).then_inc(eq_made, 1)
                    if front:
                        for k, r in enumerate((P, P, V)):
                            dve.wait_ge(staged1_T, 3 * f.n + (k + 1))
                            dve.wait_ge(table_out, 3 * f.n + (k + 1))
                            if k == 0:
                                need(dve, stage1, 4 * f.n)
                            dve.tensor_tensor(prods[k][0:r, :], tabs[k][0:r, :], banks[k][0:r, :], ALU.mult)\
                                .then_inc(product, 1)
                    if tail:
                        y, q = late_Y[t.slot], t.slot % 2
                        dve.wait_ge(max_T, t.n + 1)
                        need(dve, exped, t.n)
                        dve.tensor_tensor(diff[:, :], a_e[q][:, :], banks[7][:, 328:344], ALU.subtract)\
                            .then_inc(diffed, 1)
                    if early:
                        dve.wait_ge(gathered[s], g.loads(128))
                        need(dve, staged1_T, 3 * n)
                        need(dve, staged1, n)
                        products_with_y(stg[0], feat[s], tmp[0:3], Y[s], v_dup, 2 * (n + 1), staged1)
                    if tail:
                        need(dve, ha_made, t.n)
                    if mid:
                        dve.wait_ge(logit_T, m.n + 1)
                    if tail:
                        dve.wait_ge(exped, t.n + 1)
                        half(t, q, y, 0)
                    if mid:
                        dve.wait_ge(big_in[m.slot], m.loads(80))
                        dve.tensor_tensor_scan(run_max[:, :], cut[m.slot][:, 0:P], banks[5][0:16, 384:512], -OFF,
                                               ALU.add, ALU.max).then_inc(logit_read, 1)
                    if tail:
                        last = half(t, q, y, 1)
                        ch.wait(last)
                        dve.tensor_tensor(comp(ha[q], S), comp(hv, 0), rep(ex8[:, :, :], 2, 3), ALU.mult)\
                            .then_inc(ha_made, 1)
                    if mid:
                        need(dve, staged2_T, 3 * m.n)
                        dve.wait_ge(v2_done, m.n + 1)
                        products_with_y(stg[1], feat2, tmp[3:6], late_Y[m.slot], v2_dup, 2 * (m.n + 1), staged2)
                        dve.wait_ge(logit_read, m.n + 1)
                        need(dve, max_T, m.n)
                        dve.tensor_tensor_scan(seg_max[:, ::-1], cut[m.slot][:, P:0:-1], run_max[:, ::-1], -OFF,
                                               ALU.add, ALU.max).then_inc(maxed, 1)
                dve.memset(one[:, :], 1.0).then_inc(one_made, 1)
                steps(dve, NG, step, 4, ch)

            @block.scalar
            def _(act):
                def scaled_by_y0(st, f, y, done):
                    for j in range(TG):
                        one_scaled_by_y0(st, f, y, j, done)

                def one_scaled_by_y0(st, f, y, j, done):
                    ins_ = act.activation(st[:, j, S:S + D], f[:, j, 0:D], ACT.Copy, scale=y[:, j, 0:1])
                    if j == TG - 1:
                        ins_.then_inc(done, 1)

                def step(g, early, front, mid, tail):
                    f, m, t = (g.back(k) for k in (1, 2, 3))
                    if early:
                        e = feat[g.slot]
                        act.wait_ge(small_in[g.slot], g.loads(16))
                        need(act, ha_made, g.n - 3)
                        need(act, staged2, g.n - 3)
                        need(act, scaled2, g.n - 3)
                        act.activation(late_Y[g.slot][:, :, :], Y[g.slot][:, :, :], ACT.Copy).then_inc(v_dup, 1)
                        act.wait_ge(gathered[g.slot], g.loads(128))
                        act.activation(e[:, :, D:D + 64], e[:, :, S:S + 64], ACT.Copy).then_inc(v_dup, 1)
                    if mid:
                        act.wait_ge(stage1_out, 4 * (m.n + 1))
                        need(act, scaled2, m.n)
                        need(act, staged2_T, 3 * m.n)
                        q = m.slot % 2
                        act.activation(stg[1][:, :, 0:S], th[q][:, :, 0:S], ACT.Identity, bias=one[:, 0:1])
                        act.activation(feat2[:, :, 0:S], th[q][:, :, 0:S], ACT.Identity, bias=one[:, 0:1])\
                            .then_inc(v2_dup, 1)
                        act.wait_ge(v2_done, m.n + 1)
                        act.activation(feat2[:, :, D:D + 64], feat2[:, :, S:S + 64], ACT.Copy).then_inc(v2_dup, 1)
                        act.wait_ge(v2_dup, 2 * m.n + 1)
                        scaled_by_y0(stg[1], feat2, late_Y[m.slot], scaled2)
                    if tail:
                        q = t.slot % 2
                        if not (isinstance(t.base, int) and t.base == 0 and t.slot < 2):
                            act.wait_ge(out_done[q], t.base * 8 + 16 * (t.slot // 2))
                        act.wait_ge(diffed, t.n + 1)
                        need(act, ha_made, t.n)
                        act.activation(ha[q][:, :, D:D + H], diff[:, :].rearrange("p (t h) -> p t h", t=TG), ACT.Exp)
                        act.activation(ex8[:, :, :].rearrange("p t (h c) -> p (t h) c", h=H), rep(diff[:, :], 2, 8),
                                       ACT.Exp).then_inc(exped, 1)
                        act.activation(orow[q][:, :, D + H:AGG0],
                                       banks[7][:, 328:344].rearrange("p (t h) -> p t h", t=TG), ACT.Copy)\
                            .then_inc(max_out, 1)
                    if early:
                        need(act, staged1_T, 3 * g.n)
                        act.activation(stg[0][:, :, 0:S], e[:, :, 0:S], ACT.Copy)
                    if front:
                        q = f.slot % 2
                        need(act, v2_done, f.n - 1)
                        need(act, logit, f.n - 1)
                    for j in range(TG):
                        if front:
                            act.wait_ge(stage1, 4 * f.n + (j + 1))
                            o = banks[3 + j % 2]
                            act.activation(th[q][:, j, :], o[:, 0:V], ACT.Tanh, scale=0.5)
                            act.activation(av[q][:, j, :], o[:, V:288], ACT.Copy).then_inc(stage1_out, 1)
                        if early:
                            one_scaled_by_y0(stg[0], e, Y[g.slot], j, scaled1)
                    if front:
                        act.wait_ge(stage1_out, 4 * (f.n + 1))
                        need(act, v2_done, f.n)
                        act.activation(gate[:, :, :], th[q][:, :, S:V], ACT.Identity, bias=one[:, 0:1])\
                            .then_inc(gated, 1)
                    if tail:
                        agg_evac(t, 0)
                        agg_evac(t, 1)
                    if mid:
                        for k, r in enumerate((P, P, V)):
                            act.wait_ge(staged2_T, 3 * m.n + (k + 1))
                            need(act, stage2, 2 * m.n)
                            act.activation(st2[k][0:r, :], banks[k][0:r, :], ACT.Copy).then_inc(st2_out, 1)
                    if early:
                        n = g.n
                        for k, r in enumerate((P, P, V)):
                            act.wait_ge(table_mm, 3 * n + (k + 1))
                            need(act, product, 3 * n - 2 + k)
                            act.activation(tabs[k][0:r, :], banks[(5, 3, 4)[k]][0:r, :], ACT.Copy).then_inc(table_out, 1)
                    if tail:
                        act.wait_ge(agg_out, 2 * (t.n + 1))
                        act.dma_start(agg_v[bass.ds(t.n, 1)].squeeze(0), orow[t.slot % 2][:, :, :])\
                            .then_inc(out_done[t.slot % 2], 16)

                def agg_evac(t, b):
                    q = t.slot % 2
                    act.wait_ge(agg, 2 * t.n + (b + 1))
                    act.activation(orow[q][:, 2 * b:2 * b + 2, 0:D + H],
                                   banks[7 - b][:, 0:2 * (D + H)].rearrange("p (t c) -> p t c", t=2), ACT.Copy)\
                        .then_inc(agg_out, 1)
                act.wait_ge(one_made, 1)
                steps(act, NG, step, 4)
                for i in range(2):
                    act.wait_ge(out_done[i], 16 * (NG // 2))

            @block.tensor
            def _(pe):
                def sums(t, b):
                    q, e = t.slot % 2, t.slot
                    need(pe, agg_out, 2 * t.n - 1 + b)
                    for j in (2 * b, 2 * b + 1):
                        mm = pe.matmul(banks[7 - b][:, (j % 2) * (D + H):(j % 2 + 1) * (D + H)], eq[e][:, j, :],
                                       ha[q][:, j, :], start=True, stop=True)
                    mm.then_inc(agg, 1)

                def tables(g):
                    pe.wait_ge(big_in[g.slot], g.loads(80))
                    need(pe, stage1_out, 4 * g.n)
                    for k, r in enumerate((P, P, V)):
                        if k == 0:
                            need(pe, ha_made, g.n - 2)
                            need(pe, logit_read, g.n - 1)
                        pe.matmul(banks[(5, 3, 4)[k]][0:r, :], rbf_w[:, P * k:P * k + r], xs[g.slot][:, :],
                                  start=True, stop=True).then_inc(table_mm, 1)

                def step(g, early, front, mid, tail):
                    f, m, t = (g.back(k) for k in (1, 2, 3))
                    if front:
                        pe.wait_ge(staged1, f.n + 1)
                        pe.wait_ge(scaled1, f.n + 1)
                        for k, r in enumerate((P, P, V)):
                            need(pe, st2_out, 3 * f.n - 5 + k)
                            for j in range(TG):
                                mm = pe.transpose(banks[k][0:r, P * j:P * j + P], stg[0][:, j, P * k:P * k + r],
                                                  ident[:, :])
                            mm.then_inc(staged1_T, 1)
                    if front:
                        pe.wait_ge(table_out, 3 * f.n + 1)
                    if mid:
                        pe.wait_ge(logit, m.n + 1)
                        if not (early and front):
                            need(pe, logit_read, m.n)
                            need(pe, ha_made, m.n - 1)
                        pe.transpose(banks[5][0:16, 384:512], a_e[m.slot % 2][:, :], ident[:, :])\
                            .then_inc(logit_T, 1)
                    if tail:
                        if not (early and front):
                            pe.wait_ge(st2_out, 3 * t.n + 3)
                            need(pe, ha_made, t.n)
                            need(pe, agg_out, 2 * t.n)
                            pe.wait_ge(logit_read, t.n + 1)
                        for j in range(TG):
                            o = banks[5 + j // 2]
                            c = 192 * (j % 2)
                            e = slice(P * j, P * j + P)
                            pe.matmul(o[:, c:c + 192], st2[1][:, e], wt("W2b"), start=True, stop=False)
                            pe.matmul(o[:, c:c + 96], st2[0][:, e], wt("W2a"), start=False, stop=False)
                            mm = pe.matmul(o[:, c + 96:c + 192], st2[2][0:V, e], wt("W2c"), start=False, stop=True)
                            if j % 2:
                                mm.then_inc(stage2, 1)
                    if front:
                        pe.wait_ge(product, 3 * f.n + 3)
                        pe.wait_ge(table_out, 3 * f.n + 3)
                        for j in range(TG):
                            if j >= 2:
                                need(pe, stage1_out, 4 * f.n + j - 1)
                            o = banks[3 + j % 2]
                            e = slice(P * j, P * j + P)
                            pe.matmul(o[:, 0:288], prods[1][:, e], wt("W1b"), start=True, stop=False)
                            pe.matmul(o[:, 0:192], prods[0][:, e], wt("W1a"), start=False, stop=False)
                            pe.matmul(o[:, 192:288], prods[2][0:V, e], wt("W1c"), start=False, stop=True)\
                                .then_inc(stage1, 1)
                    if tail:
                        pe.wait_ge(eq_made, t.n + 1)
                        pe.wait_ge(ha_made, t.n + 1)
                        pe.wait_ge(max_out, t.n + 1)
                        sums(t, 0)
                        sums(t, 1)
                    if mid:
                        pe.wait_ge(staged2, m.n + 1)
                        pe.wait_ge(scaled2, m.n + 1)
                        for k, r in enumerate((P, P, V)):
                            if front:
                                pe.wait_ge(product, 3 * f.n + (k + 1))
                            for j in range(TG):
                                mm = pe.transpose(banks[k][0:r, P * j:P * j + P], stg[1][:, j, P * k:P * k + r],
                                                  ident[:, :])
                            mm.then_inc(staged2_T, 1)
                    if early:
                        tables(g)
                    if mid:
                        pe.wait_ge(maxed, m.n + 1)
                        need(pe, agg_out, 2 * m.n)
                        settle(pe)
                        pe.transpose(banks[7][:, 328:344], seg_max[:, :], ident[0:16, 0:16]).then_inc(max_T, 1)
                steps(pe, NG, step, 4)


def carry_scan(nc, ctx, sem, banks, ident, ins, agg, carry, NT, width, softmax, chain):
    SB = NT // P
    tag = "c0_" if softmax else "c1_"
    R = D + H if softmax else width
    parts = ((0, P), (P, R - P))
    with ExitStack() as ph:
        def sb(name, shape, dt=F32):
            return ph.enter_context(nc.sbuf_tensor(tag + name, shape, dt))
        last = sb("last", [P, SB, width])
        mrep = sb("mrep", [P, SB, R]) if softmax else None
        edges = [sb(f"edge{i}", [P, NT], I32) for i in range(3)]
        go_on = sb("go_on", [P, NT])
        cut = sb("cut", [P, NT])
        val = [sb(f"val{i}", [P, NT]) for i in range(2)]
        mx = [sb(f"mx{i}", [P, NT]) for i in range(2)] if softmax else None
        mtop = [sb(f"mtop{i}", [P, NT]) for i in range(2)] if softmax else None
        keep = sb("keep", [P, NT])
        gain = sb("gain", [P, NT])
        back = sb("back", [P, SB, width])
        loaded, turned, turned_out, scanned, back_T, back_out, stored = (
            sem(tag + n) for n in ("loaded", "turned", "turned_out", "scanned", "back_T", "back_out", "stored"))
        if softmax:
            rep_done, arg_done, exp_done = sem("c0_rep_done"), sem("c0_arg_done"), sem("c0_exp_done")
        with nc.Block() as block:
            @block.sync
            def _(sp):
                sp.dma_start(last[:, :, :], agg.rearrange("(b t e) c -> e t b c", t=P, e=P)[P - 1])\
                    .then_inc(loaded, 16)
                for i, n in enumerate(("first", "last", "before")):
                    sp.dma_start(edges[i][:, :], ins[n].partition_broadcast(P)).then_inc(loaded, 16)
                hold(sp, back_out, SB)
                sp.dma_start(carry[1:NT + 1].rearrange("(b t) c -> t b c", t=P), back[:, :, :]).then_inc(stored, 16)
                hold(sp, stored, 16)

            @block.tensor
            def _(pe):
                pe.wait_ge(loaded, 64)
                if softmax:
                    pe.wait_ge(rep_done, 3)
                k = 0
                for b in range(SB):
                    for i, (c, r) in enumerate(parts):
                        for src in ((last, mrep) if softmax else (last,)):
                            if k >= 4:
                                pe.wait_ge(turned_out, k - 3)
                            pe.transpose(banks[k % 4][0:r, 0:P], src[:, b, c:c + r], ident[:, :]).then_inc(turned, 1)
                            k += 1
                pe.wait_ge(scanned, 2)
                k = 0
                for b in range(SB):
                    if k >= 4:
                        pe.wait_ge(back_out, b - 3)
                    o = banks[4 + b % 4]
                    e = slice(b * P, b * P + P)
                    for i, (c, r) in enumerate(parts):
                        mm = pe.transpose(o[:, c:c + r], val[i][0:r, e], ident[0:r, 0:r])
                    if softmax:
                        mm = pe.transpose(o[:, 256:256 + R - P], mtop[1][0:R - P, e], ident[0:R - P, 0:R - P])
                    mm.then_inc(back_T, 1)
                    k += 1

            @block.scalar
            def _(act):
                k = 0
                for b in range(SB):
                    for i, (c, r) in enumerate(parts):
                        for dst in ((val, mx) if softmax else (val,)):
                            act.wait_ge(turned, k + 1)
                            act.activation(dst[i][0:r, b * P:b * P + P], banks[k % 4][0:r, 0:P], ACT.Copy)\
                                .then_inc(turned_out, 1)
                            k += 1
                if softmax:
                    for i, (c, r) in enumerate(parts):
                        act.wait_ge(arg_done, 2 * i + 2)
                        act.activation(keep[0:r, :], keep[0:r, :], ACT.Exp)
                        act.activation(gain[0:r, :], gain[0:r, :], ACT.Exp).then_inc(exp_done, 1)
                for b in range(SB):
                    act.wait_ge(back_T, b + 1)
                    o = banks[4 + b % 4]
                    if softmax:
                        act.activation(back[:, b, D + H:], o[:, 256 + R - P - H:256 + R - P], ACT.Copy)
                    act.activation(back[:, b, 0:R], o[:, 0:R], ACT.Copy).then_inc(back_out, 1)

            @block.vector
            def _(dve):
                ch = chain.on(dve)
                dve.wait_ge(loaded, 64)
                if softmax:
                    m = last[:, :, D + H:]
                    dve.tensor_copy(mrep[:, :, 0:S].rearrange("p b (h c) -> p b h c", h=H), rep(m, 3, 16))\
                        .then_inc(rep_done, 1)
                    for x in range(3):
                        ins_ = dve.tensor_copy(
                            mrep[:, :, S + C * x:S + C * x + C].rearrange("p b (h c) -> p b h c", h=H), rep(m, 3, 8))
                    ins_.then_inc(rep_done, 1)
                    dve.tensor_copy(mrep[:, :, D:R], m).then_inc(rep_done, 1)
                ch.link(dve.tensor_tensor(go_on[:, :], edges[0][:, :], edges[1][:, :], ALU.is_equal))
                ch.link(dve.tensor_tensor(cut[:, :], edges[0][:, :], edges[2][:, :], ALU.is_equal))
                ch.wait()
                ch.link(dve.tensor_tensor(go_on[:, :], go_on[:, :], cut[:, :], ALU.mult))
                ch.wait()
                dve.wait_ge(turned_out, SB * len(parts) * (2 if softmax else 1))
                if not softmax:
                    for i, (c, r) in enumerate(parts):
                        dve.tensor_tensor_scan(val[i][0:r, :], go_on[0:r, :], val[i][0:r, :], 0.0, ALU.mult, ALU.add)\
                            .then_inc(scanned, 1)
                    return
                ch.link(dve.tensor_scalar(cut[:, :], go_on[:, :], -1.0, OFF, ALU.add, ALU.mult))
                ch.wait()
                for i, (c, r) in enumerate(parts):
                    if i >= 1:
                        dve.wait_ge(scanned, i)
                    top = mtop[i]
                    ch.link(dve.tensor_tensor_scan(top[0:r, :], cut[0:r, :], mx[i][0:r, :], -OFF, ALU.add, ALU.max))
                    ch.wait()
                    ch.link(dve.memset(keep[0:r, 0:1], 0.0))
                    ch.link(dve.tensor_tensor(keep[0:r, 1:NT], top[0:r, 0:NT - 1], top[0:r, 1:NT], ALU.subtract))
                    ch.wait()
                    dve.tensor_scalar(keep[0:r, :], keep[0:r, :], 0.0, None, ALU.min).then_inc(arg_done, 1)
                    dve.tensor_tensor(gain[0:r, :], mx[i][0:r, :], top[0:r, :], ALU.subtract).then_inc(arg_done, 1)
                    dve.wait_ge(exp_done, i + 1)
                    ch.link(dve.tensor_tensor(keep[0:r, :], keep[0:r, :], go_on[0:r, :], ALU.mult))
                    ch.link(dve.tensor_tensor(gain[0:r, :], gain[0:r, :], val[i][0:r, :], ALU.mult))
                    ch.wait()
                    dve.tensor_tensor_scan(val[i][0:r, :], keep[0:r, :], gain[0:r, :], 0.0, ALU.mult, ALU.add)\
                        .then_inc(scanned, 1)


def normalise(dve, ch, X, xn, scr, stat, varred, rooted, n):
    settle(dve)
    ch.link(dve.tensor_reduce(stat[:, :], X, AX, ALU.add)); ch.wait()
    ch.link(dve.tensor_scalar(stat[:, :], stat[:, :], 1.0 / D, None, ALU.mult)); ch.wait()
    ch.link(dve.tensor_tensor(xn[:, :, :], X, rep(stat[:, :], 2, D), ALU.subtract)); ch.wait()
    ch.link(dve.tensor_tensor(scr[:, :, :], xn[:, :, :], xn[:, :, :], ALU.mult)); ch.wait()
    ch.link(dve.tensor_reduce(stat[:, :], scr[:, :, :], AX, ALU.add)); ch.wait()
    dve.tensor_scalar(stat[:, :], stat[:, :], 1.0 / D, 1e-5, ALU.mult, ALU.add).then_inc(varred, 1)
    dve.wait_ge(rooted, n + 1)
    ch.link(dve.reciprocal(stat[:, :], stat[:, :])); ch.wait()


def gather_batches(pool, NB, row_idx, carry_idx, idx_s, agg, carry, ga, gc, copied, used, gathered):
    def step(m, *_):
        if m is None:
            return
        q = m.q
        need(pool, used, m.n - 1)
        pool.tensor_copy(idx_s[q][:, 0:NODE_BATCH], row_idx[:, m.cols]).then_inc(copied, 1)
        pool.tensor_copy(idx_s[q][:, NODE_BATCH:], carry_idx[:, m.cols]).then_inc(copied, 1)
        pool.wait_ge(copied, m.n * 2 + 2)
        settle(pool)
        for j in range(NODE_BATCH):
            for i, (table, dst) in enumerate(((agg, ga[q]), (carry, gc[q]))):
                c = NODE_BATCH * i + j
                pool.indirect_dma_start(out=dst[:, j, :], out_offset=None, in_=table,
                                        in_offset=bass.IndirectOffsetOnAxis(ap=idx_s[q][:, c:c + 1], axis=0))\
                    .then_inc(gathered[q], 16)
    batches(pool, NB, step)


def node_step_0(nc, ctx, sem, banks, wt, ident, ins, agg0, carry0, conv_table, X1, row_idx, carry_idx,
                has_row, has_carry, node_a, NK):
    NB = NK // NODE_BATCH
    U = NODE_BATCH
    R = D + H
    with ExitStack() as ph:
        def sb(name, shape, dt=F32):
            return ph.enter_context(nc.sbuf_tensor("n0_" + name, shape, dt))
        idx_s = [sb(f"idx{i}", [P, 2 * U], I32) for i in range(2)]
        ga = [sb(f"ga{i}", [P, U, AGG0]) for i in range(2)]
        gc = [sb(f"gc{i}", [P, U, AGG0]) for i in range(2)]
        ea, ec, mt = sb("ea", [P, U, H]), sb("ec", [P, U, H]), sb("mt", [P, U, H])
        aggn = [sb(f"aggn{i}", [P, U, D]) for i in range(2)]
        turned = [sb(f"turned{i}", [P, 2 * P]) for i in range(2)]
        turned2 = [sb(f"turned2_{i}", [P, 2 * P]) for i in range(2)]
        xn = [sb(f"xn{i}", [P, U, D]) for i in range(2)]
        inv_a = [sb(f"inv_a{i}", [P, U]) for i in range(2)]
        tab = [sb(f"tab{i}", [P, U, D]) for i in range(2)]
        scr, st = sb("scr", [P, U, D]), sb("st", [P, U])
        (loaded, copied, exp_arg, exped, normed, T, T_out, proj, added, varred, rooted, ready,
         T2, T2_out, proj2, tabbed) = (sem("n0_" + n) for n in (
             "loaded", "copied", "exp_arg", "exped", "normed", "T", "T_out", "proj", "added",
             "varred", "rooted", "ready", "T2", "T2_out", "proj2", "tabbed"))
        gathered = [sem(f"n0_gathered{i}") for i in range(2)]
        tab_out = [sem(f"n0_tab_out{i}") for i in range(2)]
        conv_v = conv_table.rearrange("(p k) d -> p k d", k=NK)
        THIRDS = ((0, 3), (3, 3), (6, 1))

        with nc.Block() as block:
            @block.sync
            def _(sp):
                sp.dma_start(X1[:, :, :], ins["x"].rearrange("(p k) d -> p k d", k=NK)).then_inc(loaded, 16)

                def step(m, a, c):
                    if c is not None:
                        hold(sp, tabbed, c.n * U + U)
                        sp.dma_start(conv_v[:, c.cols, :], tab[c.q][:, :, :]).then_inc(tab_out[c.q], 16)
                batches(sp, NB, step)
                for q in range(2):
                    hold(sp, tab_out[q], 16 * (NB // 2))

            @block.gpsimd
            def _(pool):
                gather_batches(pool, NB, row_idx, carry_idx, idx_s, agg0, carry0, ga, gc, copied, normed, gathered)

            @block.vector
            def _(dve):
                merge_ch, norm_ch = Chain(dve, sem("n0_merge_chain")), Chain(dve, sem("n0_norm_chain"))
                dve.wait_ge(loaded, 16)
                MERGE_LINKS, NORM_LINKS = 14 + 4 * U, 3 + 6

                def merge(m):
                    ch, a, c = merge_ch, ga[m.q], gc[m.q]
                    ch.count = m.n * MERGE_LINKS
                    dve.wait_ge(gathered[m.q], m.of_parity(32 * U))
                    fa, fc = has_row[:, m.cols], has_carry[:, m.cols]
                    ch.link(dve.tensor_scalar(ea[:, :, 0], fa, -1.0, OFF, ALU.add, ALU.mult))
                    ch.link(dve.tensor_scalar(ec[:, :, 0], fc, -1.0, OFF, ALU.add, ALU.mult)); ch.wait()
                    ch.link(dve.tensor_tensor(a[:, :, R:], a[:, :, R:], rep(ea[:, :, 0], 2, H), ALU.add))
                    ch.link(dve.tensor_tensor(c[:, :, R:], c[:, :, R:], rep(ec[:, :, 0], 2, H), ALU.add)); ch.wait()
                    ch.link(dve.tensor_tensor(mt[:, :, :], a[:, :, R:], c[:, :, R:], ALU.max)); ch.wait()
                    dve.tensor_tensor(ea[:, :, :], a[:, :, R:], mt[:, :, :], ALU.subtract).then_inc(exp_arg, 1)
                    dve.tensor_tensor(ec[:, :, :], c[:, :, R:], mt[:, :, :], ALU.subtract).then_inc(exp_arg, 1)
                    dve.wait_ge(exped, m.n + 1)
                    ch.link(dve.tensor_tensor(ea[:, :, :], ea[:, :, :], rep(fa, 2, H), ALU.mult))
                    ch.link(dve.tensor_tensor(ec[:, :, :], ec[:, :, :], rep(fc, 2, H), ALU.mult)); ch.wait()
                    ch.link(dve.tensor_tensor(mt[:, :, :], a[:, :, D:R], ea[:, :, :], ALU.mult))
                    ch.link(dve.tensor_tensor(c[:, :, D:R], c[:, :, D:R], ec[:, :, :], ALU.mult)); ch.wait()
                    ch.link(dve.tensor_tensor(mt[:, :, :], mt[:, :, :], c[:, :, D:R], ALU.add)); ch.wait()
                    ch.link(dve.tensor_scalar(mt[:, :, :], mt[:, :, :], 1e-16, None, ALU.add)); ch.wait()
                    ch.link(dve.reciprocal(mt[:, :, :], mt[:, :, :])); ch.wait()
                    ch.link(dve.tensor_tensor(ea[:, :, :], ea[:, :, :], mt[:, :, :], ALU.mult))
                    ch.link(dve.tensor_tensor(ec[:, :, :], ec[:, :, :], mt[:, :, :], ALU.mult)); ch.wait()

                    def by_head(buf, t, f):
                        ch.link(dve.tensor_tensor(buf[:, t, 0:S].rearrange("p (h c) -> p h c", h=H),
                                                  buf[:, t, 0:S].rearrange("p (h c) -> p h c", h=H),
                                                  rep(f[:, t, :], 2, 16), ALU.mult))
                        ch.link(dve.tensor_tensor(buf[:, t, S:D].rearrange("p (x h c) -> p x h c", h=H, c=8),
                                                  buf[:, t, S:D].rearrange("p (x h c) -> p x h c", h=H, c=8),
                                                  rep(rep(f[:, t, :], 2, 8), 1, 3), ALU.mult))
                    for t in range(U):
                        by_head(a, t, ea)
                        by_head(c, t, ec)
                    ch.wait()
                    need(dve, T, (m.n - 1) * U)
                    dve.tensor_tensor(aggn[m.q][:, :, :], a[:, :, 0:D], c[:, :, 0:D], ALU.add).then_inc(normed, 1)

                def norm(m):
                    ch = norm_ch
                    ch.count = m.n * NORM_LINKS
                    need(dve, tabbed, (m.n - 1) * U)
                    ch.link(dve.tensor_copy(inv_a[m.q][:, :], node_a[:, m.cols]))
                    for i, (t0, count) in enumerate(THIRDS):
                        xt = X1[:, m.tiles(t0, count), :]
                        dve.wait_ge(proj, m.n * U + (t0 + count))
                        last = dve.scalar_tensor_tensor(
                            out=xt, in0=xt, scalar=2.0,
                            in1=banks[4 + i][:, 0:count * D].rearrange("p (t d) -> p t d", d=D),
                            op0=ALU.mult, op1=ALU.add)
                        if i < 2:
                            ch.link(last)
                    last.then_inc(added, 1)
                    dve.wait_ge(added, m.n + 1)
                    normalise(dve, ch, X1[:, m.cols, :], xn[m.q], scr, st, varred, rooted, m.n)
                    dve.tensor_tensor(xn[m.q][:, :, :], xn[m.q][:, :, :], rep(st[:, :], 2, D), ALU.mult)\
                        .then_inc(ready, 1)

                def tables(m):
                    dve.wait_ge(ready, m.n + 1)
                    if not (isinstance(m.n, int) and m.n < 2):
                        dve.wait_ge(tab_out[m.q], (m.n - m.q) * 8)
                    for t in range(U):
                        o, a = banks[(2, 3, 7)[t % 3]], inv_a[m.q][:, t:t + 1]
                        dve.wait_ge(proj2, m.n * U + (t + 1))
                        dve.tensor_scalar(tab[m.q][:, t, :], o[:, 0:D], a, None, ALU.mult)
                        dve.scalar_tensor_tensor(out=X1[:, m.tiles(t), :].squeeze(1), in0=o[:, D:2 * D], scalar=a,
                                                 in1=xn[m.q][:, t, :], op0=ALU.mult, op1=ALU.add)\
                            .then_inc(tabbed, 1)

                def step(m, a, c):
                    if m is not None:
                        merge(m)
                    if a is not None:
                        norm(a)
                    if c is not None:
                        tables(c)
                batches(dve, NB, step)

            @block.scalar
            def _(act):
                def turn_out(m, t, buf, T, used, done):
                    act.wait_ge(T, m.n * U + (t + 1))
                    need(act, used, m.n * U + max(t - 1, 0))
                    act.activation(buf[t % 2][:, 0:P], banks[t % 2][:, 0:P], ACT.Copy)
                    act.activation(buf[t % 2][0:C, P:], banks[t % 2][0:C, P:2 * P], ACT.Copy).then_inc(done, 1)

                def step(m, a, c):
                    if m is not None:
                        act.wait_ge(exp_arg, m.n * 2 + 2)
                        act.activation(ea[:, :, :], ea[:, :, :], ACT.Exp)
                        act.activation(ec[:, :, :], ec[:, :, :], ACT.Exp).then_inc(exped, 1)
                    if a is not None:
                        for t in range(U):
                            turn_out(a, t, turned, T, proj, T_out)
                    if c is not None:
                        for t in range(3):
                            turn_out(c, t, turned2, T2, proj2, T2_out)
                    if a is not None:
                        act.wait_ge(varred, a.n + 1)
                        act.activation(st[:, :], st[:, :], ACT.Sqrt).then_inc(rooted, 1)
                    if c is not None:
                        for t in range(3, U):
                            turn_out(c, t, turned2, T2, proj2, T2_out)
                batches(act, NB, step)

            @block.tensor
            def _(pe):
                def turn(m, t, x, T):
                    pe.transpose(banks[t % 2][:, 0:P], x[m.q][:, t, 0:P], ident[:, :])
                    pe.transpose(banks[t % 2][0:C, P:2 * P], x[m.q][:, t, P:D], ident[:, :]).then_inc(T, 1)

                def project(m):
                    pe.wait_ge(normed, m.n + 1)
                    need(pe, T2_out, (m.n - 1) * U)
                    need(pe, T_out, m.n * U)
                    need(pe, added, m.n)
                    for t in range(U + 1):
                        if t < U:
                            if t >= 2:
                                pe.wait_ge(T_out, m.n * U + (t - 1))
                            turn(m, t, aggn, T)
                        if t >= 1:
                            k = t - 1
                            pe.wait_ge(T_out, m.n * U + t)
                            o = banks[4 + k // 3][:, (k % 3) * D:(k % 3 + 1) * D]
                            pe.matmul(o, turned[k % 2][:, 0:P], wt("Wpa"), start=True, stop=False)
                            pe.matmul(o, turned[k % 2][0:C, P:], wt("Wpb"), start=False, stop=True)\
                                .then_inc(proj, 1)

                def project2(m, turned_out):
                    pe.wait_ge(ready, m.n + 1)
                    pe.wait_ge(T_out, turned_out)
                    need(pe, T2_out, m.n * U)
                    for t in range(U + 1):
                        if t < U:
                            if t >= 2:
                                pe.wait_ge(T2_out, m.n * U + (t - 1))
                            turn(m, t, xn, T2)
                        if t >= 1:
                            k = t - 1
                            pe.wait_ge(T2_out, m.n * U + t)
                            need(pe, tabbed, m.n * U + max(k - 2, 0))
                            o = banks[(2, 3, 7)[k % 3]]
                            pe.matmul(o[:, 0:2 * D], turned2[k % 2][:, 0:P], wt("W3a"), start=True, stop=False)
                            pe.matmul(o[:, 0:2 * D], turned2[k % 2][0:C, P:], wt("W3b"), start=False, stop=True)\
                                .then_inc(proj2, 1)

                def step(m, a, c):
                    if a is not None:
                        project(a)
                    if c is not None:
                        project2(c, (c.n + 2) * U if a is not None else NB * U)
                batches(pe, NB, step)


def edge_loop_1(nc, ctx, sem, banks, wt, rbf_w, ins, rbf_parts, conv_table, agg1, NG):
    with ExitStack() as ph:
        def sb(name, shape, dt=F32):
            return ph.enter_context(nc.sbuf_tensor("m_" + name, shape, dt))
        pack = [sb(f"pack{i}", [P, 32], I32) for i in range(4)]
        idx = [p[:, 0:8] for p in pack]
        Y = [p[:, 8:32].bitcast(F32).rearrange("p (t c) -> p t c", t=TG) for p in pack]
        xs = [sb(f"xs{i}", [P, 512], BF16) for i in range(4)]
        drow = [sb(f"drow{i}", [P, 512], I32) for i in range(4)]
        gs = [sb(f"gs{i}", [P, TG, D]) for i in range(4)]
        tanh = sb("tanh", [S, 512])
        hid = [sb(f"hid{i}", [S, 512]) for i in range(2)]
        u = sb("u", [P, TG, P])
        tt = sb("tt", [P, TG, V])
        dot = sb("dot", [P, TG, C])
        w2y = sb("w2y", [P, TG, C])
        mid_ = [sb(f"mid{i}", [P, TG, 3 * P]) for i in range(4)]
        eq = [sb(f"eq{i}", [P, TG, P]) for i in range(4)]
        sums = [sb(f"sums{k}", [P, 512]) for k in range(3)]
        orow = [sb(f"orow{i}", [P, TG, AGG1]) for i in range(2)]
        small_in = [sem(f"l1_small_in{i}") for i in range(4)]
        big_in = [sem(f"l1_big_in{i}") for i in range(4)]
        gathered = [sem(f"l1_gathered{i}") for i in range(4)]
        out_done = [sem(f"l1_out_done{i}") for i in range(2)]
        (hid_mm, tanhed, hid_made, weights, mids, eq_made, summed, sums_out, mapped, row_out, u_made, scaled) = (
            sem("l1_" + n) for n in ("hid_mm", "tanhed", "hid_made", "weights", "mids", "eq_made", "summed",
                                     "sums_out", "mapped", "row_out", "u_made", "scaled"))
        agg_v = agg1.rearrange("(g j p) c -> g p j c", j=TG, p=P)
        xs_v = rbf_parts.rearrange("s c (g n) -> s g c n", n=512)
        drow_v = ins["dst_flat"].rearrange("(g n) -> g n", n=512)

        with nc.Block() as block:
            @block.sync
            def _(sp):
                def step(g, front, mid, late, tail):
                    if front:
                        s, n = g.slot, g.n
                        hold(sp, hid_mm, n - 3)
                        hold(sp, mids, n - 3)
                        hold(sp, scaled, n - 3)
                        hold(sp, eq_made, n - 3)
                        if not (isinstance(g.base, int) and g.base == 0):
                            hold(sp, gathered[s], g.base * 16)
                        at = bass.ds(n, 1)
                        sp.dma_start(pack[s][:, :], ins["edge_pack"][at].squeeze(0)).then_inc(small_in[s], 16)
                        c0 = 0
                        for part, copies in ((0, 3), (1, 3), (2, 2)):
                            sp.dma_start(xs[s][c0:c0 + 16 * copies, :], rep(xs_v[part, at], 0, copies).squeeze(1))\
                                .then_inc(big_in[s], 16)
                            c0 += 16 * copies
                        sp.dma_start(drow[s][:, :], drow_v[at].broadcast_to([P, 512])).then_inc(big_in[s], 16)
                steps(sp, NG, step, 4)

            @block.gpsimd
            def _(pool):
                def step(g, front, mid, late, tail):
                    if not front:
                        return
                    s = g.slot
                    need(pool, mids, g.n - 3)
                    pool.wait_ge(small_in[s], g.loads(16))
                    settle(pool)
                    for j in range(TG):
                        pool.indirect_dma_start(
                            out=gs[s][:, j, :], out_offset=None, in_=conv_table,
                            in_offset=bass.IndirectOffsetOnAxis(ap=idx[s][:, j:j + 1], axis=0)
                        ).then_inc(gathered[s], 16)
                steps(pool, NG, step, 4)

            @block.vector
            def _(dve):
                ch = Chain(dve, sem("l1_vector_chain"))

                def x3(ap, c0, w):
                    return ap[:, :, c0:c0 + 3 * w].rearrange("p t (x c) -> p t x c", c=w)

                def step(g, front, mid, late, tail):
                    if mid:
                        m = g.back(1)
                        s, y, e = m.slot, Y[m.slot], gs[m.slot]
                        dve.wait_ge(gathered[s], m.loads(64))
                        need(dve, mids, m.n)
                        a = ch.link(dve.tensor_tensor(x3(tt, 0, C), x3(e, S, C), rep(y[:, :, 1:4], 3, C), ALU.mult))
                        need(dve, summed, 3 * (m.n - 2))
                        ch.wait(a)
                        a = ch.link(dve.tensor_tensor(dot[:, :, :], tt[:, :, 0:C], tt[:, :, C:2 * C], ALU.add))
                        dve.wait_ge(big_in[s], m.loads(64))
                        need(dve, summed, 3 * (m.n - 2))
                        dve.tensor_tensor(eq[s][:, :, :], drow[s][:, :].rearrange("p (t e) -> p t e", t=TG),
                                          rep(idx[s][:, 4:8], 2, P), ALU.is_equal).then_inc(eq_made, 1)
                    if front:
                        n = g.n
                        dve.wait_ge(tanhed, n + 1)
                        need(dve, weights, 2 * (n - 1))
                        dve.scalar_tensor_tensor(out=hid[g.slot % 2][:, :], in0=tanh[:, :], scalar=1.0,
                                                 in1=banks[0][0:S, :], op0=ALU.add, op1=ALU.mult)\
                            .then_inc(hid_made, 1)
                    if mid:
                        need(dve, scaled, m.n)
                        for b in range(2):
                            dve.wait_ge(weights, 2 * m.n + (b + 1))
                            o = banks[1 + b][:, 0:384].rearrange("p (t c) -> p t c", t=2)
                            ts2 = slice(2 * b, 2 * b + 2)
                            dve.tensor_tensor(
                                u[:, ts2, :].rearrange("p t (r c) -> p t r c", c=S),
                                o[:, :, 0:P].rearrange("p t (r c) -> p t r c", c=S), rep(e[:, ts2, 0:S], 2, 2),
                                ALU.mult).then_inc(u_made, 1)
                            bw = ch.link(dve.tensor_tensor(w2y[:, ts2, :], o[:, :, 128:160], rep(y[:, ts2, 0], 2, C),
                                                           ALU.mult))
                            if b == 0:
                                ch.wait(a)
                                a = ch.link(dve.tensor_tensor(dot[:, :, :], dot[:, :, :], tt[:, :, 2 * C:V], ALU.add))
                                ch.wait(a)
                            ch.link(dve.tensor_tensor(mid_[s][:, ts2, S:V], o[:, :, 160:192], dot[:, ts2, :], ALU.mult))
                        ch.wait(bw)
                        ch.link(dve.tensor_tensor(x3(mid_[s], V, C), x3(e, S, C), rep(w2y[:, :, :], 2, 3), ALU.mult))
                        dve.wait_ge(u_made, 2 * (m.n + 1))
                        dve.tensor_tensor(x3(mid_[s], 2 * V, S), rep(u[:, :, S:P], 2, 3), rep(y[:, :, 1:4], 3, S),
                                          ALU.mult).then_inc(mids, 1)
                steps(dve, NG, step, 4, ch)

            @block.scalar
            def _(act):
                def step(g, front, mid, late, tail):
                    n = g.n
                    if front:
                        act.wait_ge(hid_mm, n + 1)
                        need(act, hid_made, n)
                        act.activation(tanh[:, :], banks[0][0:S, :], ACT.Tanh, scale=0.125).then_inc(tanhed, 1)
                    if tail:
                        t = g.back(3)
                        q = t.slot % 2
                        for k in range(3):
                            act.wait_ge(summed, 3 * t.n + (k + 1))
                            need(act, mapped, 2 * t.n)
                            act.activation(sums[k][:, :], banks[3 + k][:, :], ACT.Copy).then_inc(sums_out, 1)
                        if not (isinstance(t.base, int) and t.base == 0 and t.slot < 2):
                            act.wait_ge(out_done[q], t.base * 8 + 16 * (t.slot // 2))
                        for b in range(2):
                            act.wait_ge(mapped, 2 * t.n + (b + 1))
                            act.activation(orow[q][:, 2 * b:2 * b + 2, :],
                                           banks[6 + b][:, 0:2 * AGG1].rearrange("p (t c) -> p t c", t=2), ACT.Copy)\
                                .then_inc(row_out, 1)
                    if mid:
                        m = g.back(1)
                        act.wait_ge(u_made, 2 * (m.n + 1))
                        need(act, summed, 3 * (m.n - 2))
                        for j in range(TG):
                            last = act.activation(mid_[m.slot][:, j, 0:S], u[:, j, 0:S], ACT.Copy,
                                                  scale=Y[m.slot][:, j, 0:1])
                        last.then_inc(scaled, 1)
                    if tail:
                        act.wait_ge(row_out, 2 * (t.n + 1))
                        act.dma_start(agg_v[bass.ds(t.n, 1)].squeeze(0), orow[q][:, :, :])\
                            .then_inc(out_done[q], 16)
                steps(act, NG, step, 4)
                for i in range(2):
                    act.wait_ge(out_done[i], 16 * (NG // 2))

            @block.tensor
            def _(pe):
                def step(g, front, mid, late, tail):
                    n = g.n
                    if front:
                        pe.wait_ge(big_in[g.slot], g.loads(64))
                        need(pe, hid_made, n)
                        pe.matmul(banks[0][0:S, :], rbf_w[:, 352:416], xs[g.slot][:, :], start=True, stop=True)\
                            .then_inc(hid_mm, 1)
                    if tail:
                        t = g.back(3)
                        pe.wait_ge(mids, t.n + 1)
                        pe.wait_ge(scaled, t.n + 1)
                        pe.wait_ge(eq_made, t.n + 1)
                        for k in range(3):
                            need(pe, sums_out, 3 * t.n - 2 + k)
                            for j in range(TG):
                                mm = pe.matmul(banks[3 + k][:, P * j:P * j + P], mid_[t.slot][:, j, P * k:P * k + P],
                                               eq[t.slot][:, j, :], start=True, stop=True)
                            mm.then_inc(summed, 1)
                    if mid:
                        m = g.back(1)
                        pe.wait_ge(hid_made, m.n + 1)
                        need(pe, mids, m.n)
                        for j in range(TG):
                            c = 192 * (j % 2)
                            mm = pe.matmul(banks[1 + j // 2][:, c:c + 192], hid[m.slot % 2][:, P * j:P * j + P],
                                           wt("Wfc2"), start=True, stop=True)
                            if j % 2:
                                mm.then_inc(weights, 1)
                    if tail:
                        pe.wait_ge(sums_out, 3 * t.n + 3)
                        for j in range(TG):
                            if j % 2 == 0:
                                need(pe, row_out, 2 * t.n - 1 + j // 2)
                            c, e = AGG1 * (j % 2), slice(P * j, P * j + P)
                            o = banks[6 + j // 2]
                            pe.matmul(o[:, c:c + 161], sums[0][:, e], wt("W4a"), start=True, stop=False)
                            pe.matmul(o[:, c + 65:c + 161], sums[1][:, e], wt("W4b"), start=False, stop=False)
                            mm = pe.matmul(o[:, c + 97:c + 161], sums[2][:, e], wt("W4c"), start=False, stop=True)
                            if j % 2:
                                mm.then_inc(mapped, 1)
                steps(pe, NG, step, 4)


def node_step_1(nc, ctx, sem, banks, agg1, carry1, out, X1, row_idx, carry_idx, has_row, has_carry, node_a,
                degree, NK):
    NB, U = NK // NODE_BATCH, NODE_BATCH
    with ExitStack() as ph:
        def sb(name, shape, dt=F32):
            return ph.enter_context(nc.sbuf_tensor("n1_" + name, shape, dt))
        idx_s = [sb(f"idx{i}", [P, 2 * U], I32) for i in range(2)]
        ga = [sb(f"ga{i}", [P, U, AGG1]) for i in range(2)]
        gc = [sb(f"gc{i}", [P, U, AGG1]) for i in range(2)]
        xn = [sb(f"xn{i}", [P, U, D]) for i in range(2)]
        cnt, st, scr = sb("cnt", [P, U]), sb("st", [P, U]), sb("scr", [P, U, D])
        copied, used, varred, rooted, done = (
            sem("n1_" + n) for n in ("copied", "used", "varred", "rooted", "done"))
        gathered = [sem(f"n1_gathered{i}") for i in range(2)]
        stored = [sem(f"n1_stored{i}") for i in range(2)]
        out_v = out.rearrange("(p k) d -> p k d", k=NK)
        with nc.Block() as block:
            @block.sync
            def _(sp):
                def step(m, *_):
                    if m is not None:
                        hold(sp, done, m.n + 1)
                        sp.dma_start(out_v[:, m.cols, :], xn[m.q][:, :, :]).then_inc(stored[m.q], 16)
                batches(sp, NB, step)
                for q in range(2):
                    hold(sp, stored[q], 16 * (NB // 2))

            @block.gpsimd
            def _(pool):
                gather_batches(pool, NB, row_idx, carry_idx, idx_s, agg1, carry1, ga, gc, copied, used, gathered)

            @block.scalar
            def _(act):
                def step(m, *_):
                    if m is not None:
                        act.wait_ge(varred, m.n + 1)
                        act.activation(st[:, :], st[:, :], ACT.Sqrt).then_inc(rooted, 1)
                batches(act, NB, step)

            @block.vector
            def _(dve):
                ch = Chain(dve, sem("n1_chain"))
                LINKS = 10 + 6

                def step(m, *_):
                    if m is None:
                        return
                    ch.count = m.n * LINKS
                    cols, a, c = m.cols, ga[m.q], gc[m.q]
                    ch.link(dve.tensor_scalar(cnt[:, :], degree[:, cols], 1.0, None, ALU.max)); ch.wait()
                    ch.link(dve.reciprocal(cnt[:, :], cnt[:, :])); ch.wait()
                    ch.link(dve.tensor_tensor(cnt[:, :], cnt[:, :], node_a[:, cols], ALU.mult)); ch.wait()
                    dve.wait_ge(gathered[m.q], m.of_parity(32 * U))
                    ch.link(dve.tensor_tensor(a[:, :, :], a[:, :, :], rep(has_row[:, cols], 2, AGG1), ALU.mult))
                    ch.link(dve.tensor_tensor(c[:, :, :], c[:, :, :], rep(has_carry[:, cols], 2, AGG1), ALU.mult))
                    ch.wait()
                    ch.link(dve.tensor_tensor(a[:, :, :], a[:, :, :], c[:, :, :], ALU.add))
                    ch.link(dve.tensor_tensor(cnt[:, :], cnt[:, :], cnt[:, :], ALU.mult)); ch.wait()
                    ch.link(dve.tensor_tensor(cnt[:, :], cnt[:, :], a[:, :, 0], ALU.mult)); ch.wait()
                    ch.link(dve.tensor_tensor(a[:, :, 1:161], a[:, :, 1:161], rep(cnt[:, :], 2, D), ALU.mult))
                    ch.wait()
                    xs, xv = X1[:, cols, 0:S], X1[:, cols, S:D].rearrange("p k (c x) -> p k x c", x=3)
                    ch.link(dve.tensor_tensor(xs, xs, a[:, :, 1:65], ALU.add))
                    dve.tensor_tensor(xv, xv, a[:, :, 65:161].rearrange("p k (x c) -> p k x c", x=3),
                                      ALU.add).then_inc(used, 1)
                    dve.wait_ge(used, m.n + 1)
                    ch.wait()
                    if not (isinstance(m.n, int) and m.n < 2):
                        dve.wait_ge(stored[m.q], (m.n - m.q) * 8)
                    normalise(dve, ch, X1[:, cols, :], xn[m.q], scr, st, varred, rooted, m.n)
                    dve.tensor_tensor(xn[m.q][:, :, :], xn[m.q][:, :, :], rep(st[:, :], 2, D), ALU.mult)\
                        .then_inc(done, 1)
                batches(dve, NB, step)


def kernel(**inputs):
    import numpy as np
    import concourse.bacc as bacc
    from concourse.bass_utils import run_bass_kernel_spmd

    g = {k: np.ascontiguousarray(v) for k, v in inputs.items()}
    f32 = np.float32
    N, E = g["x"].shape[0], g["src"].shape[0]
    SB = -(-E // (P * P))
    NT = SB * P
    EP, NG = NT * P, NT // TG
    NK = 2 * NODE_BATCH * -(-(N + 1) // (2 * NODE_BATCH * P))

    def padded(a, n, fill=0):
        out = np.full((n,) + a.shape[1:], fill, a.dtype)
        out[:a.shape[0]] = a
        return out

    src, dst = padded(g["src"], EP), padded(g["dst"], EP, N)

    def columns(a):
        return a.reshape(NG, TG, P, -1).transpose(0, 2, 1, 3)
    y = padded(g["edge_attr_4"], EP)
    before = np.concatenate([np.full(1, -1, dst.dtype), dst[:-1]])
    arrays = {
        "x": padded(g["x"], NK * P),
        "edge_pack": np.concatenate([columns(src)[..., 0], columns(dst)[..., 0], np.ascontiguousarray(
            columns(y[:, [0, 1, 2, 3, 1, 2]]).reshape(NG, P, TG * 6)).view(src.dtype)], axis=2),
        "rbf_t": padded(g["edge_attr_16"], EP).T,
        "dst_flat": dst,
        "dst_rows": np.concatenate([before.reshape(NT, P)[:, :1], dst.reshape(NT, P)], axis=1),
        "first": dst.reshape(NT, P)[:, 0], "last": dst.reshape(NT, P)[:, -1],
        "before": before.reshape(NT, P)[:, 0], "sup": dst.reshape(SB, P * P)[:, -1],
        "node_a": padded(g["node_vec1"], NK * P).reshape(P, NK),
    }

    L0 = {k[7:]: v for k, v in g.items() if k.startswith("L0_gnn_")}
    L1 = {k[7:]: v for k, v in g.items() if k.startswith("L1_gnn_")}
    c3 = 3 * np.arange(C)

    def blocks(w):
        o = np.zeros((V, V), f32)
        for x in range(3):
            o[C * x:C * x + C, C * x:C * x + C] = w
        return o

    def node_rows(w, x_major_cols=True):
        o = np.zeros((V, V), f32)
        for x in range(3):
            o[np.ix_(c3 + x, C * x + np.arange(C) if x_major_cols else c3 + x)] = w
        return o
    wr = L0["W_rbf"]
    ss, sv, vs, vv0, vv1 = wr[:, :64], wr[:, 64:128], wr[:, 128:160], wr[:, 160:192], wr[:, 192:224]
    arrays["rbf_w"] = np.concatenate([sv, ss, vs, vs, vs, vv0, vv1, vv1, vv1, L1["Wfc1"]], axis=1)
    z = lambda r, c: np.zeros((r, c), f32)
    Wal, Wsv, Wvv = L0["W_alpha"], L0["Ws_val"], L0["Wv_val"]
    Wsl, Wvl = L0["Ws_vlin"], L0["Wv_vlin"]
    parts = {}
    parts["WsSD"] = np.concatenate([L0["Ws_src"], L0["Ws_dst"]], axis=1)
    parts["WvSD"] = np.concatenate([node_rows(L0["Wv_src"]), node_rows(L0["Wv_dst"])], axis=1)
    parts["gs"], parts["bs"] = L0["gamma_s"][:, None], L0["beta_s"][:, None]
    parts["gv"] = np.repeat(L0["gamma_v"], 3)[:, None]
    parts["WvT1"], parts["WvT2"] = z(64, 128), z(64, 128)
    parts["WvT1"][:, 64:] = Wsv.T[:, :64]
    parts["WvT2"][:, 96:] = Wsv.T[:, 64:]
    parts["Wg"] = L0["Wg"]
    parts["W1a"] = z(128, 192)
    parts["W1a"][:64, 160:] = Wvv[:64]
    parts["W1a"][64:, :64], parts["W1a"][64:, 96:160] = Wsv[:64], Wal[:64]
    parts["W1b"] = z(128, 288)
    parts["W1b"][:96, 192:] = blocks(Wvv[64:96])
    parts["W1b"][96:, :64], parts["W1b"][96:, 96:160] = Wsv[64:], Wal[64:]
    parts["W1c"] = blocks(Wvv[96:])
    parts["W2a"] = z(128, 96)
    parts["W2a"][:64, 64:] = Wvl[:64]
    parts["W2a"][64:, :64] = Wsl[:64]
    parts["W2b"] = z(128, 192)
    parts["W2b"][:96, 96:] = blocks(Wvl[64:96])
    parts["W2b"][96:, :64] = Wsl[64:]
    parts["W2c"] = blocks(Wvl[96:])
    parts["r2"] = z(128, 3)
    parts["r2"][:, 0] = np.concatenate([L0["w2_sv"], L0["w2_ss"]])
    parts["r2"][:, 1] = np.concatenate([L0["w2_vs"]] * 3 + [L0["w2_vv0"]])
    parts["r2"][:96, 2] = np.concatenate([L0["w2_vv1"]] * 3)
    parts["adot"] = np.broadcast_to(L0["alpha_dot"].reshape(1, 64), (P, 64))
    po = z(160, 160)
    po[:64, :64] = L0["Wps"]
    for x in range(3):
        po[np.ix_(64 + C * x + np.arange(C), 64 + c3 + x)] = L0["Wpv"]
    parts["Wpa"], parts["Wpb"] = po[:P], po[P:]
    w3 = z(160, 320)
    w3[:64, :64], w3[:64, 160:224] = L1["Wl1_0"], L1["Wsc0"]
    w3[64:, 64:160], w3[64:, 224:] = node_rows(L1["Wl1_1"]), node_rows(L1["Wsc1"], False)
    parts["W3a"], parts["W3b"] = w3[:P], w3[P:]
    parts["Wfc2"] = L1["Wfc2"]
    w4 = z(384, 161)
    w4[:96, 0:1], w4[:96, 1:65] = L1["Wa"], L1["Wl2_s"]
    for x in range(3):
        w4[96 + C * x:96 + C * x + C, 65 + C * x:97 + C * x] = L1["Wl2_v"][64:]
        w4[192 + S * x:192 + S * x + S, 65 + C * x:97 + C * x] = L1["Wl2_v"][:64]
    parts["W4a"], parts["W4b"], parts["W4c"] = w4[:128], w4[128:256, 65:], w4[256:, 97:]
    at, cols = {}, 0
    for n, w in parts.items():
        at[n] = (cols, w.shape[0], w.shape[1])
        cols += w.shape[1]
    at["_width"] = cols
    arrays["weights"] = z(P, cols)
    for n, w in parts.items():
        arrays["weights"][:w.shape[0], at[n][0]:at[n][0] + w.shape[1]] = w

    nc = bacc.Bacc("TRN2", target_bir_lowering=False, num_devices=1)
    arrays = {"in_" + k: np.ascontiguousarray(v) for k, v in arrays.items()}
    ins = {k[3:]: nc.dram_tensor(k, v.shape, mybir.dt.from_np(v.dtype), kind="ExternalInput").ap()
           for k, v in arrays.items()}
    out = nc.dram_tensor("out_nodes", (NK * P, D), F32, kind="ExternalOutput").ap()
    build(nc, ins, out, at, NT, NK)
    r = run_bass_kernel_spmd(nc, [arrays], core_ids=[0])
    return r.results[0]["out_nodes"][:N]
```
